# Optimizing a Trainium2 kernel written in Bass

```python
import numpy as np
import jax
import jax.numpy as jnp

def _softmax(x, axis=-1):
    return jax.nn.softmax(x, axis=axis)

def _gelu(x):
    return jax.nn.gelu(x, approximate=True)

def _silu(x):
    return jax.nn.silu(x)

def _sigmoid(x):
    return jax.nn.sigmoid(x)

def _layernorm(x, axis=-1, eps=1e-05):
    m = jnp.mean(x, axis=axis, keepdims=True)
    v = jnp.var(x, axis=axis, keepdims=True)
    return (x - m) / jnp.sqrt(v + eps)

def _scatter_add(tgt, idx, src, axis=0):
    return tgt.at[idx].add(src)

def _segment_sum(src, seg, n):
    return jax.ops.segment_sum(src, seg, n)
kernel_name = 'mk_gnn_resnorm_d4_gnn_r64_904304'

def setup_inputs(seed: int=0):
    np.random.seed(seed)
    _w = jnp.asarray

    def _rec_inputs():
        import jax
        import jax.numpy as jnp
        _gk = jax.random.key(seed)
        x = -0.000202 + 1 * jax.random.normal(jax.random.fold_in(_gk, 1), (100000, 128), jnp.float32)
        src = jax.random.randint(jax.random.fold_in(_gk, 2), (25000,), 0, 100000, jnp.int32)
        dst = jnp.minimum((100000 * jax.random.uniform(jax.random.fold_in(_gk, 3), (25000,)) ** 2.0).astype(jnp.int32), 99999)
        _o = jnp.argsort(dst, stable=True)
        src = src[_o]
        dst = dst[_o]
        edge_attr_128 = -8.16379e-05 + 0.999858 * jax.random.normal(jax.random.fold_in(_gk, 12), (25000, 128), jnp.float32)
        edge_type_8 = jax.random.randint(jax.random.fold_in(_gk, 14), (25000,), 0, 8, jnp.int32)
        edge_weight = jax.random.uniform(jax.random.fold_in(_gk, 15), (25000,), jnp.float32, 0.0, 1)
        return (x, src, dst, edge_attr_128, edge_type_8, edge_weight)
    x, src, dst, edge_attr_128, edge_type_8, edge_weight = _rec_inputs()

    def _L0_gnn_setup():
        import jax, jax.numpy as jnp
        import numpy as np
        N = 50000
        E = 10000
        IN_DIM = 128
        OUT_DIM = 128
        EPS = 1e-05
        key = jax.random.key(seed)
        k1, k2, k3, k4 = jax.random.split(key, 4)
        x = jax.random.normal(k1, (N, IN_DIM), dtype=jnp.float32)
        edge_index = jax.random.randint(k2, (2, E), 0, N, dtype=jnp.int64)
        W = jax.random.normal(k3, (OUT_DIM, IN_DIM), dtype=jnp.float32) * (1.0 / np.sqrt(IN_DIM))
        b = jax.random.normal(k4, (OUT_DIM,), dtype=jnp.float32) * 0.01
        gamma = jnp.ones((OUT_DIM,), dtype=jnp.float32)
        beta = jnp.zeros((OUT_DIM,), dtype=jnp.float32)
        return {'x': x, 'edge_index': edge_index, 'W': W, 'b': b, 'gamma': gamma, 'beta': beta}
    _L0_gnn_all = _L0_gnn_setup()
    _L0_gnn_in = {k: v for k, v in _L0_gnn_all.items() if k in ('W', 'b', 'gamma', 'beta')}
    del _L0_gnn_all

    def _L1_gnn_setup():
        import jax, jax.numpy as jnp
        import numpy as np
        N_NODES = 50000
        N_EDGES = 12500
        FEAT_DIM = 128
        EMB_DIM = 64
        NUM_RELS = 8
        key = jax.random.key(seed)
        k1, k2, k3, k4, k5, k6, k7 = jax.random.split(key, 7)
        inputs = jax.random.normal(k1, (N_NODES, FEAT_DIM), dtype=jnp.float32)
        src = jax.random.randint(k2, (N_EDGES,), 0, N_NODES, dtype=jnp.int32)
        dst = jax.random.randint(k3, (N_EDGES,), 0, N_NODES, dtype=jnp.int32)
        rel = jax.random.randint(k4, (N_EDGES,), 0, NUM_RELS, dtype=jnp.int32)
        rel_emb = jax.random.normal(k5, (NUM_RELS, EMB_DIM), dtype=jnp.float32)
        in_dim = 2 * FEAT_DIM + EMB_DIM
        bound = 1.0 / np.sqrt(in_dim)
        W = jax.random.uniform(k6, (FEAT_DIM, in_dim), minval=-bound, maxval=bound, dtype=jnp.float32)
        b = jax.random.uniform(k7, (FEAT_DIM,), minval=-bound, maxval=bound, dtype=jnp.float32)
        return {'inputs': inputs, 'rel_emb': rel_emb, 'W': W, 'b': b, 'src': src, 'dst': dst, 'rel': rel}
    _L1_gnn_all = _L1_gnn_setup()
    _L1_gnn_in = {k: v for k, v in _L1_gnn_all.items() if k in ('rel_emb', 'W', 'b')}
    del _L1_gnn_all

    def _L2_gnn_setup():
        import jax, jax.numpy as jnp
        import numpy as np
        NEG_SLOPE = 0.2
        key = jax.random.key(seed)
        ks = jax.random.split(key, 8)
        N, E, H = (50000, 12500, 128)
        node_attr = jax.random.normal(ks[0], (N, H), dtype=jnp.float32)
        edge_attr = jax.random.normal(ks[1], (E, H), dtype=jnp.float32)
        edge_index = jax.random.randint(ks[2], (2, E), 0, N, dtype=jnp.int64)
        lim_n = 1.0 / np.sqrt(H)
        W_node = jax.random.uniform(ks[3], (H, H), jnp.float32, -lim_n, lim_n)
        b_node = jax.random.uniform(ks[4], (H,), jnp.float32, -lim_n, lim_n)
        lim_e = 1.0 / np.sqrt(3 * H)
        W_edge = jax.random.uniform(ks[5], (3 * H, 1), jnp.float32, -lim_e, lim_e)
        b_edge = jax.random.uniform(ks[6], (1,), jnp.float32, -lim_e, lim_e)
        return {'node_attr': node_attr, 'edge_attr': edge_attr, 'edge_index': edge_index, 'num_nodes': N, 'W_node': W_node, 'b_node': b_node, 'W_edge': W_edge, 'b_edge': b_edge}
    _L2_gnn_all = _L2_gnn_setup()
    _L2_gnn_in = {k: v for k, v in _L2_gnn_all.items() if k in ('W_node', 'b_node', 'W_edge', 'b_edge')}
    del _L2_gnn_all

    def _L3_gnn_setup():
        import jax, jax.numpy as jnp
        import numpy as np
        N_NODES = 100000
        N_EDGES = 25000
        NFEAT = 128
        NHID = 64

        def _gcn_layer(h, src, dst, edge_weight, w, b, n_nodes):
            support = h @ w
            msgs = support[src] * edge_weight[:, None]
            agg = jax.ops.segment_sum(msgs, dst, num_segments=n_nodes)
            return agg + b
        key = jax.random.key(seed)
        ks = jax.random.split(key, 8)
        x = jax.random.normal(ks[0], (N_NODES, NFEAT), dtype=jnp.float32)
        src = jax.random.randint(ks[1], (N_EDGES,), 0, N_NODES, dtype=jnp.int32)
        dst = jax.random.randint(ks[2], (N_EDGES,), 0, N_NODES, dtype=jnp.int32)
        edge_weight = jax.random.uniform(ks[3], (N_EDGES,), dtype=jnp.float32)
        w1 = jax.random.normal(ks[4], (NFEAT, NHID), dtype=jnp.float32) * (1.0 / np.sqrt(NFEAT))
        b1 = jnp.zeros((NHID,), dtype=jnp.float32)
        w2 = jax.random.normal(ks[5], (NHID, 2 * NHID), dtype=jnp.float32) * (1.0 / np.sqrt(NHID))
        b2 = jnp.zeros((2 * NHID,), dtype=jnp.float32)
        return {'x': x, 'src': src, 'dst': dst, 'edge_weight': edge_weight, 'w1': w1, 'b1': b1, 'w2': w2, 'b2': b2}
    _L3_gnn_all = _L3_gnn_setup()
    _L3_gnn_in = {k: v for k, v in _L3_gnn_all.items() if k in ('w1', 'b1', 'w2', 'b2')}
    del _L3_gnn_all
    return {'x': x, 'src': src, 'dst': dst, 'edge_attr_128': edge_attr_128, 'edge_type_8': edge_type_8, 'edge_weight': edge_weight, 'L0_gnn_W': _L0_gnn_in['W'], 'L0_gnn_b': _L0_gnn_in['b'], 'L0_gnn_gamma': _L0_gnn_in['gamma'], 'L0_gnn_beta': _L0_gnn_in['beta'], 'L1_gnn_rel_emb': _L1_gnn_in['rel_emb'], 'L1_gnn_W': _L1_gnn_in['W'], 'L1_gnn_b': _L1_gnn_in['b'], 'L2_gnn_W_node': _L2_gnn_in['W_node'], 'L2_gnn_b_node': _L2_gnn_in['b_node'], 'L2_gnn_W_edge': _L2_gnn_in['W_edge'], 'L2_gnn_b_edge': _L2_gnn_in['b_edge'], 'L3_gnn_w1': _L3_gnn_in['w1'], 'L3_gnn_b1': _L3_gnn_in['b1'], 'L3_gnn_w2': _L3_gnn_in['w2'], 'L3_gnn_b2': _L3_gnn_in['b2']}

def reference(x, src, dst, edge_attr_128, edge_type_8, edge_weight, L0_gnn_W, L0_gnn_b, L0_gnn_gamma, L0_gnn_beta, L1_gnn_rel_emb, L1_gnn_W, L1_gnn_b, L2_gnn_W_node, L2_gnn_b_node, L2_gnn_W_edge, L2_gnn_b_edge, L3_gnn_w1, L3_gnn_b1, L3_gnn_w2, L3_gnn_b2):
    import jax
    import jax.numpy as jnp

    def _L0_gnn_ref(x, edge_index, W, b, gamma, beta):
        import jax, jax.numpy as jnp
        import numpy as np
        N = 50000
        E = 10000
        IN_DIM = 128
        OUT_DIM = 128
        EPS = 1e-05
        src, dst = (edge_index[0], edge_index[1])
        n = x.shape[0]
        agg = jax.ops.segment_sum(x[src], dst, num_segments=n)
        deg = jax.ops.segment_sum(jnp.ones(src.shape[0], dtype=x.dtype), dst, num_segments=n)
        deg = jnp.maximum(deg + 1.0, 1.0)[:, None]
        out = (x + agg) / deg
        out = out @ W.T + b
        mu = jnp.mean(out, axis=-1, keepdims=True)
        var = jnp.mean((out - mu) ** 2, axis=-1, keepdims=True)
        out = (out - mu) * jax.lax.rsqrt(var + EPS) * gamma + beta
        return jax.nn.relu(out)

    def _L1_gnn_ref(inputs, rel_emb, W, b, src, dst, rel):
        import jax, jax.numpy as jnp
        import numpy as np
        N_NODES = 50000
        N_EDGES = 12500
        FEAT_DIM = 128
        EMB_DIM = 64
        NUM_RELS = 8
        N, F = inputs.shape
        R = rel_emb.shape[0]
        triple = jnp.concatenate([inputs[src], inputs[dst], rel_emb[rel]], axis=-1)
        msg = triple @ W.T + b
        seg = rel.astype(jnp.int32) * N + dst.astype(jnp.int32)
        per_rel = jax.ops.segment_sum(msg, seg, num_segments=R * N)
        out = jnp.tanh(per_rel.reshape(R, N, F)).sum(axis=0)
        return out

    def _L2_gnn_ref(node_attr, edge_attr, edge_index, num_nodes, W_node, b_node, W_edge, b_edge):
        import jax, jax.numpy as jnp
        import numpy as np
        NEG_SLOPE = 0.2
        N, H = node_attr.shape
        src, dst = (edge_index[0], edge_index[1])
        h = node_attr @ W_node + b_node
        We, Ws, Wd = (W_edge[:H], W_edge[H:2 * H], W_edge[2 * H:])
        logits = (edge_attr @ We + h[src] @ Ws + h[dst] @ Wd + b_edge).reshape(-1)
        e = jax.nn.leaky_relu(logits, NEG_SLOPE)
        seg_max = jax.ops.segment_max(e, src, num_segments=N)
        exp_e = jnp.exp(e - seg_max[src])
        seg_sum = jax.ops.segment_sum(exp_e, src, num_segments=N)
        a = exp_e / seg_sum[src]
        agg = jax.ops.segment_sum(a[:, None] * h[dst], src, num_segments=N)
        return jax.nn.leaky_relu(h + agg, NEG_SLOPE)

    def _L3_gnn_ref(x, src, dst, edge_weight, w1, b1, w2, b2):
        import jax, jax.numpy as jnp
        import numpy as np
        N_NODES = 100000
        N_EDGES = 25000
        NFEAT = 128
        NHID = 64

        def _gcn_layer(h, src, dst, edge_weight, w, b, n_nodes):
            support = h @ w
            msgs = support[src] * edge_weight[:, None]
            agg = jax.ops.segment_sum(msgs, dst, num_segments=n_nodes)
            return agg + b
        n = x.shape[0]
        h = jax.nn.sigmoid(_gcn_layer(x, src, dst, edge_weight, w1, b1, n))
        out = jax.nn.sigmoid(_gcn_layer(h, src, dst, edge_weight, w2, b2, n))
        return out
    edge_index = jnp.stack([src, dst])
    x = _layernorm(x + _L0_gnn_ref(x, edge_index, L0_gnn_W, L0_gnn_b, L0_gnn_gamma, L0_gnn_beta), axis=-1)
    x = _layernorm(x + _L1_gnn_ref(x, L1_gnn_rel_emb, L1_gnn_W, L1_gnn_b, src, dst, edge_type_8), axis=-1)
    x = _layernorm(x + _L2_gnn_ref(x, edge_attr_128, edge_index, 100000, L2_gnn_W_node, L2_gnn_b_node, L2_gnn_W_edge, L2_gnn_b_edge), axis=-1)
    x = _layernorm(x + _L3_gnn_ref(x, src, dst, edge_weight, L3_gnn_w1, L3_gnn_b1, L3_gnn_w2, L3_gnn_b2), axis=-1)
    return x

_drawn_inputs = setup_inputs


def setup_inputs(seed=0):
    import zlib

    import numpy as np

    out = dict(_drawn_inputs(seed))
    spreads = {'L0_gnn_gamma': (1.0, 0.2),
     'L0_gnn_beta': (0.0, 0.1),
     'L3_gnn_b1': (0.0, 0.8),
     'L3_gnn_b2': (0.0, 0.339)}
    factors = {'edge_attr_128': 8.0,
     'edge_weight': 3.453,
     'L0_gnn_b': 7.084,
     'L1_gnn_b': 3.587,
     'L2_gnn_W_edge': 7.878,
     'L3_gnn_w1': 8.0}
    for name, (base, spread) in spreads.items():
        noise = np.random.default_rng([zlib.crc32(name.encode()), seed]).standard_normal(out[name].shape)
        drawn = base * np.exp(spread * noise) if base else spread * noise
        out[name] = jnp.asarray(drawn.astype(out[name].dtype))
    for name, factor in factors.items():
        out[name] = (out[name] * factor).astype(out[name].dtype)
    return out
```

```python
import concourse.bass as bass
from concourse import mybir
from contextlib import ExitStack

F32 = mybir.dt.float32
BF16 = mybir.dt.bfloat16
FP16 = mybir.dt.float16
I32 = mybir.dt.int32
ALU = mybir.AluOpType
ACT = mybir.ActivationFunctionType
AX = mybir.AxisListType

P = 125
K = 8
Q = 4
D = 128
HID = 64
RELS = 8
LOW_BITS = 9
BINS = 1 << LOW_BITS
EPS = 1e-5
SLOPE = 0.2
FAR = 1 << 20
COLS = 8
SRC, DST, REL, WEIGHT, LOGIT = range(5)


class Chain:

    def __init__(self, engine, sem, turn=0, steps=0, before=0, held=None):
        self.engine, self.sem, self.base, self.steps, self.n = engine, sem, turn * steps + before, steps, 0
        self.held = held

    def done(self, instruction):
        instruction.then_inc(self.sem, 1)
        self.n += 1
        self.engine.wait_ge(self.sem, self.base + self.n)

    def hold(self):
        self.engine.sem_inc(self.held, 1)

    def close(self):
        assert self.n == self.steps, (self.n, self.steps)


class Kernel:

    def __init__(self, nc, ctx, args, n_nodes, n_edges):
        self.nc, self.ctx = nc, ctx
        self.N, self.E = n_nodes, n_edges
        self.sorting = ExitStack()
        self.in_use, self.free = [], {"dma": [], "steps": []}
        self.tiles = n_edges // P
        self.turns = self.tiles // K
        assert n_edges % (P * K) == 0 and n_nodes % (P * K) == 0
        self.groups = n_nodes // (P * K)
        assert self.groups == 4 * self.turns
        self.arg = args

    def sb(self, name, shape, dt=F32):
        return self.ctx.enter_context(self.nc.sbuf_tensor(name, shape, dt))

    def sort_sb(self, name, shape, dt=F32):
        return self.sorting.enter_context(self.nc.sbuf_tensor(name, shape, dt))

    def semaphore(self, name):
        if "gathered" in name or "scattered" in name:
            return self.nc.alloc_semaphore(name)
        if any(x in name for x in ("loaded", "stored", "moved")):
            kind = "dma"
        else:
            kind = "steps"
        free = self.free[kind]
        s = free.pop(0) if free else self.nc.alloc_semaphore(name)
        self.in_use.append((kind, s))
        return s

    def recycle(self):
        with self.nc.Block() as block:
            @block.gpsimd
            def _(pool):
                for _, s in self.in_use:
                    pool.sem_clear(s)
        for kind, s in self.in_use:
            self.free[kind].append(s)
        self.in_use = []

    def dram(self, name, shape, dt=F32):
        return self.nc.dram_tensor(name, shape, dt, kind="Internal").ap()


def row(ap):
    return ap.rearrange("(a n) -> a n", a=1)


def column(ap):
    return ap.rearrange("(n a) -> n a", a=1)


def over(ap, partitions):
    return row(ap).to_broadcast([partitions, ap.shape[0]])


def prepare(k):
    nc = k.nc
    k.ident = k.sb("ident", [D, D])
    k.ones_row = k.sb("ones_row", [1, 512])
    k.ones3 = k.sb("ones3", [3, P], BF16)
    k.eps1 = k.sb("eps1", [D, 1])
    k.eps2 = k.sb("eps2", [D, 1])
    k.W0cat = k.sb("W0cat", [D, 2 * D])
    k.bias0 = k.sb("bias0", [3, 2, 2 * D], BF16)
    k.betaB = k.sb("betaB", [P, D])
    k.sig2B = k.sb("sig2B", [P, D])
    k.sig1B = k.sb("sig1B", [P, K * HID])
    k.W2cat = k.sb("W2cat", [D, 2 * D])
    k.W2edge = k.sb("W2edge", [D, 2 * D])
    k.bias2 = k.sb("bias2", [3, 2, 2 * D], BF16)
    k.bias2e = k.sb("bias2e", [3, 2, 2 * D], BF16)
    k.WeB = k.sb("WeB", [P, D])
    k.usB = k.sb("usB", [P, D])
    k.udB = k.sb("udB", [P, D])
    k.logit0 = k.sb("logit0", [P, 1])
    k.W1aT = k.sb("W1aT", [D, D])
    k.W1bT = k.sb("W1bT", [D, D])
    k.relC = k.sb("relC", [RELS, D])
    k.w1 = k.sb("w1", [D, HID])
    k.w2 = k.sb("w2", [HID, D])
    k.b1r = k.sb("b1r", [1, Q * HID])
    k.b2r = k.sb("b2r", [1, Q * D])
    with ExitStack() as own:
        def sb(name, shape, dt=F32):
            return own.enter_context(nc.sbuf_tensor(name, shape, dt))

        def sem(name):
            return k.semaphore((name))

        W0 = sb("W0", [D, D])
        W1 = sb("W1", [D, 2 * D + HID])
        Wn = sb("Wn", [D, D])
        WnT = sb("WnT", [D, D])
        W1cT = sb("W1cT", [HID, D])
        emb = sb("emb", [RELS, HID])
        embT = sb("embT", [HID, RELS])
        gammaB = sb("gammaB", [D, D])
        b0 = sb("b0", [1, D])
        bn = sb("bn", [1, D])
        bncol = sb("bncol", [D, 1])
        b1e = sb("b1e", [1, D])
        wsd = sb("wsd", [D, 3])
        wsB = sb("wsB", [D, 3, P])
        bedge = sb("bedge", [P, 1])
        b2B = sb("b2B", [P, D])
        b1B = sb("b1B", [P, HID])
        W0T = sb("W0T", [D, D])
        mean = sb("mean", [D, 2])
        biasrow = sb("biasrow", [1, 3, 2, 2 * D])
        rest = sb("rest", [1, 2 * D])
        parts = sb("parts", [1, 3, 3, 2, 2 * D], BF16)
        b12 = sb("b12", [1, HID + D])
        ps = own.enter_context(nc.psum_tensor("ps", [D, 8, 512], F32))

        loaded = sem("weights_loaded")
        moved = sem("bias_rows_moved")
        ident_set = sem("ident_set")
        steps = sem("prepare_steps")
        cols_spread = sem("cols_spread")
        transposed = sem("weights_transposed")
        copied = sem("weights_copied")
        multiplied = sem("weights_multiplied")
        sigmoids = sem("sigmoids")
        LOADS = 20

        with nc.Block() as block:
            @block.sync
            def _(sp):
                n = 0
                for to, of in [
                    (W0[:, :], k.arg["L0_gnn_W"]), (W1[:, :], k.arg["L1_gnn_W"]), (Wn[:, :], k.arg["L2_gnn_W_node"]),
                    (emb[:, :], k.arg["L1_gnn_rel_emb"]), (gammaB[:, :], over(k.arg["L0_gnn_gamma"], D)),
                    (k.betaB[:, :], over(k.arg["L0_gnn_beta"], P)), (b0[:, :], row(k.arg["L0_gnn_b"])),
                    (bn[:, :], row(k.arg["L2_gnn_b_node"])), (bncol[:, :], column(k.arg["L2_gnn_b_node"])),
                    (b1e[:, :], row(k.arg["L1_gnn_b"])),
                    (k.WeB[:, :], over(k.arg["L2_gnn_W_edge"].rearrange("n a -> (n a)")[0:D], P)),
                    (wsd[:, 0:1], k.arg["L2_gnn_W_edge"][D:2 * D, :]), (wsd[:, 1:2], k.arg["L2_gnn_W_edge"][2 * D:3 * D, :]),
                    (bedge[:, :], over(k.arg["L2_gnn_b_edge"], P)), (b2B[:, :], over(k.arg["L3_gnn_b2"], P)),
                    (b1B[:, :], over(k.arg["L3_gnn_b1"], P)), (k.w1[:, :], k.arg["L3_gnn_w1"]), (k.w2[:, :], k.arg["L3_gnn_w2"]),
                    (b12[:, 0:HID], row(k.arg["L3_gnn_b1"])), (b12[:, HID:], row(k.arg["L3_gnn_b2"])),
                ]:
                    sp.dma_start(to, of).then_inc(loaded, 16)
                    n += 1
                assert n == LOADS
                sp.wait_ge(copied, 4)
                for m, to in enumerate((k.bias0, k.bias2, k.bias2e)):
                    sp.dma_start(to[:, :, :], parts[:, m, :, :, :]).then_inc(moved, 16)
                sp.wait_ge(moved, 48)

            @block.gpsimd
            def _(pool):
                nc.gpsimd.memset(k.ident[:, :], 0.0).then_inc(ident_set, 1)
                pool.wait_ge(ident_set, 1)
                nc.gpsimd.affine_select(out=k.ident[:, :], in_=k.ident[:, :], compare_op=ALU.not_equal, fill=1.0,
                                        base=0, pattern=[[-1, D]], channel_multiplier=1).then_inc(ident_set, 1)

            @block.scalar
            def _(act):
                act.wait_ge(loaded, 16 * LOADS)
                nc.scalar.activation(k.sig2B[:, :], b2B[:, :], ACT.Sigmoid)
                for j in range(K):
                    nc.scalar.activation(k.sig1B[:, j * HID:(j + 1) * HID], b1B[:, :], ACT.Sigmoid).then_inc(sigmoids, 1)

            @block.tensor
            def _(pe):
                pe.wait_ge(loaded, 16 * LOADS)
                pe.wait_ge(ident_set, 2)
                nc.tensor.transpose(ps[:, 0, 0:D], W0[:, :], k.ident[:, :])
                nc.tensor.transpose(ps[:, 1, 0:D], W1[:, 0:D], k.ident[:, :])
                nc.tensor.transpose(ps[:, 2, 0:D], W1[:, D:2 * D], k.ident[:, :])
                nc.tensor.transpose(ps[0:HID, 3, 0:D], W1[:, 2 * D:], k.ident[:, :])
                nc.tensor.transpose(ps[0:HID, 4, 0:RELS], emb[:, :], k.ident[0:RELS, 0:RELS])
                nc.tensor.transpose(ps[:, 5, 0:D], Wn[:, :], k.ident[:, :]).then_inc(transposed, 1)
                pe.wait_ge(copied, 1)
                nc.tensor.matmul(ps[0:RELS, 0, 0:D], embT[:, :], W1cT[:, :], start=True, stop=False)
                nc.tensor.matmul(ps[0:RELS, 0, 0:D], k.ones_row[:, 0:RELS], b1e[:, :], start=False, stop=True)
                pe.wait_ge(cols_spread, 1)
                nc.tensor.matmul(ps[0:P, 1, 0:D], wsB[:, 0, :], WnT[:, :], start=True, stop=True)
                nc.tensor.matmul(ps[0:P, 2, 0:D], wsB[:, 1, :], WnT[:, :], start=True, stop=True)
                nc.tensor.matmul(ps[0:P, 3, 0:1], wsB[:, 2, :], bncol[:, :], start=True, stop=True).then_inc(multiplied, 1)

            @block.vector
            def _(dve):
                v = nc.vector
                c = Chain(dve, steps)
                dve.wait_ge(loaded, 16 * LOADS)
                v.memset(k.ones_row[:, :], 1.0)
                v.memset(k.ones3[:, :], 1.0)
                v.memset(k.eps1[:, :], EPS)
                v.memset(k.eps2[:, :], EPS * EPS)
                c.done(v.tensor_tensor(wsd[:, 2:3], wsd[:, 0:1], wsd[:, 1:2], ALU.add))
                v.tensor_scalar(wsB[:, :, :], wsd[:, :].unsqueeze(2).to_broadcast([D, 3, P]), 1.0, None,
                                ALU.mult).then_inc(cols_spread, 1)
                dve.wait_ge(transposed, 1)
                v.tensor_copy(k.W1aT[:, :], ps[:, 1, 0:D])
                v.tensor_copy(k.W1bT[:, :], ps[:, 2, 0:D])
                v.tensor_copy(W1cT[:, :], ps[0:HID, 3, 0:D])
                v.tensor_copy(embT[:, :], ps[0:HID, 4, 0:RELS])
                v.tensor_copy(WnT[:, :], ps[:, 5, 0:D])
                c.done(v.tensor_copy(W0T[:, :], ps[:, 0, 0:D]))
                v.tensor_reduce(mean[:, 0:1], W0T[:, :], AX.X, ALU.add)
                c.done(v.tensor_reduce(mean[0:1, 1:2], b0[:, :], AX.X, ALU.add))
                c.done(v.tensor_scalar(mean[:, 0:1], mean[:, 0:1], 1.0 / D, None, ALU.mult))
                c.done(v.tensor_scalar(mean[0:1, 1:2], mean[0:1, 1:2], 1.0 / D, None, ALU.mult))
                v.tensor_scalar(k.W0cat[:, 0:D], W0T[:, :], mean[:, 0:1], None, ALU.subtract).then_inc(copied, 1)
                dve.wait_ge(copied, 1)
                v.tensor_tensor(k.W0cat[:, D:], k.W0cat[:, 0:D], gammaB[:, :], ALU.mult)
                c.done(v.tensor_scalar(biasrow[:, 0, 0, 0:D], b0[:, :], mean[0:1, 1:2], None, ALU.subtract))
                v.tensor_tensor(biasrow[:, 0, 0, D:], biasrow[:, 0, 0, 0:D], gammaB[0:1, :], ALU.mult)
                v.tensor_scalar(biasrow[:, 1, 0, 0:D], bn[:, :], 1 - SLOPE, None, ALU.mult)
                v.tensor_scalar(biasrow[:, 1, 0, D:], bn[:, :], SLOPE, None, ALU.mult)
                v.tensor_scalar(biasrow[:, 2, 0, 0:D], bn[:, :], 2 * (1 - SLOPE), None, ALU.mult)
                v.tensor_scalar(biasrow[:, 2, 0, D:], bn[:, :], 2 * SLOPE, None, ALU.mult)
                v.tensor_scalar(k.W2cat[:, 0:D], Wn[:, :], 1 - SLOPE, None, ALU.mult)
                v.tensor_scalar(k.W2edge[:, 0:D], Wn[:, :], 1 - SLOPE, None, ALU.mult)
                c.done(v.tensor_scalar(k.W2edge[:, D:], Wn[:, :], SLOPE, None, ALU.mult))
                dve.wait_ge(ident_set, 2)
                c.done(v.tensor_tensor(k.W2cat[:, D:], k.W2edge[:, D:], k.ident[:, :], ALU.add))
                for m in range(3):
                    b = biasrow[:, m, 0, :]
                    c.done(v.tensor_copy(rest[:, :], b))
                    for part in range(3):
                        c.done(v.tensor_copy(parts[:, m, part, 0, :], rest[:, :]))
                        c.done(v.tensor_tensor(rest[:, :], rest[:, :], parts[:, m, part, 0, :], ALU.subtract))
                        c.done(v.tensor_copy(parts[:, m, part, 1, :], parts[:, m, part, 0, :]))
                    dve.sem_inc(copied, 1)
                for j in range(Q):
                    v.tensor_copy(k.b1r[:, j * HID:(j + 1) * HID], b12[:, 0:HID])
                    v.tensor_copy(k.b2r[:, j * D:(j + 1) * D], b12[:, HID:])
                dve.wait_ge(multiplied, 1)
                v.tensor_copy(k.relC[:, :], ps[0:RELS, 0, 0:D])
                v.tensor_copy(k.usB[:, :], ps[0:P, 1, 0:D])
                v.tensor_copy(k.udB[:, :], ps[0:P, 2, 0:D])
                v.tensor_tensor(k.logit0[:, :], ps[0:P, 3, 0:1], bedge[:, :], ALU.add)


def edge_table(k):
    nc = k.nc
    k.edges = k.sort_sb("edges", [P, k.tiles, COLS])
    k.digits = k.sort_sb("digits", [P, 2, k.tiles])
    k.bins = k.sort_sb("bins", [P, BINS], FP16)
    k.below = k.sort_sb("below", [P, 3, P], BF16)
    k.base = k.sort_sb("base", [1, 4, BINS])
    with ExitStack() as own:
        def sb(name, shape, dt=F32):
            return own.enter_context(nc.sbuf_tensor(name, shape, dt))

        def sem(name):
            return k.semaphore((name))

        raw = sb("raw", [P, 3, k.tiles], I32)
        split = sb("split", [P, 2, 2, k.tiles], I32)
        dig = sb("dig", [P, 4, k.tiles])
        weight = sb("weight", [P, k.tiles])
        attr = sb("attr", [P, K, D])
        prod = sb("prod", [P, 2, D])
        dot = sb("dot", [P, K])
        onehot = sb("onehot", [P, 8, BINS], BF16)
        ones_col = sb("ones_col", [P, 1], BF16)
        ones_bins = sb("ones_bins", [1, BINS])
        seen = sb("seen", [1, 4, BINS])
        guard = sb("guard", [1, COLS])
        count = own.enter_context(nc.psum_tensor("count", [1, 4, 512], F32))
        loaded = sem("edges_loaded")
        attr_loaded = sem("attr_loaded")
        attr_used = sem("attr_used")
        consts_set = sem("sort_consts_set")
        steps = sem("table_steps")
        loop_steps = sem("table_loop_steps")
        onehots = sem("onehots_ready")
        counted = sem("onehots_counted")
        guards = sem("guards_stored")
        attr_rows = k.arg["edge_attr_128"].rearrange("(p t) d -> p t d", p=P)

        with nc.Block() as block:
            @block.sync
            def _(sp):
                for n, a in enumerate((k.arg["src"], k.arg["dst"], k.arg["edge_type_8"])):
                    sp.dma_start(raw[:, n, :], a.rearrange("(p t) -> p t", p=P)).then_inc(loaded, 16)
                sp.dma_start(weight[:, :], k.arg["edge_weight"].rearrange("(p t) -> p t", p=P)).then_inc(loaded, 16)
                sp.wait_ge(consts_set, 5)
                for table in (k.by_src, k.by_dst):
                    sp.dma_start(table[0:1, :], guard[:, :]).then_inc(guards, 16)
                with sp.Fori(0, k.turns) as i:
                    sp.wait_ge(attr_used, i * K)
                    sp.dma_start(attr[:, :, :], attr_rows[:, bass.ds(i * K, K), :]).then_inc(attr_loaded, 16)
                sp.wait_ge(guards, 32)

            @block.gpsimd
            def _(pool):
                g = nc.gpsimd
                g.iota(k.bins[:, :], [[1, BINS]], base=0, channel_multiplier=0,
                       allow_small_or_imprecise_dtypes=True).then_inc(consts_set, 1)
                g.memset(k.below[:, :, :], 1.0).then_inc(consts_set, 1)
                pool.wait_ge(consts_set, 2)
                g.affine_select(out=k.below[:, 0, :], in_=k.below[:, 0, :], compare_op=ALU.is_gt, fill=0.0,
                                base=0, pattern=[[1, P]], channel_multiplier=-1).then_inc(consts_set, 1)
                g.affine_select(out=k.below[:, 1, :], in_=k.below[:, 1, :], compare_op=ALU.is_ge, fill=0.0,
                                base=0, pattern=[[-1, P]], channel_multiplier=1).then_inc(consts_set, 1)
                g.memset(guard[:, :], -1.0).then_inc(consts_set, 1)

            @block.tensor
            def _(pe):
                pe.wait_ge(steps, 1)
                with pe.Fori(0, k.tiles // 2) as i:
                    for t in range(2):
                        for m in range(4):
                            pe.wait_ge(onehots, i * 8 + t * 4 + m + 1)
                            nc.tensor.matmul(count[:, m, :], ones_col[:, :], onehot[:, t * 4 + m, :], start=False,
                                             stop=True, skip_group_check=True).then_inc(counted, 1)

            @block.vector
            def _(dve):
                v = nc.vector
                c = Chain(dve, steps)
                v.memset(ones_col[:, :], 1.0)
                v.memset(ones_bins[:, :], 1.0)
                c.done(v.memset(count[:, :, :], 0.0))
                dve.wait_ge(loaded, 64)
                v.memset(k.edges[:, :, :], 0.0)
                for n in range(2):
                    v.tensor_scalar(split[:, n, 0, :], raw[:, n, :], BINS - 1, None, ALU.bitwise_and)
                    c.done(v.tensor_scalar(split[:, n, 1, :], raw[:, n, :], LOW_BITS, None,
                                           ALU.logical_shift_right))
                v.tensor_copy(dig[:, :, :], split[:, :, :, :].rearrange("p a b t -> p (a b) t"))
                c.done(v.tensor_copy(k.edges[:, :, 0:3], raw[:, :, :].rearrange("p n t -> p t n")))
                c.done(v.tensor_copy(k.edges[:, :, WEIGHT], weight[:, :]))
                dve.wait_ge(consts_set, 4)
                with dve.Fori(0, k.turns) as i:
                    dve.wait_ge(attr_loaded, i * 16 + 16)
                    c1 = Chain(dve, loop_steps, i, K + 1)
                    for t in range(K):
                        c1.done(v.tensor_tensor_reduce(out=prod[:, t % 2, :], in0=attr[:, t, :], in1=k.WeB[:, :],
                                                       scale=1.0, scalar=0.0, op0=ALU.mult, op1=ALU.add,
                                                       accum_out=dot[:, t:t + 1]))
                        dve.sem_inc(attr_used, 1)
                    c1.done(v.tensor_copy(k.edges[:, bass.ds(i * K, K), LOGIT], dot[:, :]))
                    c1.close()
                    for t in range(K):
                        for m in range(4):
                            if t >= 2:
                                dve.wait_ge(counted, i * K * 4 + (t - 2) * 4 + m + 1)
                            else:
                                dve.wait_ge(counted, i * K * 4)
                            v.tensor_scalar(onehot[:, (t % 2) * 4 + m, :], k.bins[:, :],
                                            dig[:, m, bass.ds(i * K + t, 1)], None,
                                            ALU.is_equal).then_inc(onehots, 1)
                dve.wait_ge(counted, k.tiles * 4)
                c.done(v.tensor_copy(seen[:, :, :], count[:, :, :]))
                for m in range(4):
                    c.done(v.tensor_tensor_scan(k.base[:, m, :], ones_bins[:, :], seen[:, m, :], 0.0,
                                                ALU.mult, ALU.add))
                c.done(v.tensor_tensor(k.base[:, :, :], k.base[:, :, :], seen[:, :, :], ALU.subtract))
                c.done(v.tensor_scalar(k.base[:, :, :], k.base[:, :, :], 1.0, None, ALU.add))
                for m in range(2):
                    c.done(v.tensor_copy(k.digits[:, m, :], dig[:, 2 * m, :]))


def radix_pass(k, name, base, load, digits, into):
    nc = k.nc
    with ExitStack() as own:
        def sb(what, shape, dt=F32):
            return own.enter_context(nc.sbuf_tensor(f"{what}_{name}", shape, dt))

        def sem(what):
            return k.semaphore((f"{what}_{name}"))

        onehot = sb("onehot", [P, K, BINS], BF16)
        picked = sb("picked", [P, 2, BINS])
        place = sb("place", [P, K])
        place_i = sb("place_i", [P, K], I32)
        payload = sb("payload", [P, K, COLS])
        rows = k.edges if load is None else sb("rows", [P, k.tiles, COLS])
        high = sb("high", [P, 2, k.tiles], I32)
        highf = sb("highf", [P, k.tiles])
        rank = own.enter_context(nc.psum_tensor(f"rank_{name}", [P, 2, 512], F32))
        loaded, steps, loop_steps = sem("rows_loaded"), sem("digit_steps"), sem("radix_steps")
        based, onehots, ranked = sem("bases_in"), sem("onehots"), sem("ranked")
        placed, read = sem("placed"), sem("ranks_read")
        scattered = [sem("scattered_a"), sem("scattered_b")]
        halves_taken = sem("halves_taken")
        key = digits if load is not None else None

        with nc.Block() as block:
            @block.sync
            def _(sp):
                if load is not None:
                    sp.dma_start(rows[:, :, :], load[1:k.E + 1, :].rearrange("(t p) w -> p t w", p=P)).then_inc(loaded, 16)

            @block.gpsimd
            def _(pool):
                with pool.Fori(0, k.turns) as i:
                    for h in range(2):
                        pool.wait_ge(placed, i * 2 + h + 1)
                        pool.sem_inc(halves_taken, 1)
                        for t in range(h * Q, h * Q + Q):
                            nc.gpsimd.indirect_dma_start(
                                into, bass.IndirectOffsetOnAxis(ap=place_i[:, t:t + 1], axis=0),
                                payload[:, t, :], None).then_inc(scattered[h], 16)
                for h in range(2):
                    pool.wait_ge(scattered[h], k.turns * Q * 16)

            @block.tensor
            def _(pe):
                def add(bank, mask, slot):
                    return nc.tensor.matmul(rank[:, bank, :], k.below[:, mask, :], onehot[:, slot, :],
                                            start=False, stop=True, skip_group_check=True)

                for bank in range(2):
                    nc.tensor.matmul(rank[:, bank, :], k.ones_row[:, 0:P], k.base[:, base, :],
                                     start=True, stop=True, skip_group_check=True)
                pe.wait_ge(based, 1)
                with pe.Fori(0, k.turns) as i:
                    for t in range(K):
                        pe.wait_ge(read, i * K + max(t - 1, 0))
                        add(t % 2, 1, (t - 2) % K)
                        add(t % 2, 2, (t - 1) % K)
                        pe.wait_ge(onehots, i * K + t + 1)
                        add(t % 2, 0, t).then_inc(ranked, 1)

            @block.vector
            def _(dve):
                v = nc.vector
                c = Chain(dve, steps)
                v.memset(onehot[:, K - 2:, :], 0.0).then_inc(based, 1)
                if load is None:
                    dig = k.digits[:, digits, :]
                else:
                    dve.wait_ge(loaded, 16)
                    c.done(v.tensor_copy(high[:, 0, :], rows[:, :, key]))
                    c.done(v.tensor_scalar(high[:, 1, :], high[:, 0, :], LOW_BITS, None, ALU.logical_shift_right))
                    c.done(v.tensor_copy(highf[:, :], high[:, 1, :]))
                    dig = highf[:, :]
                with dve.Fori(0, k.turns) as i:
                    c1 = Chain(dve, loop_steps, i, K + 2)

                    def mark(t, after):
                        dve.wait_ge(ranked, after)
                        v.tensor_scalar(onehot[:, t, :], k.bins[:, :], dig[:, bass.ds(i * K + t, 1)], None,
                                        ALU.is_equal).then_inc(onehots, 1)

                    for h in range(2):
                        for t in range(h * Q, h * Q + Q):
                            mark(t, i * K + max(t - 5, 0))
                        for t in range(h * Q, h * Q + Q):
                            dve.wait_ge(ranked, i * K + t + 1)
                            c1.done(v.tensor_tensor_reduce(out=picked[:, t % 2, :], in0=rank[:, t % 2, :],
                                                           in1=onehot[:, t, :], scale=1.0, scalar=0.0,
                                                           op0=ALU.mult, op1=ALU.add, accum_out=place[:, t:t + 1]))
                            dve.sem_inc(read, 1)
                        s = slice(h * Q, h * Q + Q)
                        dve.wait_ge(scattered[h], i * Q * 16)
                        v.tensor_copy(payload[:, s, :], rows[:, bass.ds(i * K + h * Q, Q), :])
                        c1.done(v.tensor_copy(place_i[:, s], place[:, s]))
                        dve.sem_inc(placed, 1)
                    c1.close()


def moments(k, c, stats, mv, s):
    for j in range(Q):
        ins = k.nc.vector.bn_stats(stats[:, j, :], s[:, j, :])
    c.done(ins)
    c.hold()
    for j in range(Q):
        ins = k.nc.vector.bn_aggr(mv[:, j, :], stats[:, j, :])
    return ins


def shifts(k, c, rs, nm, mv, std):
    c.done(k.nc.vector.reciprocal(rs, std))
    return k.nc.vector.scalar_tensor_tensor(nm, mv[:, :, 0], -1.0, rs, ALU.mult, ALU.mult)


def normalise(k, out, s, rs, nm):
    for j in range(Q):
        ins = k.nc.scalar.activation(out[:, j, :], s[:, j, :], ACT.Identity, bias=nm[:, j:j + 1],
                                     scale=rs[:, j:j + 1])
    return ins


def transpose_quad(k, out, x, rows=P):
    for j in range(Q):
        ins = k.nc.tensor.transpose(out[:, j, 0:rows], x[:, j, :], k.ident[0:rows, 0:rows])
    return ins


def project(k, out, xT, weights, bias3):
    for b in range(2):
        k.nc.tensor.matmul(out[:, b, :, :], k.ones3[:, :], bias3[:, :, :], start=True, stop=False,
                           skip_group_check=True)
        for j in range(2):
            ins = k.nc.tensor.matmul(out[:, b, j, :], xT[:, 2 * b + j, 0:P], weights[:, :], start=False,
                                     stop=True, skip_group_check=True)
    return ins


def halves(sp, to, of, sem):
    sp.dma_start(to[0:112], of[0:112]).then_inc(sem, 16)
    sp.dma_start(to[112:P], of[112:P]).then_inc(sem, 16)


def pairs(quad):
    return quad[:, :, :].rearrange("p (a b) d -> p a b d", a=2)


class Dense:

    def __init__(self, k):
        nc = k.nc
        self.k = k
        own = k.own = ExitStack()

        def sb(name, shape, dt=F32):
            return [own.enter_context(nc.sbuf_tensor(f"dense_{name}{q}", shape, dt)) for q in range(2)]

        def sem(name):
            return k.semaphore((f"dense_{name}"))

        self.own = own
        self.x, self.s, self.x1 = (sb(n, [P, Q, D]) for n in ("x", "s", "x1"))
        self.s3, self.s4, self.x4 = (sb(n, [P, Q, D]) for n in ("s3", "s4", "x4"))
        self.x23 = sb("x23", [P, Q, 2 * D])
        self.x2, self.x3 = [b[:, :, 0:D] for b in self.x23], [b[:, :, D:] for b in self.x23]
        self.xT = sb("xT", [D, Q, D])
        self.junk = sb("junk", [P, D])
        self.ss, self.std0, self.rs0 = (sb(n, [P, Q]) for n in ("ss", "std0", "rs0"))
        self.stats, self.mv = sb("stats", [P, Q, 6]), sb("mv", [P, Q, 2])
        self.std, self.rs, self.nm = (sb(n, [P, 2, Q]) for n in ("std", "rs", "nm"))
        self.T = [own.enter_context(nc.psum_tensor(f"dense_T{q}", [D, Q, D], F32)) for q in range(2)]
        self.O = [own.enter_context(nc.psum_tensor(f"dense_O{q}", [P, 2, 2, 2 * D], F32)) for q in range(2)]
        self.on = {}
        self.x_in = [sem(f"x_loaded{q}") for q in range(2)]
        self.stored12 = [sem(f"stored12_{q}") for q in range(2)]
        self.stored34 = [sem(f"stored34_{q}") for q in range(2)]
        self.stored_h = sem("stored_h")
        for name in ("t1", "c1", "o1", "square", "std0_ready", "summed", "mv1", "std1", "nm1", "x12", "t2", "c2", "o2",
                     "summed3", "mv3", "std3", "nm3", "x3_ready", "s4_ready", "mv4", "std4", "nm4", "x4_ready", "relu", "held",
                     "steps"):
            self.on[name] = sem(name)

    def rows(self, table, g, q):
        return table[bass.ds(g * (P * K), P * K), :].rearrange("(p j) d -> p j d", p=P)[:, q * Q:q * Q + Q, :]

    def sync(self, sp, g):
        k = self.k
        for q in range(2):
            sp.wait_ge(self.on["summed"], g * 2)
            halves(sp, self.x[q], self.rows(k.arg["x"], g, q), self.x_in[q])
        sp.dma_start(k.h1[bass.ds(g * (P * K), P * K), :].rearrange("(p j) d -> p (j d)", p=P),
                     k.sig1B[:, :]).then_inc(self.stored_h, 16)
        for q in range(2):
            sp.wait_ge(self.on["x12"], g * 2 + q + 1)
            halves(sp, self.rows(k.x1, g, q), self.x1[q], self.stored12[q])
        for q in range(2):
            sp.wait_ge(self.on["x4_ready"], g * 2 + q + 1)
            halves(sp, self.rows(k.x23, g, q), self.x23[q], self.stored34[q])
            halves(sp, self.rows(k.arg["out"], g, q), self.x4[q], self.stored34[q])

    def sync_end(self, sp):
        k = self.k
        for q in range(2):
            sp.wait_ge(self.stored12[q], 32 * k.groups)
            sp.wait_ge(self.stored34[q], 64 * k.groups)
        sp.wait_ge(self.stored_h, 16 * k.groups)

    def tensor(self, pe, g):
        k = self.k
        for q in range(2):
            pe.wait_ge(self.x_in[q], 32 * g + 32)
            pe.wait_ge(self.on["c2"], g * 2)
            transpose_quad(k, self.T[q], self.x[q]).then_inc(self.on["t1"], 1)
        for q in range(2):
            pe.wait_ge(self.on["c1"], g * 2 + q + 1)
            pe.wait_ge(self.on["summed3"], g * 2)
            project(k, self.O[q], self.xT[q], k.W0cat, k.bias0).then_inc(self.on["o1"], 1)
        for q in range(2):
            pe.wait_ge(self.on["x12"], g * 2 + q + 1)
            transpose_quad(k, self.T[q], self.x2[q]).then_inc(self.on["t2"], 1)
        for q in range(2):
            pe.wait_ge(self.on["c2"], g * 2 + q + 1)
            pe.wait_ge(self.on["summed"], g * 2 + q + 1)
            project(k, self.O[q], self.xT[q], k.W2cat, k.bias2).then_inc(self.on["o2"], 1)

    def scalar(self, act, g):
        k, a = self.k, self.k.nc.scalar
        for q in range(2):
            act.wait_ge(self.on["t1"], g * 2 + q + 1)
            act.wait_ge(self.on["o2"], g * 2)
            a.activation(self.xT[q][:, :, 0:P], self.T[q][:, :, 0:P], ACT.Copy).then_inc(self.on["c1"], 1)
        for q in range(2):
            act.wait_ge(self.on["o1"], g * 2 + q + 1)
            for j in range(Q):
                ins = a.activation(self.junk[q][:, :], self.O[q][:, j // 2, j % 2, 0:D], ACT.Square,
                                   accum_out=self.ss[q][:, j:j + 1])
                ins.then_inc(self.on["square"], 1)
                act.wait_ge(self.on["square"], g * 2 * Q + q * Q + j + 1)
            a.activation(self.std0[q][:, :], self.ss[q][:, :], ACT.Sqrt, bias=k.eps1[0:P, :],
                         scale=1.0 / D).then_inc(self.on["std0_ready"], 1)
        for q in range(2):
            act.wait_ge(self.on["mv1"], g * 2 + q + 1)
            a.activation(self.std[q][:, 0, :], self.mv[q][:, :, 1], ACT.Sqrt, bias=k.eps1[0:P, :])
            a.activation(self.std[q][:, 1, :], self.mv[q][:, :, 1], ACT.Sqrt, bias=k.eps2[0:P, :],
                         scale=1.0 + EPS).then_inc(self.on["std1"], 1)
        for q in range(2):
            act.wait_ge(self.on["nm1"], g * 2 + q + 1)
            act.wait_ge(self.stored12[q], 32 * g)
            act.wait_ge(self.stored34[q], 64 * g)
            normalise(k, self.x1[q], self.s[q], self.rs[q][:, 0, :], self.nm[q][:, 0, :])
            normalise(k, self.x2[q], self.s[q], self.rs[q][:, 1, :], self.nm[q][:, 1, :]).then_inc(self.on["x12"], 1)
        for q in range(2):
            act.wait_ge(self.on["t2"], g * 2 + q + 1)
            a.activation(self.xT[q][:, :, 0:P], self.T[q][:, :, 0:P], ACT.Copy).then_inc(self.on["c2"], 1)
        for q in range(2):
            act.wait_ge(self.on["o2"], g * 2 + q + 1)
            a.activation(pairs(self.s4[q]), self.O[q][:, :, :, 0:D], ACT.Relu).then_inc(self.on["relu"], 1)
        for q in range(2):
            act.wait_ge(self.on["mv3"], g * 2 + q + 1)
            a.activation(self.std[q][:, 0, :], self.mv[q][:, :, 1], ACT.Sqrt,
                         bias=k.eps1[0:P, :]).then_inc(self.on["std3"], 1)
        for q in range(2):
            act.wait_ge(self.on["nm3"], g * 2 + q + 1)
            act.wait_ge(self.stored34[q], 64 * g)
            normalise(k, self.x3[q], self.s3[q], self.rs[q][:, 0, :],
                      self.nm[q][:, 0, :]).then_inc(self.on["x3_ready"], 1)
        for q in range(2):
            act.wait_ge(self.on["mv4"], g * 2 + q + 1)
            a.activation(self.std[q][:, 0, :], self.mv[q][:, :, 1], ACT.Sqrt,
                         bias=k.eps1[0:P, :]).then_inc(self.on["std4"], 1)
        for q in range(2):
            act.wait_ge(self.on["nm4"], g * 2 + q + 1)
            normalise(k, self.x4[q], self.s4[q], self.rs[q][:, 0, :],
                      self.nm[q][:, 0, :]).then_inc(self.on["x4_ready"], 1)

    STEPS = 2 * 10

    def vector(self, dve, g):
        k, v = self.k, self.k.nc.vector
        c = Chain(dve, self.on["steps"], g, self.STEPS, held=self.on["held"])
        both = [P, Q, D]
        for q in range(2):
            dve.wait_ge(self.on["std0_ready"], g * 2 + q + 1)
            c.done(v.reciprocal(self.rs0[q][:, :], self.std0[q][:, :]))
            dve.wait_ge(self.on["x4_ready"], g * 2)
            for j in range(Q):
                ins = v.scalar_tensor_tensor(self.s[q][:, j, :], self.O[q][:, j // 2, j % 2, D:],
                                             self.rs0[q][:, j:j + 1], k.betaB[:, :], ALU.mult, ALU.add)
            c.done(ins)
            c.done(v.scalar_tensor_tensor(self.s[q][:, :, :], self.s[q][:, :, :], 0.0, self.x[q][:, :, :],
                                          ALU.max, ALU.add))
            dve.sem_inc(self.on["summed"], 1)
            moments(k, c, self.stats[q], self.mv[q], self.s[q]).then_inc(self.on["mv1"], 1)
        for q in range(2):
            dve.wait_ge(self.on["std1"], g * 2 + q + 1)
            c.done(v.reciprocal(self.rs[q][:, :, :], self.std[q][:, :, :]))
            for m in range(2):
                ins = v.scalar_tensor_tensor(self.nm[q][:, m, :], self.mv[q][:, :, 0], -1.0, self.rs[q][:, m, :],
                                             ALU.mult, ALU.mult)
            ins.then_inc(self.on["nm1"], 1)
        for q in range(2):
            dve.wait_ge(self.on["relu"], g * 2 + q + 1)
            c.done(v.tensor_tensor(pairs(self.s3[q]), self.O[q][:, :, :, D:], pairs(self.s4[q]), ALU.add))
            dve.sem_inc(self.on["summed3"], 1)
            moments(k, c, self.stats[q], self.mv[q], self.s3[q]).then_inc(self.on["mv3"], 1)
        for q in range(2):
            dve.wait_ge(self.on["std3"], g * 2 + q + 1)
            shifts(k, c, self.rs[q][:, 0, :], self.nm[q][:, 0, :], self.mv[q], self.std[q][:, 0, :]).then_inc(
                self.on["nm3"], 1)
        for q in range(2):
            dve.wait_ge(self.on["x3_ready"], g * 2 + q + 1)
            v.tensor_tensor(self.s4[q][:, :, :], self.x3[q][:, :, :],
                            k.sig2B[:, :].unsqueeze(1).to_broadcast(both), ALU.add).then_inc(self.on["s4_ready"], 1)
            dve.wait_ge(self.on["s4_ready"], g * 2 + q + 1)
            moments(k, c, self.stats[q], self.mv[q], self.s4[q]).then_inc(self.on["mv4"], 1)
        for q in range(2):
            dve.wait_ge(self.on["std4"], g * 2 + q + 1)
            shifts(k, c, self.rs[q][:, 0, :], self.nm[q][:, 0, :], self.mv[q], self.std[q][:, 0, :]).then_inc(
                self.on["nm4"], 1)
        c.close()


def dense_alone(k):
    dense = Dense(k)
    with k.nc.Block() as block:
        @block.sync
        def _(sp):
            with sp.Fori(0, k.groups) as g:
                dense.sync(sp, g)
            dense.sync_end(sp)

        @block.tensor
        def _(pe):
            with pe.Fori(0, k.groups) as g:
                dense.tensor(pe, g)

        @block.scalar
        def _(act):
            with act.Fori(0, k.groups) as g:
                dense.scalar(act, g)

        @block.vector
        def _(dve):
            with dve.Fori(0, k.groups) as g:
                dense.vector(dve, g)
    dense.own.close()


class Order:

    def __init__(self, k, name, table, key):
        nc = k.nc
        self.k, self.key = k, key
        own = self.own = ExitStack()

        def sb(what, shape, dt=F32):
            return own.enter_context(nc.sbuf_tensor(f"{name}_{what}", shape, dt))

        def sem(what):
            return k.semaphore((f"{name}_{what}"))

        self.cols = sb("cols", [P, k.tiles, COLS])
        self.ids = sb("ids", [P, 6, k.tiles + K], I32)
        self.lead = sb("lead", [P, 2, k.tiles], I32)
        self.keyB = sb("keyB", [P, k.E + 1])
        keys = k.dram(f"{name}_keys", (1, k.E + 1))
        with ExitStack() as tmp:
            raw = tmp.enter_context(nc.sbuf_tensor(f"{name}_raw", [P, k.tiles, COLS], F32))
            before = tmp.enter_context(nc.sbuf_tensor(f"{name}_before", [P, k.tiles, 1], F32))
            same = tmp.enter_context(nc.sbuf_tensor(f"{name}_same", [P, k.tiles], F32))
            end = tmp.enter_context(nc.sbuf_tensor(f"{name}_end", [1, 1], F32))
            loaded, keys_out, keys_in, steps = (sem(x) for x in ("loaded", "keys_stored", "keys_loaded", "steps"))
            with nc.Block() as block:
                @block.sync
                def _(sp):
                    sp.dma_start(raw[:, :, :], table[1:k.E + 1, :].rearrange("(t p) w -> p t w", p=P)).then_inc(loaded, 16)
                    sp.dma_start(before[:, :, :], table[0:k.E, key:key + 1].rearrange("(t p) w -> p t w", p=P),
                                 allow_slow_non_contiguous=True).then_inc(loaded, 16)
                    sp.wait_ge(loaded, 32)
                    sp.wait_ge(steps, 1)
                    sp.dma_start(keys[:, 0:k.E].rearrange("a (t p) -> p t a", p=P),
                                 raw[:, :, key:key + 1], allow_slow_non_contiguous=True).then_inc(keys_out, 16)
                    sp.dma_start(keys[:, k.E:], end[:, :]).then_inc(keys_out, 16)
                    sp.wait_ge(keys_out, 32)
                    sp.dma_start(self.keyB[0:112, :], keys.to_broadcast([112, k.E + 1])).then_inc(keys_in, 16)
                    sp.dma_start(self.keyB[112:P, :], keys.to_broadcast([P - 112, k.E + 1])).then_inc(keys_in, 16)
                    sp.wait_ge(keys_in, 32)

                @block.vector
                def _(dve):
                    v = nc.vector
                    c = Chain(dve, steps)
                    c.done(v.memset(end[:, :], -1.0))
                    dve.wait_ge(loaded, 32)
                    v.memset(self.ids[:, :, k.tiles:], 0)
                    c.done(v.tensor_copy(self.cols[:, :, :], raw[:, ::-1, :]))
                    ends = self.cols[:, :, 0:2].rearrange("p t w -> p w t")
                    v.tensor_copy(self.ids[:, 0:2, 0:k.tiles], ends)
                    v.tensor_scalar(self.ids[:, 2:4, 0:k.tiles], ends, 2.0, None, ALU.mult)
                    v.tensor_scalar(self.ids[:, 4:6, 0:k.tiles], ends, 2.0, 1.0, ALU.mult, ALU.add)
                    c.done(v.tensor_tensor(same[:, :], self.cols[:, :, key], before[:, ::-1, 0], ALU.is_equal))
                    c.done(v.scalar_tensor_tensor(same[:, :], same[:, :], float(FAR), self.cols[:, :, key],
                                                  ALU.mult, ALU.add))
                    v.tensor_copy(self.lead[:, 0, :], same[:, :])
                    v.tensor_scalar(self.lead[:, 1, :], same[:, :], 2.0, 1.0, ALU.mult, ALU.add)


class Stage:

    def __init__(self, k, name, order):
        self.k, self.name, self.order = k, name, order
        self.own = ExitStack()
        self.on = {}
        self.ix = self.sb("ix", [P, 2, 2, Q], I32)
        self.lx = self.sb("lx", [P, 2, 2, Q], I32)
        self.idx_copied, self.pool_held = self.sem("idx_copied"), self.sem("pool_held")
        self.stats = [self.sb(f"stats{q}", [P, Q, 6]) for q in range(2)]
        self.mv = [self.sb(f"mv{q}", [P, Q, 2]) for q in range(2)]
        self.std, self.rs, self.nm = ([self.sb(f"{n}{q}", [P, Q]) for q in range(2)] for n in ("std", "rs", "nm"))
        self.v_steps, self.v_held = self.sem("v_steps"), self.sem("v_held")

    def sb(self, what, shape, dt=F32):
        return self.own.enter_context(self.k.nc.sbuf_tensor(f"{self.name}_{what}", shape, dt))

    def quads(self, what, shape, dt=F32):
        return [self.sb(f"{what}{q}", shape, dt) for q in range(2)]

    def ps(self, what, shape):
        return self.own.enter_context(self.k.nc.psum_tensor(f"{self.name}_{what}", shape, F32))

    def sem(self, what):
        return self.k.semaphore((f"{self.name}_{what}"))

    def sems(self, *names):
        for n in names:
            self.on[n] = self.sem(n)

    def segments(self):
        self.sel = self.quads("sel", [P, Q, P])
        self.cm = self.quads("cm", [1, Q, P])
        self.sems("masks", "total", "carried", "totals_used")

    def gathers(self, ids, *of):
        self.gather_list, self.gather_ids = of, ids
        self.gathered = [[self.sem(f"gathered{n}_{q}") for q in range(2)] for n in range(len(of))]

    def scatters(self, *of):
        self.scatter_list = of
        self.scattered = [[self.sem(f"scattered{n}_{q}") for q in range(2)] for n in range(len(of))]

    def gpsimd(self, pool, freed):
        k, g = self.k, self.k.nc.gpsimd

        def gather(c, turn, q):
            c.done(g.tensor_copy(self.ix[:, q, 0:len(self.gather_list), :],
                                 self.order.ids[:, self.gather_ids, bass.ds(turn * K + q * Q, Q)]))
            c.hold()
            for n, (table, to, width) in enumerate(self.gather_list):
                for j in range(Q):
                    g.indirect_dma_start(to[q][:, j, 0:width], None, table,
                                         bass.IndirectOffsetOnAxis(ap=self.ix[:, q, n, j:j + 1], axis=0)
                                         ).then_inc(self.gathered[n][q], 16)

        if self.gather_list:
            first = Chain(pool, self.idx_copied, held=self.pool_held)
            for q in range(2):
                gather(first, 0, q)
        steps = 2 * bool(self.scatter_list) + 2 * bool(self.gather_list)
        with pool.Fori(0, k.turns) as i:
            c = Chain(pool, self.idx_copied, i, steps, 2 * bool(self.gather_list), held=self.pool_held)
            for q in range(2):
                if self.scatter_list:
                    for n in range(len(self.scatter_list)):
                        pool.wait_ge(self.scattered[n][q], i * Q * 16)
                        c.hold()
                    c.done(g.tensor_copy(self.lx[:, q, :, :], self.order.lead[:, :, bass.ds(i * K + q * Q, Q)]))
                    c.hold()
                for n, (table, of, width, ready, lead) in enumerate(self.scatter_list):
                    pool.wait_ge(ready, i * 2 + q + 1)
                    c.hold()
                    for j in range(Q):
                        g.indirect_dma_start(table, bass.IndirectOffsetOnAxis(ap=self.lx[:, q, lead, j:j + 1], axis=0),
                                             of[q][:, j, 0:width], None, bounds_check=table.shape[0] - 1,
                                             oob_is_err=False).then_inc(self.scattered[n][q], 16)
                if self.gather_list:
                    for freed_by, count in freed(i, q):
                        pool.wait_ge(freed_by, count)
                        c.hold()
                    gather(c, i + 1, q)
            c.close()
        for q in range(2):
            for n in range(len(self.gather_list)):
                pool.wait_ge(self.gathered[n][q], (k.turns + 1) * Q * 16)
            for n in range(len(self.scatter_list)):
                pool.wait_ge(self.scattered[n][q], k.turns * Q * 16)

    def window(self, i, q, j):
        return (i * K) * (-P) + (self.k.tiles - 1 - q * Q - j) * P

    def masks(self, dve, i, q):
        v, o = self.k.nc.vector, self.order
        dve.wait_ge(self.on["total"], i * K)
        for j in range(Q):
            at = self.window(i, q, j)
            v.tensor_scalar(self.sel[q][:, j, :], o.keyB[:, bass.ds(at, P)],
                            o.cols[:, bass.ds(i * K + q * Q + j, 1), o.key], None, ALU.is_equal)
            ins = v.tensor_scalar(self.cm[q][:, j, :], o.keyB[0:1, bass.ds(at, P)], o.keyB[0:1, bass.ds(at + P, 1)],
                                  None, ALU.is_equal)
        ins.then_inc(self.on["masks"], 1)

    def totals(self, pe, i, q, out, rows, carry):
        t = self.k.nc.tensor
        pe.wait_ge(self.on["masks"], i * 2 + q + 1)
        for j in range(Q):
            n = q * Q + j
            pe.wait_ge(self.on["carried"], i * K + n + 1)
            t.matmul(out(j), self.sel[q][:, j, :], rows(j), start=True, stop=False, skip_group_check=True)
            t.matmul(out(j), self.cm[q][:, j, :], carry(n), start=False, stop=True,
                     skip_group_check=True).then_inc(self.on["total"], 1)

    def carry_on(self, act, i, q, j, to, of):
        act.wait_ge(self.on["total"], i * K + q * Q + j + 1)
        self.k.nc.scalar.activation(to, of, ACT.Copy).then_inc(self.on["carried"], 1)


def layer0(k, order):
    nc = k.nc
    st = Stage(k, "l0", order)
    XS, XD = st.quads("xs", [P, Q, D + 4]), st.quads("xd", [P, Q, D])
    mean, s, x1 = (st.quads(n, [P, Q, D]) for n in ("mean", "s", "x1"))
    aT = st.quads("aT", [D, Q, D])
    junk, ss = st.quads("junk", [P, D]), st.quads("ss", [P, Q])
    deg, std0, rs0 = (st.quads(n, [P, Q]) for n in ("deg", "std0", "rs0"))
    W = D + 1
    carry = st.sb("carry", [1, K, W])
    T = [st.ps(f"T{q}", [D, Q, D]) for q in range(2)]
    O = [st.ps(f"O{q}", [P, 2, 2, 2 * D]) for q in range(2)]
    tot = st.ps("tot", [P, 2, 2, 2 * D])
    st.segments()
    st.sems("mean_ready", "t1", "c1", "o1", "square", "std0", "summed", "mv", "std", "nm", "x1_ready")
    st.gathers(slice(0, 2), (k.arg["x"], XS, D), (k.arg["x"], XD, D))
    st.scatters((k.x1, x1, D, st.on["x1_ready"], 0))

    with nc.Block() as block:
        @block.gpsimd
        def _(pool):
            st.gpsimd(pool, lambda i, q: [(st.on["summed"], i * 2 + q + 1)])

        @block.tensor
        def _(pe):
            with pe.Fori(0, k.turns) as i:
                for q in range(2):
                    pe.wait_ge(st.gathered[0][q], (i + 1) * Q * 16)
                    pe.wait_ge(st.on["totals_used"], i * 2 + q)
                    st.totals(pe, i, q, lambda j: tot[:, j // 2, j % 2, 0:W], lambda j: XS[q][:, j, 0:W],
                              lambda n: carry[:, (n - 1) % K, :])
                for q in range(2):
                    pe.wait_ge(st.on["mean_ready"], i * 2 + q + 1)
                    transpose_quad(k, T[q], mean[q]).then_inc(st.on["t1"], 1)
                for q in range(2):
                    pe.wait_ge(st.on["c1"], i * 2 + q + 1)
                    project(k, O[q], aT[q], k.W0cat, k.bias0).then_inc(st.on["o1"], 1)

        @block.scalar
        def _(act):
            a = nc.scalar
            with act.Fori(0, k.turns) as i:
                for q in range(2):
                    for j in range(Q):
                        st.carry_on(act, i, q, j, carry[:, q * Q + j, :], tot[0:1, j // 2, j % 2, 0:W])
                for q in range(2):
                    act.wait_ge(st.on["t1"], i * 2 + q + 1)
                    a.activation(aT[q][:, :, 0:P], T[q][:, :, 0:P], ACT.Copy).then_inc(st.on["c1"], 1)
                for q in range(2):
                    act.wait_ge(st.on["o1"], i * 2 + q + 1)
                    for j in range(Q):
                        a.activation(junk[q][:, :], O[q][:, j // 2, j % 2, 0:D], ACT.Square,
                                     accum_out=ss[q][:, j:j + 1]).then_inc(st.on["square"], 1)
                        act.wait_ge(st.on["square"], i * K + q * Q + j + 1)
                    a.activation(std0[q][:, :], ss[q][:, :], ACT.Sqrt, bias=k.eps1[0:P, :],
                                 scale=1.0 / D).then_inc(st.on["std0"], 1)
                for q in range(2):
                    act.wait_ge(st.on["mv"], i * 2 + q + 1)
                    a.activation(st.std[q][:, :], st.mv[q][:, :, 1], ACT.Sqrt, bias=k.eps1[0:P, :]).then_inc(st.on["std"], 1)
                for q in range(2):
                    act.wait_ge(st.on["nm"], i * 2 + q + 1)
                    act.wait_ge(st.scattered[0][q], i * Q * 16)
                    normalise(k, x1[q], s[q], st.rs[q], st.nm[q]).then_inc(st.on["x1_ready"], 1)

        @block.vector
        def _(dve):
            v = nc.vector
            for q in range(2):
                v.memset(XS[q][:, :, D:D + 1], 1.0)
            v.memset(carry[:, :, :], 0.0).then_inc(st.on["carried"], 1)
            with dve.Fori(0, k.turns) as i:
                c = Chain(dve, st.v_steps, i, 16, held=st.v_held)
                for q in range(2):
                    st.masks(dve, i, q)
                for q in range(2):
                    dve.wait_ge(st.on["carried"], i * K + q * Q + Q + 1)
                    c.done(v.tensor_scalar(deg[q][:, :].rearrange("p (a b) -> p a b", a=2), tot[:, :, :, D], 1.0, 1.0,
                                           ALU.add, ALU.max))
                    dve.wait_ge(st.gathered[1][q], (i + 1) * Q * 16)
                    c.done(v.tensor_tensor(pairs(mean[q]), tot[:, :, :, 0:D], pairs(XD[q]), ALU.add))
                    dve.sem_inc(st.on["totals_used"], 1)
                    c.done(v.reciprocal(deg[q][:, :], deg[q][:, :]))
                    v.tensor_tensor(mean[q][:, :, :], mean[q][:, :, :],
                                    deg[q][:, :].unsqueeze(2).to_broadcast([P, Q, D]), ALU.mult).then_inc(st.on["mean_ready"], 1)
                for q in range(2):
                    dve.wait_ge(st.on["std0"], i * 2 + q + 1)
                    c.done(v.reciprocal(rs0[q][:, :], std0[q][:, :]))
                    for j in range(Q):
                        ins = v.scalar_tensor_tensor(s[q][:, j, :], O[q][:, j // 2, j % 2, D:], rs0[q][:, j:j + 1],
                                                     k.betaB[:, :], ALU.mult, ALU.add)
                    c.done(ins)
                    c.done(v.scalar_tensor_tensor(s[q][:, :, :], s[q][:, :, :], 0.0, XD[q][:, :, :], ALU.max, ALU.add))
                    dve.sem_inc(st.on["summed"], 1)
                    moments(k, c, st.stats[q], st.mv[q], s[q]).then_inc(st.on["mv"], 1)
                for q in range(2):
                    dve.wait_ge(st.on["std"], i * 2 + q + 1)
                    shifts(k, c, st.rs[q][:, :], st.nm[q][:, :], st.mv[q], st.std[q][:, :]).then_inc(st.on["nm"], 1)
                c.close()
    st.own.close()


def layer1(k, order):
    nc = k.nc
    st = Stage(k, "l1", order)
    XS, XD, s, relu = (st.quads(n, [P, Q, D]) for n in ("xs", "xd", "s", "relu"))
    x23 = st.quads("x23", [P, Q, 2 * D])
    x2, x3 = [b[:, :, 0:D] for b in x23], [b[:, :, D:] for b in x23]
    xsT, xdT = (st.quads(n, [D, Q, D]) for n in ("xsT", "xdT"))
    rels, relsT = st.quads("rels", [P, Q, RELS]), st.quads("relsT", [RELS, Q, P])
    iota8 = st.sb("iota8", [P, RELS])
    wide = st.sb("wide", [P, 2, RELS, D])
    bent = st.sb("bent", [P, 2, RELS * D])
    carry = st.sb("carry", [1, 2, RELS * D])
    TS, TD, Y = st.ps("TS", [D, Q, D]), st.ps("TD", [D, Q, D]), st.ps("Y", [P, Q, D])
    TR = st.ps("TR", [RELS, Q, D])
    tot = st.ps("tot", [P, 2, 2, 512])
    tot2 = tot[:, :, :, :].rearrange("p q b (j d) -> p q b j d", j=2)
    st.segments()
    st.sems("iota", "rels_ready", "t", "c", "y", "wide_ready", "bent_ready", "reduced", "summed", "mv", "std", "nm",
            "x2_ready", "t2", "c2", "o2", "relu_ready", "summed3", "mv3", "std3", "nm3", "x3_ready")
    st.gathers(slice(0, 2), (k.x1, XS, D), (k.x1, XD, D))
    st.scatters((k.x23, x23, 2 * D, st.on["x3_ready"], 0))

    with nc.Block() as block:
        @block.gpsimd
        def _(pool):
            nc.gpsimd.iota(iota8[:, :], [[1, RELS]], base=0, channel_multiplier=0,
                           allow_small_or_imprecise_dtypes=True).then_inc(st.on["iota"], 1)
            st.gpsimd(pool, lambda i, q: [(st.on["summed"], i * 2 + q + 1)])

        @block.tensor
        def _(pe):
            t = nc.tensor
            with pe.Fori(0, k.turns) as i:
                for q in range(2):
                    for n in range(2):
                        pe.wait_ge(st.gathered[n][q], (i + 1) * Q * 16)
                    pe.wait_ge(st.on["rels_ready"], i * 2 + q + 1)
                    pe.wait_ge(st.on["c"], i * 2 + q)
                    pe.wait_ge(st.on["c2"], i * 2)
                    transpose_quad(k, TS, XS[q])
                    transpose_quad(k, TD, XD[q])
                    for j in range(Q):
                        ins = t.transpose(TR[:, j, 0:P], rels[q][:, j, :], k.ident[0:P, 0:P])
                    ins.then_inc(st.on["t"], 1)
                for q in range(2):
                    pe.wait_ge(st.on["c"], i * 2 + q + 1)
                    pe.wait_ge(st.on["wide_ready"], i * K + q * Q)
                    for j in range(Q):
                        t.matmul(Y[:, j, :], xsT[q][:, j, 0:P], k.W1aT[:, :], start=True, stop=False)
                        t.matmul(Y[:, j, :], xdT[q][:, j, 0:P], k.W1bT[:, :], start=False, stop=False)
                        ins = t.matmul(Y[:, j, :], relsT[q][:, j, :], k.relC[:, :], start=False, stop=True)
                    ins.then_inc(st.on["y"], 1)
                    pe.wait_ge(st.on["masks"], i * 2 + q + 1)
                    for j in range(Q):
                        n = q * Q + j
                        pe.wait_ge(st.on["wide_ready"], i * K + n + 1)
                        pe.wait_ge(st.on["bent_ready"], i * K + max(n - 1, 0))
                        pe.wait_ge(st.on["summed3"], i * 2)
                        for b in range(2):
                            t.matmul(tot[:, n % 2, b, :], st.sel[q][:, j, :],
                                     wide[:, n % 2, 4 * b:4 * b + 4, :].rearrange("p r d -> p (r d)"), start=True, stop=False,
                                     skip_group_check=True)
                        pe.wait_ge(st.on["carried"], i * K + n + 1)
                        for b in range(2):
                            ins = t.matmul(tot[:, n % 2, b, :], st.cm[q][:, j, :],
                                           carry[:, (n - 1) % 2, 512 * b:512 * b + 512], start=False, stop=True,
                                           skip_group_check=True)
                        ins.then_inc(st.on["total"], 1)
                for q, T in ((0, TS), (1, TD)):
                    pe.wait_ge(st.on["x2_ready"], i * 2 + q + 1)
                    transpose_quad(k, T, x2[q]).then_inc(st.on["t2"], 1)
                for q in range(2):
                    pe.wait_ge(st.on["c2"], i * 2 + q + 1)
                    project(k, tot2[:, q, :, :, :], xsT[q], k.W2cat, k.bias2).then_inc(st.on["o2"], 1)

        @block.scalar
        def _(act):
            a = nc.scalar
            with act.Fori(0, k.turns) as i:
                for q in range(2):
                    act.wait_ge(st.on["t"], i * 2 + q + 1)
                    a.activation(xsT[q][:, :, 0:P], TS[:, :, 0:P], ACT.Copy)
                    a.activation(xdT[q][:, :, 0:P], TD[:, :, 0:P], ACT.Copy)
                    a.activation(relsT[q][:, :, :], TR[:, :, 0:P], ACT.Copy).then_inc(st.on["c"], 1)
                for n in range(K):
                    st.carry_on(act, i, n // Q, n % Q, carry[:, n % 2, :].rearrange("p (b d) -> p b d", b=2),
                                tot[0:1, n % 2, :, :])
                    act.wait_ge(st.on["reduced"], i * K + max(n - 1, 0))
                    a.activation(bent[:, n % 2, :].rearrange("p (b d) -> p b d", b=2), tot[:, n % 2, :, :],
                                 ACT.Tanh).then_inc(st.on["bent_ready"], 1)
                for q in range(2):
                    act.wait_ge(st.on["mv"], i * 2 + q + 1)
                    a.activation(st.std[q][:, :], st.mv[q][:, :, 1], ACT.Sqrt, bias=k.eps1[0:P, :]).then_inc(st.on["std"], 1)
                for q in range(2):
                    act.wait_ge(st.on["nm"], i * 2 + q + 1)
                    act.wait_ge(st.scattered[0][q], i * Q * 16)
                    normalise(k, x2[q], s[q], st.rs[q], st.nm[q]).then_inc(st.on["x2_ready"], 1)
                for q, T in ((0, TS), (1, TD)):
                    act.wait_ge(st.on["t2"], i * 2 + q + 1)
                    a.activation(xsT[q][:, :, 0:P], T[:, :, 0:P], ACT.Copy).then_inc(st.on["c2"], 1)
                for q in range(2):
                    act.wait_ge(st.on["o2"], i * 2 + q + 1)
                    a.activation(pairs(relu[q]), tot2[:, q, :, :, 0:D], ACT.Relu).then_inc(st.on["relu_ready"], 1)
                for q in range(2):
                    act.wait_ge(st.on["mv3"], i * 2 + q + 1)
                    a.activation(st.std[q][:, :], st.mv[q][:, :, 1], ACT.Sqrt, bias=k.eps1[0:P, :]).then_inc(st.on["std3"], 1)
                for q in range(2):
                    act.wait_ge(st.on["nm3"], i * 2 + q + 1)
                    normalise(k, x3[q], s[q], st.rs[q], st.nm[q]).then_inc(st.on["x3_ready"], 1)

        @block.vector
        def _(dve):
            v = nc.vector
            dve.wait_ge(st.on["iota"], 1)
            v.memset(carry[:, :, :], 0.0).then_inc(st.on["carried"], 1)
            with dve.Fori(0, k.turns) as i:
                c = Chain(dve, st.v_steps, i, 12, held=st.v_held)

                def reduce(n):
                    dve.wait_ge(st.on["bent_ready"], i * K + n + 1)
                    dve.wait_ge(st.on["x3_ready"], i * 2)
                    v.tensor_reduce(s[n // Q][:, n % Q, :], bent[:, n % 2, :].rearrange("p (r d) -> p d r", r=RELS),
                                    AX.X, ALU.add).then_inc(st.on["reduced"], 1)

                for q in range(2):
                    dve.wait_ge(st.on["c"], i * 2)
                    v.tensor_tensor(rels[q][:, :, :],
                                    order.cols[:, bass.ds(i * K + q * Q, Q), REL:REL + 1].to_broadcast([P, Q, RELS]),
                                    iota8[:, :].unsqueeze(1).to_broadcast([P, Q, RELS]),
                                    ALU.is_equal).then_inc(st.on["rels_ready"], 1)
                    st.masks(dve, i, q)
                for n in range(K):
                    q, j = n // Q, n % Q
                    if n >= 2:
                        reduce(n - 2)
                    if j == 0:
                        dve.wait_ge(st.on["y"], i * 2 + q + 1)
                        dve.wait_ge(st.on["rels_ready"], i * 2 + q + 1)
                    dve.wait_ge(st.on["total"], i * K + max(n - 1, 0))
                    v.tensor_tensor(wide[:, n % 2, :, :], Y[:, j, :].unsqueeze(1).to_broadcast([P, RELS, D]),
                                    rels[q][:, j, :].unsqueeze(2).to_broadcast([P, RELS, D]),
                                    ALU.mult).then_inc(st.on["wide_ready"], 1)
                for n in (K - 2, K - 1):
                    reduce(n)
                for q in range(2):
                    dve.wait_ge(st.on["reduced"], i * K + q * Q + Q)
                    c.done(v.tensor_tensor(s[q][:, :, :], s[q][:, :, :], XD[q][:, :, :], ALU.add))
                    dve.sem_inc(st.on["summed"], 1)
                    moments(k, c, st.stats[q], st.mv[q], s[q]).then_inc(st.on["mv"], 1)
                for q in range(2):
                    dve.wait_ge(st.on["std"], i * 2 + q + 1)
                    shifts(k, c, st.rs[q][:, :], st.nm[q][:, :], st.mv[q], st.std[q][:, :]).then_inc(st.on["nm"], 1)
                for q in range(2):
                    dve.wait_ge(st.on["relu_ready"], i * 2 + q + 1)
                    c.done(v.tensor_tensor(pairs(s[q]), tot2[:, q, :, :, D:], pairs(relu[q]), ALU.add))
                    dve.sem_inc(st.on["summed3"], 1)
                    moments(k, c, st.stats[q], st.mv[q], s[q]).then_inc(st.on["mv3"], 1)
                for q in range(2):
                    dve.wait_ge(st.on["std3"], i * 2 + q + 1)
                    shifts(k, c, st.rs[q][:, :], st.nm[q][:, :], st.mv[q], st.std[q][:, :]).then_inc(st.on["nm3"], 1)
                c.close()
    st.own.close()


def logits(k, order, rows_s, rows_d, scores):
    nc = k.nc
    st = Stage(k, "l2a", order)
    XS, XD = st.quads("xs", [P, Q, D]), st.quads("xd", [P, Q, D])
    prod = st.quads("prod", [P, 2, D])
    part = st.quads("part", [P, 2, Q])
    e = st.quads("e", [P, 2, Q])
    stored = [st.sem(f"stored{q}") for q in range(2)]
    st.sems("dotted")
    st.gathers(slice(2, 4), (k.x23h, XS, D), (k.x23h, XD, D))
    st.scatters()

    with nc.Block() as block:
        @block.gpsimd
        def _(pool):
            st.gpsimd(pool, lambda i, q: [(st.on["dotted"], i * 2 + q + 1), (stored[q], i * 64 + 64)])

        @block.sync
        def _(sp):
            with sp.Fori(0, k.turns) as i:
                for q in range(2):
                    for n, (to, of) in enumerate(((rows_s, XS), (rows_d, XD))):
                        sp.wait_ge(st.gathered[n][q], (i + 1) * Q * 16)
                        halves(sp, to[bass.ds(i * 2 + q, 1), :, :].rearrange("a p n -> (a p) n"),
                               of[q][:, :, :].rearrange("p q d -> p (q d)"), stored[q])
            for q in range(2):
                sp.wait_ge(stored[q], k.turns * 64)

        @block.vector
        def _(dve):
            v = nc.vector
            with dve.Fori(0, k.turns) as i:
                c = Chain(dve, st.v_steps, i, 2 * (2 * Q + 4), held=st.v_held)
                for q in range(2):
                    for n in range(2):
                        dve.wait_ge(st.gathered[n][q], (i + 1) * Q * 16)
                    for j in range(Q):
                        for n, (x, u) in enumerate(((XS, k.usB), (XD, k.udB))):
                            c.done(v.tensor_tensor_reduce(out=prod[q][:, n, :], in0=x[q][:, j, :], in1=u[:, :],
                                                          scale=1.0, scalar=0.0, op0=ALU.mult, op1=ALU.add,
                                                          accum_out=part[q][:, n, j:j + 1]))
                    dve.sem_inc(st.on["dotted"], 1)
                    c.done(v.tensor_tensor(e[q][:, 0, :], part[q][:, 0, :], part[q][:, 1, :], ALU.add))
                    c.done(v.tensor_tensor(e[q][:, 0, :], e[q][:, 0, :],
                                           order.cols[:, bass.ds(i * K + q * Q, Q), LOGIT], ALU.add))
                    c.done(v.tensor_scalar(e[q][:, 1, :], e[q][:, 0, :], k.logit0[:, :], None, ALU.add))
                    c.done(v.scalar_tensor_tensor(scores[:, bass.ds(i * K + q * Q, Q)], e[q][:, 1, :], SLOPE,
                                                  e[q][:, 1, :], ALU.mult, ALU.max))
                c.close()
    st.own.close()


def segment_softmax(k, table, key, scores, probs):
    nc = k.nc
    L = k.tiles
    LOW = -1e30
    s_d, p_d = k.dram("scores_edges", (1, k.E)), k.dram("probs_edges", (1, k.E))
    ends_d, carry_d = k.dram("row_ends", (P, 6)), k.dram("row_carries", (2, P))
    with ExitStack() as own:
        def sb(what, shape, dt=F32):
            return own.enter_context(nc.sbuf_tensor(f"smax_{what}", shape, dt))

        def sem(what):
            return k.semaphore((f"smax_{what}"))

        turned = sb("turned", [P, L, 1])
        keys3 = sb("keys3", [P, 3, L])
        e = sb("e", [P, L])
        pen = sb("pen", [P, 2, L])
        run = sb("run", [P, 2, L])
        own_end = sb("own_end", [P, 2, L])
        ends = sb("ends", [P, 6])
        rows = sb("rows", [1, 6, P])
        scan_in = sb("scan_in", [1, 2, 2, P])
        carries = sb("carries", [1, 2, P])
        carry = sb("carry", [P, 2])
        guard = sb("guard", [P, 1])
        both = sb("both", [P, 3, L])
        p = sb("p", [P, L])
        loaded, dma, steps, exped = sem("loaded"), sem("moved"), sem("steps"), sem("exped")
        asked = sem("asked")
        flat = s_d.rearrange("a (p l) -> (a p) l", p=P)

        with nc.Block() as block:
            @block.sync
            def _(sp):
                n = [0]

                def move(to, of, when):
                    sp.wait_ge(asked, when)
                    sp.dma_start(to, of, allow_slow_non_contiguous=True).then_inc(dma, 16)
                    n[0] += 16
                    sp.wait_ge(dma, n[0])

                for at in range(2):
                    sp.dma_start(keys3[:, at, :].unsqueeze(2),
                                 table[at:at + k.E, key:key + 1].rearrange("(p l) w -> p l w", p=P),
                                 allow_slow_non_contiguous=True).then_inc(loaded, 16)
                move(s_d.rearrange("a (t p) -> p t a", p=P), turned[:, :, :], 1)
                move(e[:, :], flat, 1)
                move(ends_d, ends[:, :], 2)
                move(rows[:, :, :], ends_d.rearrange("p (a c) -> a c p", a=1), 2)
                move(carry_d.rearrange("(a c) p -> a c p", a=1), carries[:, :, :], 3)
                move(carry[:, :], carry_d.rearrange("c p -> p c"), 3)
                sp.wait_ge(exped, 1)
                move(p_d.rearrange("a (p l) -> (a p) l", p=P), p[:, :], 3)
                move(turned[:, :, :], p_d.rearrange("a (t p) -> p t a", p=P), 3)

            @block.scalar
            def _(act):
                act.wait_ge(asked, 4)
                nc.scalar.activation(p[:, :], both[:, 2, :], ACT.Exp).then_inc(exped, 1)

            @block.vector
            def _(dve):
                v = nc.vector
                c = Chain(dve, steps)
                c.done(v.tensor_copy(turned[:, :, 0], scores[:, ::-1]))
                dve.sem_inc(asked, 1)
                dve.wait_ge(loaded, 32)
                v.memset(keys3[:, 2, L - 1:], -2.0)
                c.done(v.tensor_copy(keys3[:, 2, 0:L - 1], keys3[:, 1, 1:L]))
                for w, at in ((0, 0), (1, 2)):
                    c.done(v.tensor_tensor(pen[:, w, :], keys3[:, at, :], keys3[:, 1, :], ALU.is_equal))
                    edge = keys3[:, 1, 0:1] if w == 0 else keys3[:, 1, L - 1:L]
                    c.done(v.tensor_scalar(own_end[:, w, :], keys3[:, 1, :], edge, None, ALU.is_equal))
                c.done(v.tensor_copy(ends[:, 4:5], pen[:, 0, 0:1]))
                c.done(v.tensor_copy(ends[:, 2:3], own_end[:, 0, L - 1:L]))
                for x in (pen, own_end):
                    c.done(v.tensor_scalar(x[:, :, :], x[:, :, :], -1.0, -LOW, ALU.add, ALU.mult))
                dve.wait_ge(dma, 32)
                v.tensor_tensor_scan(run[:, 0, :], pen[:, 0, :], e[:, :], LOW, ALU.add, ALU.max)
                c.done(v.tensor_tensor_scan(run[:, 1, ::-1], pen[:, 1, ::-1], e[:, ::-1], LOW, ALU.add, ALU.max))
                v.tensor_copy(ends[:, 0:1], run[:, 0, L - 1:L])
                v.tensor_copy(ends[:, 1:2], run[:, 1, 0:1])
                v.memset(ends[:, 3:4], 0.0)
                c.done(v.memset(ends[:, 5:6], 0.0))
                dve.sem_inc(asked, 1)
                dve.wait_ge(dma, 64)
                c.done(v.memset(scan_in[:, :, :, :], LOW))
                c.done(v.tensor_scalar(rows[:, 2, :], rows[:, 2, :], -1.0, -LOW, ALU.add, ALU.mult))
                c.done(v.tensor_scalar(rows[:, 4, :], rows[:, 4, :], -1.0, -LOW, ALU.add, ALU.mult))
                for m, x in enumerate((rows[:, 2, :], rows[:, 0, :])):
                    c.done(v.tensor_tensor(scan_in[:, 0, m, 1:], x[:, 0:P - 1], rows[:, 4, 1:], ALU.add))
                for m, x in enumerate((rows[:, 2, :], rows[:, 1, :])):
                    c.done(v.tensor_tensor(scan_in[:, 1, m, 0:P - 1], x[:, 1:], rows[:, 4, 1:], ALU.add))
                v.tensor_tensor_scan(carries[:, 0, :], scan_in[:, 0, 0, :], scan_in[:, 0, 1, :], LOW, ALU.add, ALU.max)
                c.done(v.tensor_tensor_scan(carries[:, 1, ::-1], scan_in[:, 1, 0, ::-1], scan_in[:, 1, 1, ::-1], LOW,
                                            ALU.add, ALU.max))
                dve.sem_inc(asked, 1)
                dve.wait_ge(dma, 96)
                c.done(v.scalar_tensor_tensor(both[:, 0, :], own_end[:, 0, :], carry[:, 0:1], run[:, 0, :],
                                              ALU.add, ALU.max))
                c.done(v.scalar_tensor_tensor(both[:, 1, :], own_end[:, 1, :], carry[:, 1:2], run[:, 1, :],
                                              ALU.add, ALU.max))
                c.done(v.tensor_tensor(both[:, 0, :], both[:, 0, :], both[:, 1, :], ALU.max))
                c.done(v.tensor_tensor(both[:, 2, :], e[:, :], both[:, 0, :], ALU.subtract))
                dve.sem_inc(asked, 1)
                dve.wait_ge(dma, 128)
                v.tensor_copy(probs[:, :], turned[:, ::-1, 0])


def layer2(k, order, rows_s, rows_d, probs):
    nc = k.nc
    st = Stage(k, "l2b", order)
    W = D + 1
    XS, XD, z, relu, s, x3, s4, x4 = (st.quads(n, [P, Q, D]) for n in ("xs", "xd", "z", "relu", "s", "x3", "s4", "x4"))
    V = st.quads("v", [P, Q, D + 4])
    zT = st.quads("zT", [D, Q, D])
    den = st.quads("den", [P, Q])
    carry = st.sb("carry", [1, K, W])
    T = [st.ps(f"T{q}", [D, Q, D]) for q in range(2)]
    O = [st.ps(f"O{q}", [P, 2, 2, 2 * D]) for q in range(2)]
    tot = st.ps("tot", [P, 2, 2, 2 * D])
    loaded = [st.sem(f"loaded{q}") for q in range(2)]
    st.segments()
    st.sems("weighted", "z_ready", "t", "c", "o", "relu_ready", "summed", "mv", "std", "nm", "x3_ready", "s4_ready",
            "mv4", "std4", "nm4", "x4_ready")
    st.gathers(None)
    st.scatters((k.x23h, x3, D, st.on["x3_ready"], 1), (k.arg["out"], x4, D, st.on["x4_ready"], 0))

    with nc.Block() as block:
        @block.gpsimd
        def _(pool):
            st.gpsimd(pool, None)

        @block.sync
        def _(sp):
            with sp.Fori(0, k.turns) as i:
                for q in range(2):
                    sp.wait_ge(st.on["summed"], i * 2)
                    for to, of in ((XS, rows_s), (XD, rows_d)):
                        halves(sp, to[q][:, :, :].rearrange("p q d -> p (q d)"),
                               of[bass.ds(i * 2 + q, 1), :, :].rearrange("a p n -> (a p) n"), loaded[q])

        @block.tensor
        def _(pe):
            with pe.Fori(0, k.turns) as i:
                for q in range(2):
                    pe.wait_ge(st.on["weighted"], i * 2 + q + 1)
                    pe.wait_ge(st.on["totals_used"], i * 2 + q)
                    st.totals(pe, i, q, lambda j: tot[:, j // 2, j % 2, 0:W], lambda j: V[q][:, j, 0:W],
                              lambda n: carry[:, (n - 1) % K, :])
                for q in range(2):
                    pe.wait_ge(st.on["z_ready"], i * 2 + q + 1)
                    transpose_quad(k, T[q], z[q]).then_inc(st.on["t"], 1)
                for q in range(2):
                    pe.wait_ge(st.on["c"], i * 2 + q + 1)
                    project(k, O[q], zT[q], k.W2edge, k.bias2e).then_inc(st.on["o"], 1)

        @block.scalar
        def _(act):
            a = nc.scalar
            with act.Fori(0, k.turns) as i:
                for q in range(2):
                    act.wait_ge(loaded[q], 64 * i + 64)
                    act.wait_ge(st.on["total"], i * K)
                    for j in range(Q):
                        prob = probs[:, bass.ds(i * K + q * Q + j, 1)]
                        a.activation(V[q][:, j, 0:D], XD[q][:, j, :], ACT.Copy, scale=prob)
                        ins = a.activation(V[q][:, j, D:D + 1], prob, ACT.Copy)
                    ins.then_inc(st.on["weighted"], 1)
                for q in range(2):
                    for j in range(Q):
                        st.carry_on(act, i, q, j, carry[:, q * Q + j, :], tot[0:1, j // 2, j % 2, 0:W])
                for q in range(2):
                    act.wait_ge(st.on["t"], i * 2 + q + 1)
                    a.activation(zT[q][:, :, 0:P], T[q][:, :, 0:P], ACT.Copy).then_inc(st.on["c"], 1)
                for q in range(2):
                    act.wait_ge(st.on["o"], i * 2 + q + 1)
                    a.activation(pairs(relu[q]), O[q][:, :, :, 0:D], ACT.Relu).then_inc(st.on["relu_ready"], 1)
                for q in range(2):
                    act.wait_ge(st.on["mv"], i * 2 + q + 1)
                    a.activation(st.std[q][:, :], st.mv[q][:, :, 1], ACT.Sqrt, bias=k.eps1[0:P, :]).then_inc(st.on["std"], 1)
                for q in range(2):
                    act.wait_ge(st.on["nm"], i * 2 + q + 1)
                    act.wait_ge(st.scattered[0][q], i * Q * 16)
                    normalise(k, x3[q], s[q], st.rs[q], st.nm[q]).then_inc(st.on["x3_ready"], 1)
                for q in range(2):
                    act.wait_ge(st.on["mv4"], i * 2 + q + 1)
                    a.activation(st.std[q][:, :], st.mv[q][:, :, 1], ACT.Sqrt, bias=k.eps1[0:P, :]).then_inc(st.on["std4"], 1)
                for q in range(2):
                    act.wait_ge(st.on["nm4"], i * 2 + q + 1)
                    act.wait_ge(st.scattered[1][q], i * Q * 16)
                    normalise(k, x4[q], s4[q], st.rs[q], st.nm[q]).then_inc(st.on["x4_ready"], 1)

        @block.vector
        def _(dve):
            v = nc.vector
            v.memset(carry[:, :, :], 0.0).then_inc(st.on["carried"], 1)
            with dve.Fori(0, k.turns) as i:
                c = Chain(dve, st.v_steps, i, 20, held=st.v_held)
                for q in range(2):
                    st.masks(dve, i, q)
                for q in range(2):
                    dve.wait_ge(st.on["carried"], i * K + q * Q + Q + 1)
                    c.done(v.tensor_scalar(den[q][:, :].rearrange("p (a b) -> p a b", a=2), tot[:, :, :, D], 1e-30, None,
                                           ALU.max))
                    c.done(v.reciprocal(den[q][:, :], den[q][:, :]))
                    for b in range(2):
                        ins = v.tensor_tensor(z[q][:, 2 * b:2 * b + 2, :], tot[:, b, :, 0:D],
                                              den[q][:, 2 * b:2 * b + 2].unsqueeze(2).to_broadcast([P, 2, D]), ALU.mult)
                    c.done(ins)
                    dve.sem_inc(st.on["totals_used"], 1)
                    v.tensor_tensor(z[q][:, :, :], z[q][:, :, :], XS[q][:, :, :], ALU.add).then_inc(st.on["z_ready"], 1)
                for q in range(2):
                    dve.wait_ge(st.on["relu_ready"], i * 2 + q + 1)
                    c.done(v.tensor_tensor(pairs(s[q]), O[q][:, :, :, D:], pairs(relu[q]), ALU.add))
                    c.done(v.tensor_tensor(s[q][:, :, :], s[q][:, :, :], XS[q][:, :, :], ALU.add))
                    dve.sem_inc(st.on["summed"], 1)
                    moments(k, c, st.stats[q], st.mv[q], s[q]).then_inc(st.on["mv"], 1)
                for q in range(2):
                    dve.wait_ge(st.on["std"], i * 2 + q + 1)
                    shifts(k, c, st.rs[q][:, :], st.nm[q][:, :], st.mv[q], st.std[q][:, :]).then_inc(st.on["nm"], 1)
                for q in range(2):
                    dve.wait_ge(st.on["x3_ready"], i * 2 + q + 1)
                    c.done(v.tensor_tensor(s4[q][:, :, :], x3[q][:, :, :],
                                           k.sig2B[:, :].unsqueeze(1).to_broadcast([P, Q, D]), ALU.add))
                    moments(k, c, st.stats[q], st.mv[q], s4[q]).then_inc(st.on["mv4"], 1)
                for q in range(2):
                    dve.wait_ge(st.on["std4"], i * 2 + q + 1)
                    shifts(k, c, st.rs[q][:, :], st.nm[q][:, :], st.mv[q], st.std[q][:, :]).then_inc(st.on["nm4"], 1)
                c.close()
    st.own.close()


def layer3(k, order, last):
    nc = k.nc
    st = Stage(k, f"l3{'b' if last else 'a'}", order)
    W, to_width = (HID, D) if last else (D, HID)
    XS, V, A = (st.quads(n, [P, Q, W]) for n in ("xs", "v", "a"))
    XD, s = (st.quads(n, [P, Q, D]) for n in ("xd", "s"))
    y = st.quads("y", [P, Q, to_width])
    x4 = st.quads("x4", [P, Q, D])
    AT = st.quads("aT", [W, Q, D])
    carry = st.sb("carry", [1, K, W])
    T = [st.ps(f"T{q}", [W, Q, D]) for q in range(2)]
    O = [st.ps(f"O{q}", [P, Q, to_width if last else D]) for q in range(2)]
    tot = st.ps("tot", [P, Q, D])
    weights, bias = (k.w2, k.b2r) if last else (k.w1, k.b1r)
    st.segments()
    st.sems("weighted", "a_ready", "a_taken", "t", "c", "o", "y_ready", "summed", "mv", "std", "nm", "x4_ready")
    if last:
        st.gathers(slice(0, 6, 5), (k.h1, XS, HID), (k.x23h, XD, D))
        st.scatters((k.arg["out"], x4, D, st.on["x4_ready"], 0))
    else:
        st.gathers(slice(4, 5), (k.x23h, XS, D))
        st.scatters((k.h1, y, HID, st.on["y_ready"], 0))

    with nc.Block() as block:
        @block.gpsimd
        def _(pool):
            st.gpsimd(pool, lambda i, q: [(st.on["summed"] if last else st.on["weighted"], i * 2 + q + 1)])

        @block.tensor
        def _(pe):
            t = nc.tensor
            with pe.Fori(0, k.turns) as i:
                for q in range(2):
                    pe.wait_ge(st.on["weighted"], i * 2 + q + 1)
                    pe.wait_ge(st.on["totals_used"], i * 2 + q)
                    st.totals(pe, i, q, lambda j: tot[:, j, 0:W], lambda j: V[q][:, j, :],
                              lambda n: carry[:, (n - 1) % K, :])
                for q in range(2):
                    pe.wait_ge(st.on["a_ready"], i * 2 + q + 1)
                    pe.sem_inc(st.on["a_taken"], 1)
                    transpose_quad(k, T[q], A[q]).then_inc(st.on["t"], 1)
                for q in range(2):
                    pe.wait_ge(st.on["c"], i * 2 + q + 1)
                    flat = O[q][:, :, 0:to_width]
                    t.matmul(flat, k.ones_row[:, 0:P], bias[:, :].rearrange("a (q d) -> a q d", q=Q), start=True,
                             stop=False, skip_group_check=True)
                    for j in range(Q):
                        ins = t.matmul(O[q][:, j, 0:to_width], AT[q][:, j, 0:P], weights[:, :], start=False,
                                       stop=True, skip_group_check=True)
                    ins.then_inc(st.on["o"], 1)

        @block.scalar
        def _(act):
            a = nc.scalar
            with act.Fori(0, k.turns) as i:
                for q in range(2):
                    act.wait_ge(st.gathered[0][q], (i + 1) * Q * 16)
                    act.wait_ge(st.on["total"], i * K)
                    for j in range(Q):
                        ins = a.activation(V[q][:, j, :], XS[q][:, j, :], ACT.Copy,
                                           scale=order.cols[:, bass.ds(i * K + q * Q + j, 1), WEIGHT])
                    ins.then_inc(st.on["weighted"], 1)
                for q in range(2):
                    for j in range(Q):
                        st.carry_on(act, i, q, j, carry[:, q * Q + j, :], tot[0:1, j, 0:W])
                for q in range(2):
                    act.wait_ge(st.on["t"], i * 2 + q + 1)
                    a.activation(AT[q][:, :, 0:P], T[q][:, :, 0:P], ACT.Copy).then_inc(st.on["c"], 1)
                for q in range(2):
                    act.wait_ge(st.on["o"], i * 2 + q + 1)
                    if not last:
                        act.wait_ge(st.scattered[0][q], i * Q * 16)
                    a.activation(y[q][:, :, :], O[q][:, :, 0:to_width], ACT.Sigmoid).then_inc(st.on["y_ready"], 1)
                if last:
                    for q in range(2):
                        act.wait_ge(st.on["mv"], i * 2 + q + 1)
                        a.activation(st.std[q][:, :], st.mv[q][:, :, 1], ACT.Sqrt,
                                     bias=k.eps1[0:P, :]).then_inc(st.on["std"], 1)
                    for q in range(2):
                        act.wait_ge(st.on["nm"], i * 2 + q + 1)
                        act.wait_ge(st.scattered[0][q], i * Q * 16)
                        normalise(k, x4[q], s[q], st.rs[q], st.nm[q]).then_inc(st.on["x4_ready"], 1)

        @block.vector
        def _(dve):
            v = nc.vector
            v.memset(carry[:, :, :], 0.0).then_inc(st.on["carried"], 1)
            with dve.Fori(0, k.turns) as i:
                c = Chain(dve, st.v_steps, i, 6 if last else 0, held=st.v_held)
                for q in range(2):
                    st.masks(dve, i, q)
                for q in range(2):
                    dve.wait_ge(st.on["carried"], i * K + q * Q + Q + 1)
                    v.tensor_copy(A[q][:, :, :], tot[:, :, 0:W]).then_inc(st.on["a_ready"], 1)
                    dve.wait_ge(st.on["a_ready"], i * 2 + q + 1)
                    dve.sem_inc(st.on["totals_used"], 1)
                if last:
                    for q in range(2):
                        dve.wait_ge(st.on["y_ready"], i * 2 + q + 1)
                        dve.wait_ge(st.gathered[1][q], (i + 1) * Q * 16)
                        c.done(v.tensor_tensor(s[q][:, :, :], XD[q][:, :, :], y[q][:, :, :], ALU.add))
                        dve.sem_inc(st.on["summed"], 1)
                        moments(k, c, st.stats[q], st.mv[q], s[q]).then_inc(st.on["mv"], 1)
                    for q in range(2):
                        dve.wait_ge(st.on["std"], i * 2 + q + 1)
                        shifts(k, c, st.rs[q][:, :], st.nm[q][:, :], st.mv[q], st.std[q][:, :]).then_inc(st.on["nm"], 1)
                c.close()
    st.own.close()


def program(nc, args, n_nodes, n_edges, upto=99, probe=None):
    with ExitStack() as ctx:
        k = Kernel(nc, ctx, args, n_nodes, n_edges)
        k.by_src1 = k.dram("by_src_low", (k.E + 1, COLS))
        k.by_dst1 = k.dram("by_dst_low", (k.E + 1, COLS))
        k.by_src = k.dram("by_src", (k.E + 1, COLS)) if probe is None else probe["by_src"]
        k.by_dst = k.dram("by_dst", (k.E + 1, COLS)) if probe is None else probe["by_dst"]
        prepare(k)
        k.recycle()
        edge_table(k)
        k.recycle()
        radix_pass(k, "src_low", 0, None, 0, k.by_src1)
        k.recycle()
        radix_pass(k, "src_high", 1, k.by_src1, SRC, k.by_src)
        k.recycle()
        radix_pass(k, "dst_low", 2, None, 1, k.by_dst1)
        k.recycle()
        radix_pass(k, "dst_high", 3, k.by_dst1, DST, k.by_dst)
        k.recycle()
        k.sorting.close()

        k.x1, k.x23 = k.dram("x1_nodes", (k.N, D)), k.dram("x2_x3_nodes", (k.N, 2 * D))
        k.h1 = k.dram("h1_nodes", (k.N, HID))
        if probe:
            k.x1, k.x23, k.h1 = probe["x1"], probe["x23"], probe["h1"]
        k.x23h = k.x23.rearrange("n (h d) -> (n h) d", h=2)
        dense_alone(k)
        k.recycle()

        k.scores = k.sb("scores", [P, k.tiles])
        k.probs = k.sb("probs", [P, k.tiles])
        dst = Order(k, "dst", k.by_dst, DST)
        k.recycle()
        layer0(k, dst)
        k.recycle()
        layer1(k, dst)
        k.recycle()
        dst.own.close()
        rows_s = k.dram("x2_of_src", (2 * k.turns, P, Q * D))
        rows_d = k.dram("x2_of_dst", (2 * k.turns, P, Q * D))
        src = Order(k, "src", k.by_src, SRC)
        k.recycle()
        logits(k, src, rows_s, rows_d, k.scores)
        k.recycle()
        segment_softmax(k, k.by_src, SRC, k.scores, k.probs)
        k.recycle()
        layer2(k, src, rows_s, rows_d, k.probs)
        k.recycle()
        src.own.close()
        again = Order(k, "dst_again", k.by_dst, DST)
        k.recycle()
        layer3(k, again, False)
        k.recycle()
        layer3(k, again, True)
        k.recycle()
        again.own.close()


_INS = ["x", "src", "dst", "edge_attr_128", "edge_type_8", "edge_weight",
        "L0_gnn_W", "L0_gnn_b", "L0_gnn_gamma", "L0_gnn_beta",
        "L1_gnn_rel_emb", "L1_gnn_W", "L1_gnn_b",
        "L2_gnn_W_node", "L2_gnn_b_node", "L2_gnn_W_edge", "L2_gnn_b_edge",
        "L3_gnn_w1", "L3_gnn_b1", "L3_gnn_w2", "L3_gnn_b2"]


def kernel(**inputs):
    import numpy as _np
    import concourse.bacc as _bacc
    from concourse import mybir as _mybir
    from concourse.bass_utils import run_bass_kernel_spmd as _run

    nc = _bacc.Bacc("TRN2", target_bir_lowering=False, num_devices=1)
    arrays, args = {}, {}
    for name in _INS:
        a = _np.ascontiguousarray(inputs[name])
        arrays[f"in_{name}"] = a
        args[name] = nc.dram_tensor(f"in_{name}", a.shape, _mybir.dt.from_np(a.dtype), kind="ExternalInput").ap()
    n_nodes, features = inputs["x"].shape
    args["out"] = nc.dram_tensor("out", (n_nodes, features), _mybir.dt.float32, kind="ExternalOutput").ap()
    program(nc, args, n_nodes, inputs["src"].shape[0])
    r = _run(nc, [arrays], core_ids=[0])
    return r.results[0]["out"]
```

```python
import concourse.bass as bass
from concourse import mybir
from contextlib import ExitStack

F32 = mybir.dt.float32
BF16 = mybir.dt.bfloat16
FP16 = mybir.dt.float16
I32 = mybir.dt.int32
ALU = mybir.AluOpType
ACT = mybir.ActivationFunctionType
AX = mybir.AxisListType

P = 125
R = P + 1
K = 8
Q = 4
D = 128
HID = 64
RELS = 8
LOW_BITS = 9
BINS = 1 << LOW_BITS
EPS = 1e-5
SLOPE = 0.2
FAR = 1 << 20
COLS = 8
SRC, DST, REL, WEIGHT, LOGIT = range(5)


class Chain:

    def __init__(self, engine, sem, turn=0, steps=0, before=0, held=None):
        self.engine, self.sem, self.base, self.steps, self.n = engine, sem, turn * steps + before, steps, 0
        self.held = held

    def done(self, instruction):
        instruction.then_inc(self.sem, 1)
        self.n += 1
        self.engine.wait_ge(self.sem, self.base + self.n)

    def hold(self):
        self.engine.sem_inc(self.held, 1)

    def close(self):
        assert self.n == self.steps, (self.n, self.steps)


class Queue:

    def __init__(self, sem):
        self.sem, self.before, self.added = sem, 0, 0


class Kernel:

    def __init__(self, nc, ctx, args, n_nodes, n_edges):
        self.nc, self.ctx = nc, ctx
        self.N, self.E = n_nodes, n_edges
        self.sorting = ExitStack()
        self.in_use, self.free, self.queues = [], {"dma": [], "steps": []}, {}
        self.tiles = n_edges // P
        self.turns = self.tiles // K
        assert n_edges % (P * K) == 0 and n_nodes % (P * K) == 0
        self.groups = n_nodes // (P * K)
        self.arg = args

    def sb(self, name, shape, dt=F32):
        return self.ctx.enter_context(self.nc.sbuf_tensor(name, shape, dt))

    def sort_sb(self, name, shape, dt=F32):
        return self.sorting.enter_context(self.nc.sbuf_tensor(name, shape, dt))

    def semaphore(self, name):
        if any(x in name for x in ("loaded", "stored", "moved")):
            kind = "dma"
        else:
            kind = "steps"
        free = self.free[kind]
        s = free.pop(0) if free else self.nc.alloc_semaphore(name)
        self.in_use.append((kind, s))
        return s

    def queue(self, name, added):
        if name not in self.queues:
            self.queues[name] = Queue(self.nc.alloc_semaphore(name))
        q = self.queues[name]
        q.before, q.added = q.before + q.added, added
        return q

    def recycle(self):
        with self.nc.Block() as block:
            @block.gpsimd
            def _(pool):
                for _, s in self.in_use:
                    pool.sem_clear(s)
        for kind, s in self.in_use:
            self.free[kind].append(s)
        self.in_use = []

    def dram(self, name, shape, dt=F32):
        return self.nc.dram_tensor(name, shape, dt, kind="Internal").ap()


def row(ap):
    return ap.rearrange("(a n) -> a n", a=1)


def column(ap):
    return ap.rearrange("(n a) -> n a", a=1)


def over(ap, partitions):
    return row(ap).to_broadcast([partitions, ap.shape[0]])


def prepare(k):
    nc = k.nc
    k.ident = k.sb("ident", [D, D])
    k.ones_row = k.sb("ones_row", [1, 512])
    k.ones3 = k.sb("ones3", [3, R], BF16)
    k.eps1 = k.sb("eps1", [D, 1])
    k.eps2 = k.sb("eps2", [D, 1])
    k.W0cat = k.sb("W0cat", [D, 2 * D])
    k.bias0 = k.sb("bias0", [3, 2, 2 * D], BF16)
    k.betaB = k.sb("betaB", [R, D])
    k.sig2B = k.sb("sig2B", [R, D])
    k.sig1B = k.sb("sig1B", [P, K * HID])
    k.W2cat = k.sb("W2cat", [D, 2 * D])
    k.W2edge = k.sb("W2edge", [D, 2 * D])
    k.bias2 = k.sb("bias2", [3, 2, 2 * D], BF16)
    k.bias2e = k.sb("bias2e", [3, 2, 2 * D], BF16)
    k.WeB = k.sb("WeB", [P, D])
    k.usB = k.sb("usB", [R, D])
    k.udB = k.sb("udB", [R, D])
    k.logit0 = k.sb("logit0", [R, 1])
    k.W1aT = k.sb("W1aT", [D, D])
    k.W1bT = k.sb("W1bT", [D, D])
    k.relC = k.sb("relC", [RELS, D])
    k.w1 = k.sb("w1", [D, HID])
    k.w2 = k.sb("w2", [HID, D])
    k.b1r = k.sb("b1r", [1, Q * HID])
    k.b2r = k.sb("b2r", [1, Q * D])
    with ExitStack() as own:
        def sb(name, shape, dt=F32):
            return own.enter_context(nc.sbuf_tensor(name, shape, dt))

        def sem(name):
            return k.semaphore((name))

        W0 = sb("W0", [D, D])
        W1 = sb("W1", [D, 2 * D + HID])
        Wn = sb("Wn", [D, D])
        WnT = sb("WnT", [D, D])
        W1cT = sb("W1cT", [HID, D])
        emb = sb("emb", [RELS, HID])
        embT = sb("embT", [HID, RELS])
        gammaB = sb("gammaB", [D, D])
        b0 = sb("b0", [1, D])
        bn = sb("bn", [1, D])
        bncol = sb("bncol", [D, 1])
        b1e = sb("b1e", [1, D])
        wsd = sb("wsd", [D, 3])
        wsB = sb("wsB", [D, 3, R])
        bedge = sb("bedge", [R, 1])
        b2B = sb("b2B", [R, D])
        b1B = sb("b1B", [P, HID])
        W0T = sb("W0T", [D, D])
        mean = sb("mean", [D, 2])
        biasrow = sb("biasrow", [1, 3, 2, 2 * D])
        rest = sb("rest", [1, 2 * D])
        parts = sb("parts", [1, 3, 3, 2, 2 * D], BF16)
        b12 = sb("b12", [1, HID + D])
        ps = own.enter_context(nc.psum_tensor("ps", [D, 8, 512], F32))

        loaded = sem("weights_loaded")
        moved = sem("bias_rows_moved")
        ident_set = sem("ident_set")
        steps = sem("prepare_steps")
        cols_spread = sem("cols_spread")
        transposed = sem("weights_transposed")
        copied = sem("weights_copied")
        multiplied = sem("weights_multiplied")
        sigmoids = sem("sigmoids")
        LOADS = 20

        with nc.Block() as block:
            @block.sync
            def _(sp):
                n = 0
                for to, of in [
                    (W0[:, :], k.arg["L0_gnn_W"]), (W1[:, :], k.arg["L1_gnn_W"]), (Wn[:, :], k.arg["L2_gnn_W_node"]),
                    (emb[:, :], k.arg["L1_gnn_rel_emb"]), (gammaB[:, :], over(k.arg["L0_gnn_gamma"], D)),
                    (k.betaB[:, :], over(k.arg["L0_gnn_beta"], R)), (b0[:, :], row(k.arg["L0_gnn_b"])),
                    (bn[:, :], row(k.arg["L2_gnn_b_node"])), (bncol[:, :], column(k.arg["L2_gnn_b_node"])),
                    (b1e[:, :], row(k.arg["L1_gnn_b"])),
                    (k.WeB[:, :], over(k.arg["L2_gnn_W_edge"].rearrange("n a -> (n a)")[0:D], P)),
                    (wsd[:, 0:1], k.arg["L2_gnn_W_edge"][D:2 * D, :]), (wsd[:, 1:2], k.arg["L2_gnn_W_edge"][2 * D:3 * D, :]),
                    (bedge[:, :], over(k.arg["L2_gnn_b_edge"], R)), (b2B[:, :], over(k.arg["L3_gnn_b2"], R)),
                    (b1B[:, :], over(k.arg["L3_gnn_b1"], P)), (k.w1[:, :], k.arg["L3_gnn_w1"]), (k.w2[:, :], k.arg["L3_gnn_w2"]),
                    (b12[:, 0:HID], row(k.arg["L3_gnn_b1"])), (b12[:, HID:], row(k.arg["L3_gnn_b2"])),
                ]:
                    sp.dma_start(to, of).then_inc(loaded, 16)
                    n += 1
                assert n == LOADS
                sp.wait_ge(copied, 4)
                for m, to in enumerate((k.bias0, k.bias2, k.bias2e)):
                    sp.dma_start(to[:, :, :], parts[:, m, :, :, :]).then_inc(moved, 16)
                sp.wait_ge(moved, 48)

            @block.gpsimd
            def _(pool):
                nc.gpsimd.memset(k.ident[:, :], 0.0).then_inc(ident_set, 1)
                pool.wait_ge(ident_set, 1)
                nc.gpsimd.affine_select(out=k.ident[:, :], in_=k.ident[:, :], compare_op=ALU.not_equal, fill=1.0,
                                        base=0, pattern=[[-1, D]], channel_multiplier=1).then_inc(ident_set, 1)

            @block.scalar
            def _(act):
                act.wait_ge(loaded, 16 * LOADS)
                nc.scalar.activation(k.sig2B[:, :], b2B[:, :], ACT.Sigmoid)
                for j in range(K):
                    nc.scalar.activation(k.sig1B[:, j * HID:(j + 1) * HID], b1B[:, :], ACT.Sigmoid).then_inc(sigmoids, 1)

            @block.tensor
            def _(pe):
                pe.wait_ge(loaded, 16 * LOADS)
                pe.wait_ge(ident_set, 2)
                nc.tensor.transpose(ps[:, 0, 0:D], W0[:, :], k.ident[:, :])
                nc.tensor.transpose(ps[:, 1, 0:D], W1[:, 0:D], k.ident[:, :])
                nc.tensor.transpose(ps[:, 2, 0:D], W1[:, D:2 * D], k.ident[:, :])
                nc.tensor.transpose(ps[0:HID, 3, 0:D], W1[:, 2 * D:], k.ident[:, :])
                nc.tensor.transpose(ps[0:HID, 4, 0:RELS], emb[:, :], k.ident[0:RELS, 0:RELS])
                nc.tensor.transpose(ps[:, 5, 0:D], Wn[:, :], k.ident[:, :]).then_inc(transposed, 1)
                pe.wait_ge(copied, 1)
                nc.tensor.matmul(ps[0:RELS, 0, 0:D], embT[:, :], W1cT[:, :], start=True, stop=False)
                nc.tensor.matmul(ps[0:RELS, 0, 0:D], k.ones_row[:, 0:RELS], b1e[:, :], start=False, stop=True)
                pe.wait_ge(cols_spread, 1)
                nc.tensor.matmul(ps[0:R, 1, 0:D], wsB[:, 0, :], WnT[:, :], start=True, stop=True)
                nc.tensor.matmul(ps[0:R, 2, 0:D], wsB[:, 1, :], WnT[:, :], start=True, stop=True)
                nc.tensor.matmul(ps[0:R, 3, 0:1], wsB[:, 2, :], bncol[:, :], start=True, stop=True).then_inc(multiplied, 1)

            @block.vector
            def _(dve):
                v = nc.vector
                c = Chain(dve, steps)
                dve.wait_ge(loaded, 16 * LOADS)
                v.memset(k.ones_row[:, :], 1.0)
                v.memset(k.ones3[:, :], 1.0)
                v.memset(k.eps1[:, :], EPS)
                v.memset(k.eps2[:, :], EPS * EPS)
                c.done(v.tensor_tensor(wsd[:, 2:3], wsd[:, 0:1], wsd[:, 1:2], ALU.add))
                v.tensor_scalar(wsB[:, :, :], wsd[:, :].unsqueeze(2).to_broadcast([D, 3, R]), 1.0, None,
                                ALU.mult).then_inc(cols_spread, 1)
                dve.wait_ge(transposed, 1)
                v.tensor_copy(k.W1aT[:, :], ps[:, 1, 0:D])
                v.tensor_copy(k.W1bT[:, :], ps[:, 2, 0:D])
                v.tensor_copy(W1cT[:, :], ps[0:HID, 3, 0:D])
                v.tensor_copy(embT[:, :], ps[0:HID, 4, 0:RELS])
                v.tensor_copy(WnT[:, :], ps[:, 5, 0:D])
                c.done(v.tensor_copy(W0T[:, :], ps[:, 0, 0:D]))
                v.tensor_reduce(mean[:, 0:1], W0T[:, :], AX.X, ALU.add)
                c.done(v.tensor_reduce(mean[0:1, 1:2], b0[:, :], AX.X, ALU.add))
                c.done(v.tensor_scalar(mean[:, 0:1], mean[:, 0:1], 1.0 / D, None, ALU.mult))
                c.done(v.tensor_scalar(mean[0:1, 1:2], mean[0:1, 1:2], 1.0 / D, None, ALU.mult))
                v.tensor_scalar(k.W0cat[:, 0:D], W0T[:, :], mean[:, 0:1], None, ALU.subtract).then_inc(copied, 1)
                dve.wait_ge(copied, 1)
                v.tensor_tensor(k.W0cat[:, D:], k.W0cat[:, 0:D], gammaB[:, :], ALU.mult)
                c.done(v.tensor_scalar(biasrow[:, 0, 0, 0:D], b0[:, :], mean[0:1, 1:2], None, ALU.subtract))
                v.tensor_tensor(biasrow[:, 0, 0, D:], biasrow[:, 0, 0, 0:D], gammaB[0:1, :], ALU.mult)
                v.tensor_scalar(biasrow[:, 1, 0, 0:D], bn[:, :], 1 - SLOPE, None, ALU.mult)
                v.tensor_scalar(biasrow[:, 1, 0, D:], bn[:, :], SLOPE, None, ALU.mult)
                v.tensor_scalar(biasrow[:, 2, 0, 0:D], bn[:, :], 2 * (1 - SLOPE), None, ALU.mult)
                v.tensor_scalar(biasrow[:, 2, 0, D:], bn[:, :], 2 * SLOPE, None, ALU.mult)
                v.tensor_scalar(k.W2cat[:, 0:D], Wn[:, :], 1 - SLOPE, None, ALU.mult)
                v.tensor_scalar(k.W2edge[:, 0:D], Wn[:, :], 1 - SLOPE, None, ALU.mult)
                c.done(v.tensor_scalar(k.W2edge[:, D:], Wn[:, :], SLOPE, None, ALU.mult))
                dve.wait_ge(ident_set, 2)
                c.done(v.tensor_tensor(k.W2cat[:, D:], k.W2edge[:, D:], k.ident[:, :], ALU.add))
                for m in range(3):
                    b = biasrow[:, m, 0, :]
                    c.done(v.tensor_copy(rest[:, :], b))
                    for part in range(3):
                        c.done(v.tensor_copy(parts[:, m, part, 0, :], rest[:, :]))
                        c.done(v.tensor_tensor(rest[:, :], rest[:, :], parts[:, m, part, 0, :], ALU.subtract))
                        c.done(v.tensor_copy(parts[:, m, part, 1, :], parts[:, m, part, 0, :]))
                    dve.sem_inc(copied, 1)
                for j in range(Q):
                    v.tensor_copy(k.b1r[:, j * HID:(j + 1) * HID], b12[:, 0:HID])
                    v.tensor_copy(k.b2r[:, j * D:(j + 1) * D], b12[:, HID:])
                dve.wait_ge(multiplied, 1)
                v.tensor_copy(k.relC[:, :], ps[0:RELS, 0, 0:D])
                v.tensor_copy(k.usB[:, :], ps[0:R, 1, 0:D])
                v.tensor_copy(k.udB[:, :], ps[0:R, 2, 0:D])
                v.tensor_tensor(k.logit0[:, :], ps[0:R, 3, 0:1], bedge[:, :], ALU.add)


def edge_table(k):
    nc = k.nc
    k.edges = k.sort_sb("edges", [P, k.tiles, COLS])
    k.digits = k.sort_sb("digits", [P, 2, k.tiles])
    k.bins = k.sort_sb("bins", [P, BINS], FP16)
    k.below = k.sort_sb("below", [P, 3, P], BF16)
    k.base = k.sort_sb("base", [1, 4, BINS])
    with ExitStack() as own:
        def sb(name, shape, dt=F32):
            return own.enter_context(nc.sbuf_tensor(name, shape, dt))

        def sem(name):
            return k.semaphore((name))

        raw = sb("raw", [P, 3, k.tiles], I32)
        split = sb("split", [P, 2, 2, k.tiles], I32)
        dig = sb("dig", [P, 4, k.tiles])
        weight = sb("weight", [P, k.tiles])
        attr = sb("attr", [P, K, D])
        prod = sb("prod", [P, 2, D])
        dot = sb("dot", [P, K])
        onehot = sb("onehot", [P, 8, BINS], BF16)
        ones_col = sb("ones_col", [P, 1], BF16)
        ones_bins = sb("ones_bins", [1, BINS])
        seen = sb("seen", [1, 4, BINS])
        guard = sb("guard", [1, COLS])
        count = own.enter_context(nc.psum_tensor("count", [1, 4, 512], F32))
        loaded = sem("edges_loaded")
        attr_loaded = sem("attr_loaded")
        attr_used = sem("attr_used")
        consts_set = sem("sort_consts_set")
        steps = sem("table_steps")
        loop_steps = sem("table_loop_steps")
        onehots = sem("onehots_ready")
        counted = sem("onehots_counted")
        guards = sem("guards_stored")
        attr_rows = k.arg["edge_attr_128"].rearrange("(p t) d -> p t d", p=P)

        with nc.Block() as block:
            @block.sync
            def _(sp):
                for n, a in enumerate((k.arg["src"], k.arg["dst"], k.arg["edge_type_8"])):
                    sp.dma_start(raw[:, n, :], a.rearrange("(p t) -> p t", p=P)).then_inc(loaded, 16)
                sp.dma_start(weight[:, :], k.arg["edge_weight"].rearrange("(p t) -> p t", p=P)).then_inc(loaded, 16)
                sp.wait_ge(consts_set, 5)
                for table in (k.by_src, k.by_dst):
                    sp.dma_start(table[0:1, :], guard[:, :]).then_inc(guards, 16)
                with sp.Fori(0, k.turns) as i:
                    sp.wait_ge(attr_used, i * K)
                    sp.dma_start(attr[:, :, :], attr_rows[:, bass.ds(i * K, K), :]).then_inc(attr_loaded, 16)
                sp.wait_ge(guards, 32)

            @block.gpsimd
            def _(pool):
                g = nc.gpsimd
                g.iota(k.bins[:, :], [[1, BINS]], base=0, channel_multiplier=0,
                       allow_small_or_imprecise_dtypes=True).then_inc(consts_set, 1)
                g.memset(k.below[:, :, :], 1.0).then_inc(consts_set, 1)
                pool.wait_ge(consts_set, 2)
                g.affine_select(out=k.below[:, 0, :], in_=k.below[:, 0, :], compare_op=ALU.is_gt, fill=0.0,
                                base=0, pattern=[[1, P]], channel_multiplier=-1).then_inc(consts_set, 1)
                g.affine_select(out=k.below[:, 1, :], in_=k.below[:, 1, :], compare_op=ALU.is_ge, fill=0.0,
                                base=0, pattern=[[-1, P]], channel_multiplier=1).then_inc(consts_set, 1)
                g.memset(guard[:, :], -1.0).then_inc(consts_set, 1)

            @block.tensor
            def _(pe):
                pe.wait_ge(steps, 1)
                with pe.Fori(0, k.tiles // 2) as i:
                    for t in range(2):
                        for m in range(4):
                            pe.wait_ge(onehots, i * 8 + t * 4 + m + 1)
                            nc.tensor.matmul(count[:, m, :], ones_col[:, :], onehot[:, t * 4 + m, :], start=False,
                                             stop=True, skip_group_check=True).then_inc(counted, 1)

            @block.vector
            def _(dve):
                v = nc.vector
                c = Chain(dve, steps)
                v.memset(ones_col[:, :], 1.0)
                v.memset(ones_bins[:, :], 1.0)
                c.done(v.memset(count[:, :, :], 0.0))
                dve.wait_ge(loaded, 64)
                v.memset(k.edges[:, :, :], 0.0)
                for n in range(2):
                    v.tensor_scalar(split[:, n, 0, :], raw[:, n, :], BINS - 1, None, ALU.bitwise_and)
                    c.done(v.tensor_scalar(split[:, n, 1, :], raw[:, n, :], LOW_BITS, None,
                                           ALU.logical_shift_right))
                v.tensor_copy(dig[:, :, :], split[:, :, :, :].rearrange("p a b t -> p (a b) t"))
                c.done(v.tensor_copy(k.edges[:, :, 0:3], raw[:, :, :].rearrange("p n t -> p t n")))
                c.done(v.tensor_copy(k.edges[:, :, WEIGHT], weight[:, :]))
                dve.wait_ge(consts_set, 4)
                with dve.Fori(0, k.turns) as i:
                    dve.wait_ge(attr_loaded, i * 16 + 16)
                    c1 = Chain(dve, loop_steps, i, K + 1)
                    for t in range(K):
                        c1.done(v.tensor_tensor_reduce(out=prod[:, t % 2, :], in0=attr[:, t, :], in1=k.WeB[:, :],
                                                       scale=1.0, scalar=0.0, op0=ALU.mult, op1=ALU.add,
                                                       accum_out=dot[:, t:t + 1]))
                        dve.sem_inc(attr_used, 1)
                    c1.done(v.tensor_copy(k.edges[:, bass.ds(i * K, K), LOGIT], dot[:, :]))
                    c1.close()
                    for t in range(K):
                        for m in range(4):
                            if t >= 2:
                                dve.wait_ge(counted, i * K * 4 + (t - 2) * 4 + m + 1)
                            else:
                                dve.wait_ge(counted, i * K * 4)
                            v.tensor_scalar(onehot[:, (t % 2) * 4 + m, :], k.bins[:, :],
                                            dig[:, m, bass.ds(i * K + t, 1)], None,
                                            ALU.is_equal).then_inc(onehots, 1)
                dve.wait_ge(counted, k.tiles * 4)
                c.done(v.tensor_copy(seen[:, :, :], count[:, :, :]))
                for m in range(4):
                    c.done(v.tensor_tensor_scan(k.base[:, m, :], ones_bins[:, :], seen[:, m, :], 0.0,
                                                ALU.mult, ALU.add))
                c.done(v.tensor_tensor(k.base[:, :, :], k.base[:, :, :], seen[:, :, :], ALU.subtract))
                c.done(v.tensor_scalar(k.base[:, :, :], k.base[:, :, :], 1.0, None, ALU.add))
                for m in range(2):
                    c.done(v.tensor_copy(k.digits[:, m, :], dig[:, 2 * m, :]))


def radix_pass(k, name, base, load, digits, into):
    nc = k.nc
    with ExitStack() as own:
        def sb(what, shape, dt=F32):
            return own.enter_context(nc.sbuf_tensor(f"{what}_{name}", shape, dt))

        def sem(what):
            return k.semaphore((f"{what}_{name}"))

        onehot = sb("onehot", [P, K, BINS], BF16)
        picked = sb("picked", [P, 2, BINS])
        place = sb("place", [P, K])
        place_i = sb("place_i", [P, K], I32)
        payload = sb("payload", [P, K, COLS])
        rows = k.edges if load is None else sb("rows", [P, k.tiles, COLS])
        high = sb("high", [P, 2, k.tiles], I32)
        highf = sb("highf", [P, k.tiles])
        rank = own.enter_context(nc.psum_tensor(f"rank_{name}", [P, 2, 512], F32))
        loaded, steps, loop_steps = sem("rows_loaded"), sem("digit_steps"), sem("radix_steps")
        based, onehots, ranked = sem("bases_in"), sem("onehots"), sem("ranked")
        placed, read = sem("placed"), sem("ranks_read")
        scattered = [k.queue(f"scattered_0_{h}", k.turns * Q * 16) for h in range(2)]
        halves_taken = sem("halves_taken")
        key = digits if load is not None else None

        with nc.Block() as block:
            @block.sync
            def _(sp):
                if load is not None:
                    sp.dma_start(rows[:, :, :], load[1:k.E + 1, :].rearrange("(t p) w -> p t w", p=P)).then_inc(loaded, 16)

            @block.gpsimd
            def _(pool):
                with pool.Fori(0, k.turns) as i:
                    for h in range(2):
                        pool.wait_ge(placed, i * 2 + h + 1)
                        pool.sem_inc(halves_taken, 1)
                        for t in range(h * Q, h * Q + Q):
                            nc.gpsimd.indirect_dma_start(
                                into, bass.IndirectOffsetOnAxis(ap=place_i[:, t:t + 1], axis=0),
                                payload[:, t, :], None).then_inc(scattered[h].sem, 16)
                for h in range(2):
                    pool.wait_ge(scattered[h].sem, scattered[h].before + k.turns * Q * 16)

            @block.tensor
            def _(pe):
                def add(bank, mask, slot):
                    return nc.tensor.matmul(rank[:, bank, :], k.below[:, mask, :], onehot[:, slot, :],
                                            start=False, stop=True, skip_group_check=True)

                for bank in range(2):
                    nc.tensor.matmul(rank[:, bank, :], k.ones_row[:, 0:P], k.base[:, base, :],
                                     start=True, stop=True, skip_group_check=True)
                pe.wait_ge(based, 1)
                with pe.Fori(0, k.turns) as i:
                    for t in range(K):
                        pe.wait_ge(read, i * K + max(t - 1, 0))
                        add(t % 2, 1, (t - 2) % K)
                        add(t % 2, 2, (t - 1) % K)
                        pe.wait_ge(onehots, i * K + t + 1)
                        add(t % 2, 0, t).then_inc(ranked, 1)

            @block.vector
            def _(dve):
                v = nc.vector
                c = Chain(dve, steps)
                v.memset(onehot[:, K - 2:, :], 0.0).then_inc(based, 1)
                if load is None:
                    dig = k.digits[:, digits, :]
                else:
                    dve.wait_ge(loaded, 16)
                    c.done(v.tensor_copy(high[:, 0, :], rows[:, :, key]))
                    c.done(v.tensor_scalar(high[:, 1, :], high[:, 0, :], LOW_BITS, None, ALU.logical_shift_right))
                    c.done(v.tensor_copy(highf[:, :], high[:, 1, :]))
                    dig = highf[:, :]
                with dve.Fori(0, k.turns) as i:
                    c1 = Chain(dve, loop_steps, i, K + 2)

                    def mark(t, after):
                        dve.wait_ge(ranked, after)
                        v.tensor_scalar(onehot[:, t, :], k.bins[:, :], dig[:, bass.ds(i * K + t, 1)], None,
                                        ALU.is_equal).then_inc(onehots, 1)

                    for h in range(2):
                        for t in range(h * Q, h * Q + Q):
                            mark(t, i * K + max(t - 5, 0))
                        for t in range(h * Q, h * Q + Q):
                            dve.wait_ge(ranked, i * K + t + 1)
                            c1.done(v.tensor_tensor_reduce(out=picked[:, t % 2, :], in0=rank[:, t % 2, :],
                                                           in1=onehot[:, t, :], scale=1.0, scalar=0.0,
                                                           op0=ALU.mult, op1=ALU.add, accum_out=place[:, t:t + 1]))
                            dve.sem_inc(read, 1)
                        s = slice(h * Q, h * Q + Q)
                        dve.wait_ge(scattered[h].sem, i * Q * 16 + scattered[h].before)
                        v.tensor_copy(payload[:, s, :], rows[:, bass.ds(i * K + h * Q, Q), :])
                        c1.done(v.tensor_copy(place_i[:, s], place[:, s]))
                        dve.sem_inc(placed, 1)
                    c1.close()


class Norms:

    def __init__(self, flow, rows, tiles):
        self.flow, self.k, self.rows = flow, flow.k, rows
        self.stats, self.mv = flow.each("stats", [rows, tiles, 6]), flow.each("mv", [rows, tiles, 2])
        self.std, self.rs, self.nm = (flow.each(n, [rows, tiles]) for n in ("std", "rs", "nm"))

    def moments(self, c, b, s):
        v, n = self.k.nc.vector, s.shape[1]
        for j in range(n):
            ins = v.bn_stats(self.stats[b][:, j, :], s[:, j, :])
        c.done(ins)
        c.hold()
        for j in range(n):
            ins = v.bn_aggr(self.mv[b][:, j, :], self.stats[b][:, j, :])
        return ins

    def root(self, act, which=""):
        def step(i, b):
            self.flow.wait(act, "mv" + which, i, b)
            self.k.nc.scalar.activation(self.std[b][:, :], self.mv[b][:, :, 1], ACT.Sqrt,
                                        bias=self.k.eps1[0:self.rows, :]).then_inc(self.flow.on["std" + which], 1)
        return step

    def shift(self, dve, which=""):
        def step(i, b):
            v = self.k.nc.vector
            c = self.flow.chain(dve, "v_shift" + which, i, b, 1)
            self.flow.wait(dve, "std" + which, i, b)
            c.done(v.reciprocal(self.rs[b][:, :], self.std[b][:, :]))
            v.scalar_tensor_tensor(self.nm[b][:, :], self.mv[b][:, :, 0], -1.0, self.rs[b][:, :], ALU.mult,
                                   ALU.mult).then_inc(self.flow.on["nm" + which], 1)
        return step


def normalise(k, out, s, rs, nm):
    for j in range(out.shape[1]):
        ins = k.nc.scalar.activation(out[:, j, :], s[:, j, :], ACT.Identity, bias=nm[:, j:j + 1],
                                     scale=rs[:, j:j + 1])
    return ins


def transpose_tiles(k, out, x):
    rows = x.shape[0]
    for j in range(x.shape[1]):
        ins = k.nc.tensor.transpose(out[:, j, 0:rows], x[:, j, :], k.ident[0:rows, 0:rows])
    return ins


def project_pair(k, out, xT, weights, bias3):
    rows = out.shape[0]
    k.nc.tensor.matmul(out[:, :, :], k.ones3[:, 0:rows], bias3[:, :, :], start=True, stop=False, skip_group_check=True)
    for j in range(2):
        ins = k.nc.tensor.matmul(out[:, j, :], xT[:, j, :], weights[:, :], start=False, stop=True,
                                 skip_group_check=True)
    return ins


def halves(sp, to, of, sem):
    rows = to.shape[0]
    sp.dma_start(to[0:112], of[0:112]).then_inc(sem, 16)
    sp.dma_start(to[112:rows], of[112:rows]).then_inc(sem, 16)


def pairs(quad):
    return quad[:, :, :].rearrange("p (a b) d -> p a b d", a=2)


class Flow:

    def __init__(self, k, name, turns, slots, stages):
        assert stages % slots == 0 and turns > 2
        self.k, self.name, self.turns, self.slots, self.stages = k, name, turns, slots, stages
        self.items = turns * slots
        self.own = ExitStack()
        self.on = {}
        self.links, self.held = {}, {}

    def sb(self, what, shape, dt=F32):
        return self.own.enter_context(self.k.nc.sbuf_tensor(f"{self.name}_{what}", shape, dt))

    def each(self, what, shape, dt=F32, copies=None):
        n = copies or self.slots
        some = [self.sb(f"{what}{b}", shape, dt) for b in range(n)]
        return [some[b % n] for b in range(self.slots)]

    def ps(self, what, shape, copies=1):
        some = [self.own.enter_context(self.k.nc.psum_tensor(f"{self.name}_{what}{n}", shape, F32))
                for n in range(copies)]
        return [some[b % copies] for b in range(self.slots)]

    def sem(self, what):
        return self.k.semaphore(f"{self.name}_{what}")

    def sems(self, *names):
        for n in names:
            self.on[n] = self.sem(n)

    def norms(self, rows, tiles):
        return Norms(self, rows, tiles)

    def item(self, i, b):
        return i * self.slots + b

    def wait(self, engine, event, i, b, back=0, per=1, part=1):
        if isinstance(event, str):
            event = self.on[event]
        value = (self.item(i, b) - back) * per + part
        if isinstance(value, int):
            value = min(value, self.items * per)
        if not isinstance(value, int) or value > 0:
            engine.wait_ge(event, value)

    def arrived(self, engine, sem, i, amount=16, before=0):
        value = (i + (1 - before)) * amount
        if isinstance(sem, Queue):
            sem, value = sem.sem, value + sem.before
        if not isinstance(value, int) or value > 0:
            engine.wait_ge(sem, value)

    def chain(self, engine, what, i, b, steps):
        if what not in self.links:
            self.links[what] = self.sem(what)
        return Chain(engine, self.links[what], self.item(i, b), steps, held=self.holder(engine))

    def holder(self, engine):
        if engine not in self.held:
            self.held[engine] = self.sem(f"held{len(self.held)}")
        return self.held[engine]

    def hold(self, engine):
        engine.sem_inc(self.holder(engine), 1)

    def run(self, engine, steps):
        lag = self.stages // self.slots

        def turn(i, first=False, last=False):
            for tau in range(self.stages):
                for b in reversed(range(self.slots)):
                    stage, back = tau - lag * b, 0
                    if stage < 0:
                        stage, back = stage + self.stages, 1
                    if stage in steps and not (back and first) and not (not back and last):
                        steps[stage](i - back, b)

        turn(0, first=True)
        turn(1)
        with engine.Fori(2, self.turns) as i:
            turn(i)
        turn(self.turns, last=True)


def dense(k):
    nc = k.nc
    fl = Flow(k, "dense", k.groups // 4, 8, 24)
    x, s, x1, s3, s4, x4 = (fl.each(n, [P, Q, D]) for n in ("x", "s", "x1", "s3", "s4", "x4"))
    x23 = fl.each("x23", [P, Q, 2 * D])
    x2, x3 = [t[:, :, 0:D] for t in x23], [t[:, :, D:] for t in x23]
    xT, x2T = fl.each("xT", [D, Q, D], copies=2), fl.each("x2T", [D, Q, D], copies=2)
    junk = fl.each("junk", [P, D], copies=2)
    ss, std0, rs0, std2, rs2, nm2 = (fl.each(n, [P, Q]) for n in ("ss", "std0", "rs0", "std2", "rs2", "nm2"))
    norm = fl.norms(P, Q)
    T, T2, O, O2 = fl.ps("T", [D, Q, D]), fl.ps("T2", [D, Q, D]), fl.ps("O", [P, 2, 2, 2 * D]), fl.ps("O2", [P, 2, 2, 2 * D])
    x_loaded, x1_stored, x23_stored, out_stored = ([fl.sem(f"{n}{b}") for b in range(fl.slots)] for n in (
        "x_loaded", "x1_stored", "x23_stored", "out_stored"))
    h1_stored = fl.sem("h1_stored")
    fl.sems("t", "c", "o", "square", "std0", "summed", "mv", "std", "nm", "x1", "x2", "t2", "c2", "o2", "relu", "summed3",
            "mv3", "std3", "nm3", "x3", "mv4", "std4", "nm4", "x4")

    def rows(table, i, b):
        group = table[bass.ds((i * 4 + b // 2) * (P * K), P * K), :].rearrange("(p j) d -> p j d", p=P)
        return group[:, (b % 2) * Q:(b % 2) * Q + Q, :]

    with nc.Block() as block:
        @block.gpsimd
        def _(pool):
            def norm2(i, b):
                fl.wait(pool, "nm", i, b)
                fl.arrived(pool, x23_stored[b], i, 32, before=1)
                fl.hold(pool)
                for j in range(Q):
                    ins = nc.gpsimd.tensor_scalar(x2[b][:, j, :], s[b][:, j, :], rs2[b][:, j:j + 1], nm2[b][:, j:j + 1],
                                                  ALU.mult, ALU.add)
                ins.then_inc(fl.on["x2"], 1)

            fl.run(pool, {10: norm2})

        @block.sync
        def _(sp):
            def load(i, b):
                fl.wait(sp, "summed", i, b, back=fl.slots)
                fl.hold(sp)
                halves(sp, x[b], rows(k.arg["x"], i, b), x_loaded[b])

            def store_h1(i, b):
                if b % 2 == 0:
                    sp.dma_start(k.h1[bass.ds((i * 4 + b // 2) * (P * K), P * K), :].rearrange("(p j) d -> p (j d)", p=P),
                                 k.sig1B[:, :]).then_inc(h1_stored, 16)

            def store_x1(i, b):
                fl.wait(sp, "x1", i, b)
                fl.hold(sp)
                halves(sp, rows(k.x1, i, b), x1[b], x1_stored[b])

            def store_x23(i, b):
                fl.wait(sp, "x3", i, b)
                fl.hold(sp)
                halves(sp, rows(k.x23, i, b), x23[b], x23_stored[b])

            def store_out(i, b):
                fl.wait(sp, "x4", i, b)
                fl.hold(sp)
                halves(sp, rows(k.arg["out"], i, b), x4[b], out_stored[b])

            fl.run(sp, {0: load, 1: store_h1, 11: store_x1, 19: store_x23, 23: store_out})
            for b in range(fl.slots):
                for stored in (x1_stored, x23_stored, out_stored):
                    sp.wait_ge(stored[b], 32 * fl.turns)
            sp.wait_ge(h1_stored, 16 * k.groups)

        @block.tensor
        def _(pe):
            def transpose(i, b):
                fl.arrived(pe, x_loaded[b], i, 32)
                fl.wait(pe, "c", i, b, back=1)
                transpose_tiles(k, T[b], x[b]).then_inc(fl.on["t"], 1)

            def layer0(i, b):
                fl.wait(pe, "c", i, b)
                fl.wait(pe, "summed", i, b, back=1)
                for h in range(2):
                    ins = project_pair(k, O[b][:, h, :, :], xT[b][:, 2 * h:2 * h + 2, 0:P], k.W0cat, k.bias0)
                ins.then_inc(fl.on["o"], 1)

            def transpose2(i, b):
                fl.wait(pe, "x2", i, b)
                fl.wait(pe, "c2", i, b, back=1)
                transpose_tiles(k, T2[b], x2[b]).then_inc(fl.on["t2"], 1)

            def layer2(i, b):
                fl.wait(pe, "c2", i, b)
                fl.wait(pe, "summed3", i, b, back=1)
                for h in range(2):
                    ins = project_pair(k, O2[b][:, h, :, :], x2T[b][:, 2 * h:2 * h + 2, 0:P], k.W2cat, k.bias2)
                ins.then_inc(fl.on["o2"], 1)

            fl.run(pe, {3: transpose, 5: layer0, 11: transpose2, 13: layer2})

        @block.scalar
        def _(act):
            a = nc.scalar

            def copy(i, b):
                fl.wait(act, "t", i, b)
                fl.wait(act, "o", i, b, back=2)
                a.activation(xT[b][:, :, 0:P], T[b][:, :, 0:P], ACT.Copy).then_inc(fl.on["c"], 1)

            def variance0(i, b):
                fl.wait(act, "o", i, b)
                fl.wait(act, "summed", i, b, back=fl.slots)
                for j in range(Q):
                    a.activation(junk[b][:, :], O[b][:, j // 2, j % 2, 0:D], ACT.Square,
                                 accum_out=ss[b][:, j:j + 1]).then_inc(fl.on["square"], 1)
                    fl.wait(act, "square", i, b, per=Q, part=j + 1)
                a.activation(std0[b][:, :], ss[b][:, :], ACT.Sqrt, bias=k.eps1[0:P, :],
                             scale=1.0 / D).then_inc(fl.on["std0"], 1)

            def root1(i, b):
                fl.wait(act, "mv", i, b)
                a.activation(norm.std[b][:, :], norm.mv[b][:, :, 1], ACT.Sqrt, bias=k.eps1[0:P, :])
                a.activation(std2[b][:, :], norm.mv[b][:, :, 1], ACT.Sqrt, bias=k.eps2[0:P, :],
                             scale=1.0 + EPS).then_inc(fl.on["std"], 1)

            def norm1(i, b):
                fl.wait(act, "nm", i, b)
                fl.arrived(act, x1_stored[b], i, 32, before=1)
                normalise(k, x1[b], s[b], norm.rs[b], norm.nm[b]).then_inc(fl.on["x1"], 1)

            def copy2(i, b):
                fl.wait(act, "t2", i, b)
                fl.wait(act, "o2", i, b, back=2)
                a.activation(x2T[b][:, :, 0:P], T2[b][:, :, 0:P], ACT.Copy).then_inc(fl.on["c2"], 1)

            def relu(i, b):
                fl.wait(act, "o2", i, b)
                a.activation(pairs(s4[b]), O2[b][:, :, :, 0:D], ACT.Relu).then_inc(fl.on["relu"], 1)

            def norm3(i, b):
                fl.wait(act, "nm3", i, b)
                normalise(k, x3[b], s3[b], norm.rs[b], norm.nm[b]).then_inc(fl.on["x3"], 1)

            def norm4(i, b):
                fl.wait(act, "nm4", i, b)
                fl.arrived(act, out_stored[b], i, 32, before=1)
                normalise(k, x4[b], s4[b], norm.rs[b], norm.nm[b]).then_inc(fl.on["x4"], 1)

            fl.run(act, {4: copy, 6: variance0, 8: root1, 10: norm1, 12: copy2, 14: relu, 16: norm.root(act, "3"),
                         18: norm3, 20: norm.root(act, "4"), 22: norm4})

        @block.vector
        def _(dve):
            v = nc.vector

            def sum1(i, b):
                c = fl.chain(dve, "v_sum1", i, b, 4)
                fl.wait(dve, "std0", i, b)
                fl.wait(dve, "x2", i, b, back=fl.slots)
                c.done(v.reciprocal(rs0[b][:, :], std0[b][:, :]))
                for j in range(Q):
                    ins = v.scalar_tensor_tensor(s[b][:, j, :], O[b][:, j // 2, j % 2, D:], rs0[b][:, j:j + 1],
                                                 k.betaB[0:P, :], ALU.mult, ALU.add)
                c.done(ins)
                c.done(v.scalar_tensor_tensor(s[b][:, :, :], s[b][:, :, :], 0.0, x[b][:, :, :], ALU.max, ALU.add))
                dve.sem_inc(fl.on["summed"], 1)
                norm.moments(c, b, s[b]).then_inc(fl.on["mv"], 1)
                c.close()

            def shift1(i, b):
                c = fl.chain(dve, "v_shift1", i, b, 1)
                fl.wait(dve, "std", i, b)
                v.reciprocal(norm.rs[b][:, :], norm.std[b][:, :])
                c.done(v.reciprocal(rs2[b][:, :], std2[b][:, :]))
                for nm, rs in ((norm.nm, norm.rs), (nm2, rs2)):
                    ins = v.scalar_tensor_tensor(nm[b][:, :], norm.mv[b][:, :, 0], -1.0, rs[b][:, :], ALU.mult, ALU.mult)
                ins.then_inc(fl.on["nm"], 1)

            def sum3(i, b):
                c = fl.chain(dve, "v_sum3", i, b, 2)
                fl.wait(dve, "relu", i, b)
                c.done(v.tensor_tensor(pairs(s3[b]), O2[b][:, :, :, D:], pairs(s4[b]), ALU.add))
                dve.sem_inc(fl.on["summed3"], 1)
                norm.moments(c, b, s3[b]).then_inc(fl.on["mv3"], 1)
                c.close()

            def sum4(i, b):
                c = fl.chain(dve, "v_sum4", i, b, 2)
                fl.wait(dve, "x3", i, b)
                c.done(v.tensor_tensor(s4[b][:, :, :], x3[b], k.sig2B[0:P, :].unsqueeze(1).to_broadcast([P, Q, D]), ALU.add))
                norm.moments(c, b, s4[b]).then_inc(fl.on["mv4"], 1)
                c.close()

            fl.run(dve, {7: sum1, 9: shift1, 15: sum3, 17: norm.shift(dve, "3"), 19: sum4, 21: norm.shift(dve, "4")})
    fl.own.close()


class Order:

    def __init__(self, k, name, table, key):
        nc = k.nc
        self.k, self.key = k, key
        own = self.own = ExitStack()

        def sb(what, shape, dt=F32):
            return own.enter_context(nc.sbuf_tensor(f"{name}_{what}", shape, dt))

        def sem(what):
            return k.semaphore((f"{name}_{what}"))

        self.cols = sb("cols", [R, k.tiles, COLS])
        self.keys = sb("keys_in", [R, k.tiles])
        self.ids = sb("ids", [R, 6, k.tiles], I32)
        self.lead = sb("lead", [R, 2, k.tiles], I32)
        self.keyB = sb("keyB", [R, k.tiles * R])
        keys = k.dram(f"{name}_keys", (1, k.tiles * R))
        with ExitStack() as tmp:
            raw = tmp.enter_context(nc.sbuf_tensor(f"{name}_raw", [R, k.tiles, COLS], F32))
            before = tmp.enter_context(nc.sbuf_tensor(f"{name}_before", [R, k.tiles, 1], F32))
            same = tmp.enter_context(nc.sbuf_tensor(f"{name}_same", [R, k.tiles], F32))
            loaded, keys_out, keys_in, steps = (sem(x) for x in ("loaded", "keys_stored", "keys_loaded", "steps"))
            with nc.Block() as block:
                @block.sync
                def _(sp):
                    slow = dict(allow_slow_non_contiguous=True)
                    sp.dma_start(raw[1:R, :, :], table[1:k.E + 1, :].rearrange("(t p) w -> p t w", p=P)).then_inc(loaded, 16)
                    sp.dma_start(raw[0:1, 0:k.tiles - 1, :],
                                 table[1 + P:k.E + 1, :].rearrange("(t p) w -> p t w", p=P)[0:1]).then_inc(loaded, 16)
                    sp.dma_start(before[1:R, :, :], table[0:k.E, key:key + 1].rearrange("(t p) w -> p t w", p=P),
                                 **slow).then_inc(loaded, 16)
                    sp.wait_ge(loaded, 48)
                    out = keys.rearrange("a (t r) -> r t a", r=R)
                    sp.dma_start(out[1:R], raw[1:R, :, key:key + 1], **slow).then_inc(keys_out, 16)
                    sp.dma_start(out[0:1], raw[1:2, :, key:key + 1], **slow).then_inc(keys_out, 16)
                    sp.wait_ge(keys_out, 32)
                    sp.dma_start(self.keyB[0:112, :], keys.to_broadcast([112, k.tiles * R])).then_inc(keys_in, 16)
                    sp.dma_start(self.keyB[112:R, :], keys.to_broadcast([R - 112, k.tiles * R])).then_inc(keys_in, 16)
                    sp.wait_ge(keys_in, 32)

                @block.vector
                def _(dve):
                    v = nc.vector
                    c = Chain(dve, steps)
                    v.memset(raw[0:1, k.tiles - 1:, :], 0.0)
                    c.done(v.memset(before[0:1, :, :], 0.0))
                    dve.wait_ge(loaded, 48)
                    c.done(v.tensor_copy(self.cols[:, :, :], raw[:, ::-1, :]))
                    c.done(v.tensor_copy(self.keys[:, :], self.cols[:, :, key]))
                    v.memset(self.keys[0:1, 0:1], -1.0)
                    ends = self.cols[:, :, 0:2].rearrange("p t w -> p w t")
                    v.tensor_copy(self.ids[:, 0:2, :], ends)
                    v.tensor_scalar(self.ids[:, 2:4, :], ends, 2.0, None, ALU.mult)
                    v.tensor_scalar(self.ids[:, 4:6, :], ends, 2.0, 1.0, ALU.mult, ALU.add)
                    c.done(v.tensor_tensor(same[:, :], self.cols[:, :, key], before[:, ::-1, 0], ALU.is_equal))
                    c.done(v.memset(same[0:1, :], 1.0))
                    c.done(v.scalar_tensor_tensor(same[:, :], same[:, :], float(FAR), self.cols[:, :, key],
                                                  ALU.mult, ALU.add))
                    v.tensor_copy(self.lead[:, 0, :], same[:, :])
                    v.tensor_scalar(self.lead[:, 1, :], same[:, :], 2.0, 1.0, ALU.mult, ALU.add)


class Edges(Flow):

    def __init__(self, k, name, order, stages):
        slots = 10
        assert k.tiles % (2 * slots) == 0
        super().__init__(k, name, k.tiles // (2 * slots), slots, stages)
        self.order = order
        self.gather_list, self.scatter_list = (), ()

    def tile(self, i, b):
        return (i * self.slots + b) * 2

    def gathers(self, ids, freed, *of):
        self.gather_list, self.gather_ids, self.freed = of, ids, freed
        self.ix = self.each("ix", [R, len(of), 2], I32)
        self.gathered = [self.k.queue(f"gathered_{b}", self.turns * 32 * len(of)) for b in range(self.slots)]

    def scatters(self, *of):
        self.scatter_list = of
        self.lx = [self.each(f"lx{n}_", [R, 2], I32) for n in range(len(of))]
        self.scattered = [[self.k.queue(f"scattered_{n}_{b}", self.turns * 32) for b in range(self.slots)]
                          for n in range(len(of))]

    def gathered_all(self, engine, i, b):
        self.arrived(engine, self.gathered[b], i, 32 * len(self.gather_list))

    def scattered_before(self, engine, n, i, b):
        self.arrived(engine, self.scattered[n][b], i, 32, before=1)

    def gather(self, pool, i, b):
        g = self.k.nc.gpsimd
        for event in self.freed:
            self.wait(pool, event, i, b, back=self.slots)
            self.hold(pool)
        c = self.chain(pool, "rows_chosen", i, b, 1)
        c.done(g.tensor_copy(self.ix[b][:, :, :], self.order.ids[:, self.gather_ids, bass.ds(self.tile(i, b), 2)]))
        c.hold()
        for n, (table, to, width) in enumerate(self.gather_list):
            for j in range(2):
                g.indirect_dma_start(to[b][:, j, 0:width], None, table,
                                     bass.IndirectOffsetOnAxis(ap=self.ix[b][:, n, j:j + 1], axis=0)
                                     ).then_inc(self.gathered[b].sem, 16)

    def scatter(self, pool, n, i, b):
        g = self.k.nc.gpsimd
        table, of, width, ready, lead = self.scatter_list[n]
        self.scattered_before(pool, n, i, b)
        self.hold(pool)
        c = self.chain(pool, f"leads_chosen{n}", i, b, 1)
        c.done(g.tensor_copy(self.lx[n][b][:, :], self.order.lead[:, lead, bass.ds(self.tile(i, b), 2)]))
        c.hold()
        self.wait(pool, ready, i, b)
        self.hold(pool)
        for j in range(2):
            g.indirect_dma_start(table, bass.IndirectOffsetOnAxis(ap=self.lx[n][b][:, j:j + 1], axis=0),
                                 of[b][:, j, 0:width], None, bounds_check=table.shape[0] - 1,
                                 oob_is_err=False).then_inc(self.scattered[n][b].sem, 16)

    def landed(self, pool):
        for b in range(self.slots):
            if self.gather_list:
                self.arrived(pool, self.gathered[b], self.turns - 1, 32 * len(self.gather_list))
            for n in range(len(self.scatter_list)):
                self.arrived(pool, self.scattered[n][b], self.turns - 1, 32)

    def segments(self, width):
        self.sel = self.each("sel", [R, 2, R], copies=2)
        self.spare_row = self.sb("spare_row", [1, width])
        self.sems("masks", "total", "carried")

    def masks(self, dve, i, b):
        self.wait(dve, "total", i, b, back=2, per=2, part=2)
        for j in range(2):
            n = self.tile(i, b) + j
            ins = self.k.nc.vector.tensor_scalar(self.sel[b][:, j, :],
                                                 self.order.keyB[:, bass.ds((self.k.tiles - 1 - j) * R - self.tile(i, b) * R, R)],
                                                 self.order.keys[:, bass.ds(n, 1)], None, ALU.is_equal)
        ins.then_inc(self.on["masks"], 1)

    def totals(self, pe, i, b, out, rows):
        self.wait(pe, "masks", i, b)
        for j in range(2):
            self.wait(pe, "carried", i, b, per=2, part=j)
            self.k.nc.tensor.matmul(out(j), self.sel[b][:, j, :], rows(j), start=True,
                                    stop=True).then_inc(self.on["total"], 1)

    def carry(self, act, i, b, buffers, tot, filled):
        width = self.spare_row.shape[1]
        for j in range(2):
            self.wait(act, "total", i, b, per=2, part=j + 1)
            if j == 0:
                to = buffers[b][0:1, 1, 0:width]
            else:
                next_i, next_b = (i + 1, 0) if b == self.slots - 1 else (i, b + 1)
                if isinstance(next_i, int) and next_i == self.turns:
                    to = self.spare_row[:, :]
                else:
                    filled(next_i, next_b)
                    to = buffers[next_b][0:1, 0, 0:width]
            self.k.nc.scalar.activation(to, tot[b][0:1, j, 0:width], ACT.Copy).then_inc(self.on["carried"], 1)

    def carried(self, engine, i, b):
        self.wait(engine, "carried", i, b, per=2, part=2)


def layer0(k, order):
    nc = k.nc
    fl = Edges(k, "l0", order, 30)
    W = D + 1
    XS, XD, mean, s, x1 = (fl.each(n, [R, 2, w]) for n, w in (("xs", D + 4), ("xd", D), ("mean", D), ("s", D), ("x1", D)))
    aT = fl.each("aT", [D, 2, R], copies=2)
    junk = fl.each("junk", [R, D])
    ss, deg, std0, rs0 = (fl.each(n, [R, 2]) for n in ("ss", "deg", "std0", "rs0"))
    norm = fl.norms(R, 2)
    T, O, tot = fl.ps("T", [D, 4, D], 2), fl.ps("O", [R, 2, 2 * D], 2), fl.ps("tot", [R, 2, 2 * D], 2)
    fl.segments(W)
    fl.sems("mean", "totals_used", "t", "c", "o", "square", "std0", "summed", "mv", "std", "nm", "x1")
    fl.gathers(slice(0, 2), ("summed",), (k.arg["x"], XS, D), (k.arg["x"], XD, D))
    fl.scatters((k.x1, x1, D, "x1", 0))

    with nc.Block() as block:
        @block.gpsimd
        def _(pool):
            fl.run(pool, {0: lambda i, b: fl.gather(pool, i, b), 20: lambda i, b: fl.scatter(pool, 0, i, b)})
            fl.landed(pool)

        @block.tensor
        def _(pe):
            def totals(i, b):
                fl.gathered_all(pe, i, b)
                fl.wait(pe, "totals_used", i, b, back=2)
                fl.totals(pe, i, b, lambda j: tot[b][:, j, 0:W], lambda j: XS[b][:, j, 0:W])

            def transpose(i, b):
                fl.wait(pe, "mean", i, b)
                fl.wait(pe, "c", i, b, back=2)
                transpose_tiles(k, T[b], mean[b]).then_inc(fl.on["t"], 1)

            def project(i, b):
                fl.wait(pe, "c", i, b)
                fl.wait(pe, "summed", i, b, back=2)
                project_pair(k, O[b], aT[b], k.W0cat, k.bias0).then_inc(fl.on["o"], 1)

            fl.run(pe, {10: totals, 12: transpose, 14: project})

        @block.scalar
        def _(act):
            a = nc.scalar

            def carry(i, b):
                fl.carry(act, i, b, XS, tot, lambda ni, nb: fl.gathered_all(act, ni, nb))

            def copy(i, b):
                fl.wait(act, "t", i, b)
                fl.wait(act, "o", i, b, back=2)
                a.activation(aT[b][:, :, :], T[b][:, 0:2, 0:R], ACT.Copy).then_inc(fl.on["c"], 1)

            def variance0(i, b):
                fl.wait(act, "o", i, b)
                fl.wait(act, "summed", i, b, back=fl.slots)
                for j in range(2):
                    a.activation(junk[b][:, :], O[b][:, j, 0:D], ACT.Square,
                                 accum_out=ss[b][:, j:j + 1]).then_inc(fl.on["square"], 1)
                    fl.wait(act, "square", i, b, per=2, part=j + 1)
                a.activation(std0[b][:, :], ss[b][:, :], ACT.Sqrt, bias=k.eps1[0:R, :],
                             scale=1.0 / D).then_inc(fl.on["std0"], 1)

            def norm1(i, b):
                fl.wait(act, "nm", i, b)
                fl.scattered_before(act, 0, i, b)
                normalise(k, x1[b][:, :, :], s[b], norm.rs[b], norm.nm[b]).then_inc(fl.on["x1"], 1)

            fl.run(act, {10: carry, 13: copy, 15: variance0, 17: norm.root(act), 19: norm1})

        @block.vector
        def _(dve):
            v = nc.vector
            for x in XS:
                v.memset(x[:, :, D:D + 1], 1.0)

            def masks(i, b):
                fl.masks(dve, i, b)

            def mean_of(i, b):
                c = fl.chain(dve, "v_mean", i, b, 3)
                fl.carried(dve, i, b)
                c.done(v.tensor_scalar(deg[b][:, :], tot[b][:, :, D], 1.0, 1.0, ALU.add, ALU.max))
                fl.gathered_all(dve, i, b)
                c.done(v.tensor_tensor(mean[b][:, :, :], tot[b][:, :, 0:D], XD[b][:, :, :], ALU.add))
                dve.sem_inc(fl.on["totals_used"], 1)
                c.done(v.reciprocal(deg[b][:, :], deg[b][:, :]))
                v.tensor_tensor(mean[b][:, :, :], mean[b][:, :, :], deg[b][:, :].unsqueeze(2).to_broadcast([R, 2, D]),
                                ALU.mult).then_inc(fl.on["mean"], 1)

            def sum1(i, b):
                c = fl.chain(dve, "v_sum", i, b, 4)
                fl.wait(dve, "std0", i, b)
                c.done(v.reciprocal(rs0[b][:, :], std0[b][:, :]))
                for j in range(2):
                    ins = v.scalar_tensor_tensor(s[b][:, j, :], O[b][:, j, D:], rs0[b][:, j:j + 1], k.betaB[:, :],
                                                 ALU.mult, ALU.add)
                c.done(ins)
                c.done(v.scalar_tensor_tensor(s[b][:, :, :], s[b][:, :, :], 0.0, XD[b][:, :, :], ALU.max, ALU.add))
                dve.sem_inc(fl.on["summed"], 1)
                norm.moments(c, b, s[b]).then_inc(fl.on["mv"], 1)
                c.close()

            fl.run(dve, {9: masks, 11: mean_of, 16: sum1, 18: norm.shift(dve)})
    fl.own.close()


def layer1(k, order):
    nc = k.nc
    fl = Edges(k, "l1", order, 40)
    XS, XD = fl.each("xs", [R, 2, D]), fl.each("xd", [R, 2, D])
    s = s3 = XS
    x23 = fl.each("x23", [R, 2, 2 * D])
    x2, x3 = [t[:, :, 0:D] for t in x23], [t[:, :, D:] for t in x23]
    xT, x2T = fl.each("xT", [D, 4, R], copies=2), fl.each("x2T", [D, 2, R], copies=2)
    rels, relsT = fl.each("rels", [R, 2, RELS]), fl.each("relsT", [RELS, 2, R], copies=2)
    iota8 = fl.sb("iota8", [R, RELS])
    wide = fl.sb("wide", [R, 2, RELS * D])
    bent = fl.sb("bent", [R, 2, RELS * D])
    norm = fl.norms(R, 2)
    T, TR = fl.ps("T", [D, 4, D]), fl.ps("TR", [RELS, 4, D])
    Y, O2 = fl.ps("Y", [R, 4, D]), fl.ps("O2", [R, 2, 2 * D])
    tot = fl.ps("tot", [R, 2, 2, 512])[0]
    fl.segments(RELS * D)
    fl.sems("iota", "rels", "t", "c", "y", "wide", "bent", "reduced", "summed", "mv", "std", "nm", "x2", "t2", "c2", "o2", "relu",
            "summed3", "mv3", "std3", "nm3", "x3")
    fl.gathers(slice(0, 2), ("x3",), (k.x1, XS, D), (k.x1, XD, D))
    fl.scatters((k.x23, x23, 2 * D, "x3", 0))

    with nc.Block() as block:
        @block.gpsimd
        def _(pool):
            nc.gpsimd.iota(iota8[:, :], [[1, RELS]], base=0, channel_multiplier=0,
                           allow_small_or_imprecise_dtypes=True).then_inc(fl.on["iota"], 1)
            fl.run(pool, {0: lambda i, b: fl.gather(pool, i, b), 34: lambda i, b: fl.scatter(pool, 0, i, b)})
            fl.landed(pool)

        @block.tensor
        def _(pe):
            t = nc.tensor

            def transpose(i, b):
                fl.gathered_all(pe, i, b)
                fl.wait(pe, "rels", i, b)
                fl.wait(pe, "c", i, b, back=1)
                fl.wait(pe, "c2", i, b, back=5)
                transpose_tiles(k, T[b], XS[b])
                transpose_tiles(k, T[b][:, 2:4, :], XD[b])
                transpose_tiles(k, TR[b], rels[b]).then_inc(fl.on["t"], 1)

            def message(i, b):
                fl.wait(pe, "c", i, b)
                fl.wait(pe, "wide", i, b, back=1, per=2, part=2)
                for j in range(2):
                    t.matmul(Y[b][:, j, :], xT[b][:, j, :], k.W1aT[:, :], start=True, stop=False)
                    t.matmul(Y[b][:, j, :], xT[b][:, 2 + j, :], k.W1bT[:, :], start=False, stop=False)
                    ins = t.matmul(Y[b][:, j, :], relsT[b][:, j, :], k.relC[:, :], start=False, stop=True)
                ins.then_inc(fl.on["y"], 1)

            def total(j):
                def step(i, b):
                    fl.wait(pe, "masks", i, b)
                    fl.wait(pe, "wide", i, b, per=2, part=j + 1)
                    fl.wait(pe, "carried", i, b, per=2, part=j)
                    fl.wait(pe, "bent", i, b, back=1, per=2, part=j + 1)
                    for h in range(2):
                        ins = t.matmul(tot[:, j, h, :], fl.sel[b][:, j, :], wide[:, j, 512 * h:512 * h + 512],
                                       start=True, stop=True)
                    ins.then_inc(fl.on["total"], 1)
                return step

            def transpose2(i, b):
                fl.wait(pe, "x2", i, b)
                fl.wait(pe, "c2", i, b, back=1)
                fl.wait(pe, "c", i, b, back=-4)
                transpose_tiles(k, T[b], x2[b]).then_inc(fl.on["t2"], 1)

            def project2(i, b):
                fl.wait(pe, "c2", i, b)
                fl.wait(pe, "summed3", i, b, back=1)
                project_pair(k, O2[b], x2T[b], k.W2cat, k.bias2).then_inc(fl.on["o2"], 1)

            fl.run(pe, {5: transpose, 7: message, 10: total(0), 13: total(1), 23: transpose2, 25: project2})

        @block.scalar
        def _(act):
            a = nc.scalar

            def copy(i, b):
                fl.wait(act, "t", i, b)
                fl.wait(act, "y", i, b, back=2)
                a.activation(xT[b][:, :, :], T[b][:, :, 0:R], ACT.Copy)
                a.activation(relsT[b][:, :, :], TR[b][:, 0:2, 0:R], ACT.Copy).then_inc(fl.on["c"], 1)

            def carry_in(i, b):
                fl.wait(act, "wide", i, b, per=2, part=1)
                fl.wait(act, "total", i, b, per=2, part=0)
                if not (isinstance(i, int) and fl.item(i, b) == 0):
                    a.activation(wide[0:1, 0, :].rearrange("p (h d) -> p h d", h=2), tot[0:1, 1, :, :],
                                 ACT.Copy).then_inc(fl.on["carried"], 1)

            def carry_over(i, b):
                fl.wait(act, "wide", i, b, per=2, part=2)
                fl.wait(act, "total", i, b, per=2, part=1)
                a.activation(wide[0:1, 1, :].rearrange("p (h d) -> p h d", h=2), tot[0:1, 0, :, :],
                             ACT.Copy).then_inc(fl.on["carried"], 1)

            def bend(j):
                def step(i, b):
                    fl.wait(act, "total", i, b, per=2, part=j + 1)
                    fl.wait(act, "reduced", i, b, back=1, per=2, part=j + 1)
                    if j == 0:
                        carry_over(i, b)
                    a.activation(bent[:, j, :].rearrange("p (h d) -> p h d", h=2), tot[:, j, :, :],
                                 ACT.Tanh).then_inc(fl.on["bent"], 1)
                return step

            def norm2(i, b):
                fl.wait(act, "nm", i, b)
                fl.scattered_before(act, 0, i, b)
                normalise(k, x2[b], s[b], norm.rs[b], norm.nm[b]).then_inc(fl.on["x2"], 1)

            def copy2(i, b):
                fl.wait(act, "t2", i, b)
                fl.wait(act, "o2", i, b, back=2)
                a.activation(x2T[b][:, :, :], T[b][:, 0:2, 0:R], ACT.Copy).then_inc(fl.on["c2"], 1)

            def relu(i, b):
                fl.wait(act, "o2", i, b)
                a.activation(s3[b][:, :, :], O2[b][:, :, 0:D], ACT.Relu).then_inc(fl.on["relu"], 1)

            def norm3(i, b):
                fl.wait(act, "nm3", i, b)
                normalise(k, x3[b], s3[b], norm.rs[b], norm.nm[b]).then_inc(fl.on["x3"], 1)

            fl.run(act, {6: copy, 9: carry_in, 12: bend(0), 14: bend(1), 19: norm.root(act), 21: norm2, 24: copy2, 26: relu,
                         31: norm.root(act, "3"), 33: norm3})

        @block.vector
        def _(dve):
            v = nc.vector
            dve.wait_ge(fl.on["iota"], 1)

            def relations(i, b):
                fl.wait(dve, "wide", i, b, back=fl.slots, per=2, part=2)
                v.tensor_tensor(rels[b][:, :, :],
                                order.cols[:, bass.ds(fl.tile(i, b), 2), REL:REL + 1].to_broadcast([R, 2, RELS]),
                                iota8[:, :].unsqueeze(1).to_broadcast([R, 2, RELS]),
                                ALU.is_equal).then_inc(fl.on["rels"], 1)

            def widen(j):
                def step(i, b):
                    if j == 0:
                        fl.masks(dve, i, b)
                    fl.wait(dve, "y", i, b)
                    fl.wait(dve, "rels", i, b)
                    fl.wait(dve, "total", i, b, back=1, per=2, part=j + 1)
                    v.tensor_tensor(wide[:, j, :].rearrange("p (r d) -> p r d", r=RELS),
                                    Y[b][:, j, :].unsqueeze(1).to_broadcast([R, RELS, D]),
                                    rels[b][:, j, :].unsqueeze(2).to_broadcast([R, RELS, D]),
                                    ALU.mult).then_inc(fl.on["wide"], 1)
                return step

            def reduce(j):
                def step(i, b):
                    fl.wait(dve, "bent", i, b, per=2, part=j + 1)
                    fl.wait(dve, "x2", i, b, back=fl.slots)
                    v.tensor_reduce(s[b][:, j, :], bent[:, j, :].rearrange("p (r d) -> p d r", r=RELS),
                                    AX.X, ALU.add).then_inc(fl.on["reduced"], 1)
                return step

            def sum2(i, b):
                c = fl.chain(dve, "v_sum2", i, b, 2)
                fl.wait(dve, "reduced", i, b, per=2, part=2)
                c.done(v.tensor_tensor(s[b][:, :, :], s[b][:, :, :], XD[b][:, :, :], ALU.add))
                dve.sem_inc(fl.on["summed"], 1)
                norm.moments(c, b, s[b]).then_inc(fl.on["mv"], 1)
                c.close()

            def sum3(i, b):
                c = fl.chain(dve, "v_sum3", i, b, 2)
                fl.wait(dve, "relu", i, b)
                c.done(v.tensor_tensor(s3[b][:, :, :], O2[b][:, :, D:], s3[b][:, :, :], ALU.add))
                dve.sem_inc(fl.on["summed3"], 1)
                norm.moments(c, b, s3[b]).then_inc(fl.on["mv3"], 1)
                c.close()

            fl.run(dve, {4: relations, 8: widen(0), 10: widen(1), 13: reduce(0), 15: reduce(1), 16: sum2,
                         20: norm.shift(dve), 27: sum3, 32: norm.shift(dve, "3")})
    fl.own.close()


def logits(k, order, rows_s, rows_d, scores):
    nc = k.nc
    fl = Edges(k, "l2a", order, 10)
    XS, XD = fl.each("xs", [R, 2, D]), fl.each("xd", [R, 2, D])
    prod = fl.each("prod", [R, 2, D])
    part, e = fl.each("part", [R, 2, 2]), fl.each("e", [R, 2, 2])
    rows_stored = [fl.sem(f"stored{b}") for b in range(fl.slots)]
    fl.sems("dotted")
    fl.gathers(slice(2, 4), ("dotted",), (k.x23h, XS, D), (k.x23h, XD, D))

    with nc.Block() as block:
        @block.gpsimd
        def _(pool):
            def gather(i, b):
                fl.arrived(pool, rows_stored[b], i, 64, before=1)
                fl.hold(pool)
                fl.gather(pool, i, b)

            fl.run(pool, {0: gather})
            fl.landed(pool)

        @block.sync
        def _(sp):
            def store(i, b):
                fl.gathered_all(sp, i, b)
                fl.hold(sp)
                for to, of in ((rows_s, XS), (rows_d, XD)):
                    halves(sp, to[bass.ds(fl.item(i, b), 1), :, :].rearrange("a p n -> (a p) n"),
                           of[b][:, :, :].rearrange("p q d -> p (q d)"), rows_stored[b])

            fl.run(sp, {5: store})
            for b in range(fl.slots):
                sp.wait_ge(rows_stored[b], fl.turns * 64)

        @block.vector
        def _(dve):
            v = nc.vector

            def dots(i, b):
                c = fl.chain(dve, "v_dots", i, b, 4)
                fl.gathered_all(dve, i, b)
                for n, (x, u) in enumerate(((XS, k.usB), (XD, k.udB))):
                    for j in range(2):
                        ins = v.tensor_tensor_reduce(out=prod[b][:, j, :], in0=x[b][:, j, :], in1=u[:, :],
                                                     scale=1.0, scalar=0.0, op0=ALU.mult, op1=ALU.add,
                                                     accum_out=part[b][:, n, j:j + 1])
                    c.done(ins)
                dve.sem_inc(fl.on["dotted"], 1)
                c.done(v.tensor_tensor(e[b][:, 0, :], part[b][:, 0, :], part[b][:, 1, :], ALU.add))
                c.done(v.scalar_tensor_tensor(e[b][:, 1, :], e[b][:, 0, :], k.logit0[:, :],
                                              order.cols[:, bass.ds(fl.tile(i, b), 2), LOGIT], ALU.add, ALU.add))
                v.scalar_tensor_tensor(scores[:, bass.ds(fl.tile(i, b), 2)], e[b][:, 1, :], SLOPE,
                                       e[b][:, 1, :], ALU.mult, ALU.max)
                c.close()

            fl.run(dve, {5: dots})
    fl.own.close()


def segment_softmax(k, table, key, scores, probs):
    nc = k.nc
    L = k.tiles
    LOW = -1e30
    s_d, p_d = k.dram("scores_edges", (1, k.E)), k.dram("probs_edges", (1, k.E))
    ends_d, carry_d = k.dram("row_ends", (P, 6)), k.dram("row_carries", (2, P))
    with ExitStack() as own:
        def sb(what, shape, dt=F32):
            return own.enter_context(nc.sbuf_tensor(f"smax_{what}", shape, dt))

        def sem(what):
            return k.semaphore((f"smax_{what}"))

        turned = sb("turned", [R, L, 1])
        keys3 = sb("keys3", [P, 3, L])
        e = sb("e", [P, L])
        pen = sb("pen", [P, 2, L])
        run = sb("run", [P, 2, L])
        own_end = sb("own_end", [P, 2, L])
        ends = sb("ends", [P, 6])
        rows = sb("rows", [1, 6, P])
        scan_in = sb("scan_in", [1, 2, 2, P])
        carries = sb("carries", [1, 2, P])
        carry = sb("carry", [P, 2])
        guard = sb("guard", [P, 1])
        both = sb("both", [P, 3, L])
        p = sb("p", [P, L])
        loaded, dma, steps, exped = sem("loaded"), sem("moved"), sem("steps"), sem("exped")
        asked = sem("asked")
        flat = s_d.rearrange("a (p l) -> (a p) l", p=P)

        with nc.Block() as block:
            @block.sync
            def _(sp):
                n = [0]

                def move(to, of, when):
                    sp.wait_ge(asked, when)
                    sp.dma_start(to, of, allow_slow_non_contiguous=True).then_inc(dma, 16)
                    n[0] += 16
                    sp.wait_ge(dma, n[0])

                for at in range(2):
                    sp.dma_start(keys3[:, at, :].unsqueeze(2),
                                 table[at:at + k.E, key:key + 1].rearrange("(p l) w -> p l w", p=P),
                                 allow_slow_non_contiguous=True).then_inc(loaded, 16)
                move(s_d.rearrange("a (t p) -> p t a", p=P), turned[1:R, :, :], 1)
                move(e[:, :], flat, 1)
                move(ends_d, ends[:, :], 2)
                move(rows[:, :, :], ends_d.rearrange("p (a c) -> a c p", a=1), 2)
                move(carry_d.rearrange("(a c) p -> a c p", a=1), carries[:, :, :], 3)
                move(carry[:, :], carry_d.rearrange("c p -> p c"), 3)
                sp.wait_ge(exped, 1)
                move(p_d.rearrange("a (p l) -> (a p) l", p=P), p[:, :], 3)
                move(turned[1:R, :, :], p_d.rearrange("a (t p) -> p t a", p=P), 3)

            @block.scalar
            def _(act):
                act.wait_ge(asked, 4)
                nc.scalar.activation(p[:, :], both[:, 2, :], ACT.Exp).then_inc(exped, 1)

            @block.vector
            def _(dve):
                v = nc.vector
                c = Chain(dve, steps)
                c.done(v.tensor_copy(turned[:, :, 0], scores[:, ::-1]))
                dve.sem_inc(asked, 1)
                dve.wait_ge(loaded, 32)
                v.memset(keys3[:, 2, L - 1:], -2.0)
                c.done(v.tensor_copy(keys3[:, 2, 0:L - 1], keys3[:, 1, 1:L]))
                for w, at in ((0, 0), (1, 2)):
                    c.done(v.tensor_tensor(pen[:, w, :], keys3[:, at, :], keys3[:, 1, :], ALU.is_equal))
                    edge = keys3[:, 1, 0:1] if w == 0 else keys3[:, 1, L - 1:L]
                    c.done(v.tensor_scalar(own_end[:, w, :], keys3[:, 1, :], edge, None, ALU.is_equal))
                c.done(v.tensor_copy(ends[:, 4:5], pen[:, 0, 0:1]))
                c.done(v.tensor_copy(ends[:, 2:3], own_end[:, 0, L - 1:L]))
                for x in (pen, own_end):
                    c.done(v.tensor_scalar(x[:, :, :], x[:, :, :], -1.0, -LOW, ALU.add, ALU.mult))
                dve.wait_ge(dma, 32)
                v.tensor_tensor_scan(run[:, 0, :], pen[:, 0, :], e[:, :], LOW, ALU.add, ALU.max)
                c.done(v.tensor_tensor_scan(run[:, 1, ::-1], pen[:, 1, ::-1], e[:, ::-1], LOW, ALU.add, ALU.max))
                v.tensor_copy(ends[:, 0:1], run[:, 0, L - 1:L])
                v.tensor_copy(ends[:, 1:2], run[:, 1, 0:1])
                v.memset(ends[:, 3:4], 0.0)
                c.done(v.memset(ends[:, 5:6], 0.0))
                dve.sem_inc(asked, 1)
                dve.wait_ge(dma, 64)
                c.done(v.memset(scan_in[:, :, :, :], LOW))
                c.done(v.tensor_scalar(rows[:, 2, :], rows[:, 2, :], -1.0, -LOW, ALU.add, ALU.mult))
                c.done(v.tensor_scalar(rows[:, 4, :], rows[:, 4, :], -1.0, -LOW, ALU.add, ALU.mult))
                for m, x in enumerate((rows[:, 2, :], rows[:, 0, :])):
                    c.done(v.tensor_tensor(scan_in[:, 0, m, 1:], x[:, 0:P - 1], rows[:, 4, 1:], ALU.add))
                for m, x in enumerate((rows[:, 2, :], rows[:, 1, :])):
                    c.done(v.tensor_tensor(scan_in[:, 1, m, 0:P - 1], x[:, 1:], rows[:, 4, 1:], ALU.add))
                v.tensor_tensor_scan(carries[:, 0, :], scan_in[:, 0, 0, :], scan_in[:, 0, 1, :], LOW, ALU.add, ALU.max)
                c.done(v.tensor_tensor_scan(carries[:, 1, ::-1], scan_in[:, 1, 0, ::-1], scan_in[:, 1, 1, ::-1], LOW,
                                            ALU.add, ALU.max))
                dve.sem_inc(asked, 1)
                dve.wait_ge(dma, 96)
                c.done(v.scalar_tensor_tensor(both[:, 0, :], own_end[:, 0, :], carry[:, 0:1], run[:, 0, :],
                                              ALU.add, ALU.max))
                c.done(v.scalar_tensor_tensor(both[:, 1, :], own_end[:, 1, :], carry[:, 1:2], run[:, 1, :],
                                              ALU.add, ALU.max))
                c.done(v.tensor_tensor(both[:, 0, :], both[:, 0, :], both[:, 1, :], ALU.max))
                c.done(v.tensor_tensor(both[:, 2, :], e[:, :], both[:, 0, :], ALU.subtract))
                dve.sem_inc(asked, 1)
                dve.wait_ge(dma, 128)
                v.tensor_copy(probs[:, :], turned[:, ::-1, 0])


def layer2(k, order, rows_s, rows_d, probs):
    nc = k.nc
    fl = Edges(k, "l2b", order, 30)
    W = D + 1
    XS, XD, z, x3, x4 = (fl.each(n, [R, 2, D]) for n in ("xs", "xd", "z", "x3", "x4"))
    s = s4 = z
    V = fl.each("v", [R, 2, D + 4])
    zT = fl.each("zT", [D, 2, R], copies=2)
    den = fl.each("den", [R, 2])
    norm = fl.norms(R, 2)
    T, O, tot = fl.ps("T", [D, 4, D], 2), fl.ps("O", [R, 2, 2 * D], 2), fl.ps("tot", [R, 2, 2 * D], 2)
    rows_loaded = [fl.sem(f"loaded{b}") for b in range(fl.slots)]
    fl.segments(W)
    fl.sems("weighted", "totals_used", "z", "t", "c", "o", "relu", "taken", "summed", "mv", "std", "nm", "x3", "mv4", "std4", "nm4", "x4")
    fl.scatters((k.x23h, x3, D, "x3", 1), (k.arg["out"], x4, D, "x4", 0))

    with nc.Block() as block:
        @block.gpsimd
        def _(pool):
            fl.run(pool, {21: lambda i, b: fl.scatter(pool, 0, i, b), 25: lambda i, b: fl.scatter(pool, 1, i, b)})
            fl.landed(pool)

        @block.sync
        def _(sp):
            def load(i, b):
                fl.wait(sp, "summed", i, b, back=fl.slots)
                fl.hold(sp)
                for to, of in ((XS, rows_s), (XD, rows_d)):
                    halves(sp, to[b][:, :, :].rearrange("p q d -> p (q d)"),
                           of[bass.ds(fl.item(i, b), 1), :, :].rearrange("a p n -> (a p) n"), rows_loaded[b])

            fl.run(sp, {0: load})

        @block.tensor
        def _(pe):
            def totals(i, b):
                fl.wait(pe, "weighted", i, b)
                fl.wait(pe, "totals_used", i, b, back=2)
                fl.totals(pe, i, b, lambda j: tot[b][:, j, 0:W], lambda j: V[b][:, j, 0:W])

            def transpose(i, b):
                fl.wait(pe, "z", i, b)
                fl.wait(pe, "c", i, b, back=2)
                transpose_tiles(k, T[b], z[b]).then_inc(fl.on["t"], 1)

            def project(i, b):
                fl.wait(pe, "c", i, b)
                fl.wait(pe, "taken", i, b, back=2)
                project_pair(k, O[b], zT[b], k.W2edge, k.bias2e).then_inc(fl.on["o"], 1)

            fl.run(pe, {11: totals, 13: transpose, 15: project})

        @block.scalar
        def _(act):
            a = nc.scalar

            def weigh(i, b):
                fl.arrived(act, rows_loaded[b], i, 64)
                fl.wait(act, "total", i, b, back=fl.slots, per=2, part=2)
                for j in range(2):
                    prob = probs[:, bass.ds(fl.tile(i, b) + j, 1)]
                    a.activation(V[b][:, j, 0:D], XD[b][:, j, :], ACT.Copy, scale=prob)
                a.activation(V[b][:, :, D], probs[:, bass.ds(fl.tile(i, b), 2)], ACT.Copy).then_inc(fl.on["weighted"], 1)

            def carry(i, b):
                fl.carry(act, i, b, V, tot, lambda ni, nb: fl.wait(act, "weighted", ni, nb))

            def copy(i, b):
                fl.wait(act, "t", i, b)
                fl.wait(act, "o", i, b, back=2)
                a.activation(zT[b][:, :, :], T[b][:, 0:2, 0:R], ACT.Copy).then_inc(fl.on["c"], 1)

            def relu(i, b):
                fl.wait(act, "o", i, b)
                fl.wait(act, "x3", i, b, back=fl.slots)
                a.activation(s[b][:, :, :], O[b][:, :, 0:D], ACT.Relu).then_inc(fl.on["relu"], 1)

            def norm3(i, b):
                fl.wait(act, "nm", i, b)
                fl.scattered_before(act, 0, i, b)
                normalise(k, x3[b], s[b], norm.rs[b], norm.nm[b]).then_inc(fl.on["x3"], 1)

            def norm4(i, b):
                fl.wait(act, "nm4", i, b)
                fl.scattered_before(act, 1, i, b)
                normalise(k, x4[b], s4[b], norm.rs[b], norm.nm[b]).then_inc(fl.on["x4"], 1)

            fl.run(act, {2: weigh, 11: carry, 14: copy, 16: relu, 18: norm.root(act), 20: norm3, 22: norm.root(act, "4"),
                         24: norm4})

        @block.vector
        def _(dve):
            v = nc.vector

            def attend(i, b):
                c = fl.chain(dve, "v_attend", i, b, 3)
                fl.carried(dve, i, b)
                c.done(v.tensor_scalar(den[b][:, :], tot[b][:, :, D], 1e-30, None, ALU.max))
                c.done(v.reciprocal(den[b][:, :], den[b][:, :]))
                c.done(v.tensor_tensor(z[b][:, :, :], tot[b][:, :, 0:D], den[b][:, :].unsqueeze(2).to_broadcast([R, 2, D]),
                                       ALU.mult))
                dve.sem_inc(fl.on["totals_used"], 1)
                v.tensor_tensor(z[b][:, :, :], z[b][:, :, :], XS[b][:, :, :], ALU.add).then_inc(fl.on["z"], 1)

            def sum3(i, b):
                c = fl.chain(dve, "v_sum3", i, b, 3)
                fl.wait(dve, "relu", i, b)
                c.done(v.tensor_tensor(s[b][:, :, :], O[b][:, :, D:], s[b][:, :, :], ALU.add))
                dve.sem_inc(fl.on["taken"], 1)
                c.done(v.tensor_tensor(s[b][:, :, :], s[b][:, :, :], XS[b][:, :, :], ALU.add))
                dve.sem_inc(fl.on["summed"], 1)
                norm.moments(c, b, s[b]).then_inc(fl.on["mv"], 1)
                c.close()

            def sum4(i, b):
                c = fl.chain(dve, "v_sum4", i, b, 2)
                fl.wait(dve, "x3", i, b)
                c.done(v.tensor_tensor(s4[b][:, :, :], x3[b][:, :, :], k.sig2B[:, :].unsqueeze(1).to_broadcast([R, 2, D]),
                                       ALU.add))
                norm.moments(c, b, s4[b]).then_inc(fl.on["mv4"], 1)
                c.close()

            fl.run(dve, {10: lambda i, b: fl.masks(dve, i, b), 12: attend, 17: sum3, 19: norm.shift(dve),
                         21: sum4, 23: norm.shift(dve, "4")})
    fl.own.close()


def layer3(k, order, last):
    nc = k.nc
    fl = Edges(k, f"l3{'b' if last else 'a'}", order, 30)
    W, to_width = (HID, D) if last else (D, HID)
    XS, V, A = (fl.each(n, [R, 2, W]) for n in ("xs", "v", "a"))
    XD, s, x4 = (fl.each(n, [R, 2, D]) for n in ("xd", "s", "x4"))
    y = fl.each("y", [R, 2, to_width])
    AT = fl.each("aT", [W, 2, R], copies=2)
    norm = fl.norms(R, 2)
    T, O, tot = fl.ps("T", [W, 4, D], 2), fl.ps("O", [R, 4, D], 2), fl.ps("tot", [R, 4, D], 2)
    weights, bias = (k.w2, k.b2r) if last else (k.w1, k.b1r)
    fl.segments(W)
    fl.sems("weighted", "a", "totals_used", "t", "c", "o", "y", "summed", "mv", "std", "nm", "x4")
    if last:
        fl.gathers(slice(0, 6, 5), ("weighted", "summed"), (k.h1, XS, HID), (k.x23h, XD, D))
        fl.scatters((k.arg["out"], x4, D, "x4", 0))
    else:
        fl.gathers(slice(4, 5), ("weighted",), (k.x23h, XS, D))
        fl.scatters((k.h1, y, HID, "y", 0))

    with nc.Block() as block:
        @block.gpsimd
        def _(pool):
            fl.run(pool, {0: lambda i, b: fl.gather(pool, i, b),
                          21 if last else 17: lambda i, b: fl.scatter(pool, 0, i, b)})
            fl.landed(pool)

        @block.tensor
        def _(pe):
            t = nc.tensor

            def totals(i, b):
                fl.wait(pe, "weighted", i, b)
                fl.wait(pe, "totals_used", i, b, back=2)
                fl.totals(pe, i, b, lambda j: tot[b][:, j, 0:W], lambda j: V[b][:, j, :])

            def transpose(i, b):
                fl.wait(pe, "a", i, b)
                fl.wait(pe, "c", i, b, back=2)
                fl.hold(pe)
                transpose_tiles(k, T[b], A[b]).then_inc(fl.on["t"], 1)

            def project(i, b):
                fl.wait(pe, "c", i, b)
                fl.wait(pe, "y", i, b, back=2)
                t.matmul(O[b][:, 0:2, 0:to_width], k.ones_row[:, 0:R],
                         bias[:, 0:2 * to_width].rearrange("a (q d) -> a q d", q=2), start=True, stop=False,
                         skip_group_check=True)
                for j in range(2):
                    ins = t.matmul(O[b][:, j, 0:to_width], AT[b][:, j, :], weights[:, :], start=False, stop=True,
                                   skip_group_check=True)
                ins.then_inc(fl.on["o"], 1)

            fl.run(pe, {11: totals, 13: transpose, 15: project})

        @block.scalar
        def _(act):
            a = nc.scalar

            def weigh(i, b):
                fl.gathered_all(act, i, b)
                fl.wait(act, "total", i, b, back=fl.slots, per=2, part=2)
                for j in range(2):
                    ins = a.activation(V[b][:, j, :], XS[b][:, j, :], ACT.Copy,
                                       scale=order.cols[:, bass.ds(fl.tile(i, b) + j, 1), WEIGHT])
                ins.then_inc(fl.on["weighted"], 1)

            def carry(i, b):
                fl.carry(act, i, b, V, tot, lambda ni, nb: fl.wait(act, "weighted", ni, nb))

            def copy(i, b):
                fl.wait(act, "t", i, b)
                fl.wait(act, "o", i, b, back=2)
                a.activation(AT[b][:, :, :], T[b][:, 0:2, 0:R], ACT.Copy).then_inc(fl.on["c"], 1)

            def bend(i, b):
                fl.wait(act, "o", i, b)
                if last:
                    fl.wait(act, "summed", i, b, back=fl.slots)
                else:
                    fl.scattered_before(act, 0, i, b)
                a.activation(y[b][:, :, :], O[b][:, 0:2, 0:to_width], ACT.Sigmoid).then_inc(fl.on["y"], 1)

            def norm4(i, b):
                fl.wait(act, "nm", i, b)
                fl.scattered_before(act, 0, i, b)
                normalise(k, x4[b], s[b], norm.rs[b], norm.nm[b]).then_inc(fl.on["x4"], 1)

            steps = {4: weigh, 11: carry, 14: copy, 16: bend}
            if last:
                steps[18], steps[20] = norm.root(act), norm4
            fl.run(act, steps)

        @block.vector
        def _(dve):
            v = nc.vector

            def take(i, b):
                fl.carried(dve, i, b)
                fl.wait(dve, "t", i, b, back=fl.slots)
                v.tensor_copy(A[b][:, :, :], tot[b][:, 0:2, 0:W]).then_inc(fl.on["a"], 1)
                fl.wait(dve, "a", i, b)
                dve.sem_inc(fl.on["totals_used"], 1)

            def sum4(i, b):
                c = fl.chain(dve, "v_sum4", i, b, 2)
                fl.wait(dve, "y", i, b)
                fl.gathered_all(dve, i, b)
                fl.wait(dve, "x4", i, b, back=fl.slots)
                c.done(v.tensor_tensor(s[b][:, :, :], XD[b][:, :, :], y[b][:, :, :], ALU.add))
                dve.sem_inc(fl.on["summed"], 1)
                norm.moments(c, b, s[b]).then_inc(fl.on["mv"], 1)
                c.close()

            steps = {10: lambda i, b: fl.masks(dve, i, b), 12: take}
            if last:
                steps[17], steps[19] = sum4, norm.shift(dve)
            fl.run(dve, steps)
    fl.own.close()


def program(nc, args, n_nodes, n_edges, upto=99, probe=None):
    with ExitStack() as ctx:
        k = Kernel(nc, ctx, args, n_nodes, n_edges)
        k.by_src1 = k.dram("by_src_low", (k.E + 1, COLS))
        k.by_dst1 = k.dram("by_dst_low", (k.E + 1, COLS))
        k.by_src = k.dram("by_src", (k.E + 1, COLS)) if probe is None else probe["by_src"]
        k.by_dst = k.dram("by_dst", (k.E + 1, COLS)) if probe is None else probe["by_dst"]
        prepare(k)
        k.recycle()
        edge_table(k)
        k.recycle()
        radix_pass(k, "src_low", 0, None, 0, k.by_src1)
        k.recycle()
        radix_pass(k, "src_high", 1, k.by_src1, SRC, k.by_src)
        k.recycle()
        radix_pass(k, "dst_low", 2, None, 1, k.by_dst1)
        k.recycle()
        radix_pass(k, "dst_high", 3, k.by_dst1, DST, k.by_dst)
        k.recycle()
        k.sorting.close()

        k.x1, k.x23 = k.dram("x1_nodes", (k.N, D)), k.dram("x2_x3_nodes", (k.N, 2 * D))
        k.h1 = k.dram("h1_nodes", (k.N, HID))
        if probe:
            k.x1, k.x23, k.h1 = probe["x1"], probe["x23"], probe["h1"]
        k.x23h = k.x23.rearrange("n (h d) -> (n h) d", h=2)
        dense(k)
        k.recycle()

        k.scores = k.sb("scores", [R, k.tiles])
        k.probs = k.sb("probs", [R, k.tiles])
        dst = Order(k, "dst", k.by_dst, DST)
        k.recycle()
        layer0(k, dst)
        k.recycle()
        layer1(k, dst)
        k.recycle()
        dst.own.close()
        rows_s = k.dram("x2_of_src", (k.tiles // 2, R, 2 * D))
        rows_d = k.dram("x2_of_dst", (k.tiles // 2, R, 2 * D))
        src = Order(k, "src", k.by_src, SRC)
        k.recycle()
        logits(k, src, rows_s, rows_d, k.scores)
        k.recycle()
        segment_softmax(k, k.by_src, SRC, k.scores, k.probs)
        k.recycle()
        layer2(k, src, rows_s, rows_d, k.probs)
        k.recycle()
        src.own.close()
        again = Order(k, "dst_again", k.by_dst, DST)
        k.recycle()
        layer3(k, again, False)
        k.recycle()
        layer3(k, again, True)
        k.recycle()
        again.own.close()


_INS = ["x", "src", "dst", "edge_attr_128", "edge_type_8", "edge_weight",
        "L0_gnn_W", "L0_gnn_b", "L0_gnn_gamma", "L0_gnn_beta",
        "L1_gnn_rel_emb", "L1_gnn_W", "L1_gnn_b",
        "L2_gnn_W_node", "L2_gnn_b_node", "L2_gnn_W_edge", "L2_gnn_b_edge",
        "L3_gnn_w1", "L3_gnn_b1", "L3_gnn_w2", "L3_gnn_b2"]


def kernel(**inputs):
    import numpy as _np
    import concourse.bacc as _bacc
    from concourse import mybir as _mybir
    from concourse.bass_utils import run_bass_kernel_spmd as _run

    nc = _bacc.Bacc("TRN2", target_bir_lowering=False, num_devices=1)
    arrays, args = {}, {}
    for name in _INS:
        a = _np.ascontiguousarray(inputs[name])
        arrays[f"in_{name}"] = a
        args[name] = nc.dram_tensor(f"in_{name}", a.shape, _mybir.dt.from_np(a.dtype), kind="ExternalInput").ap()
    n_nodes, features = inputs["x"].shape
    args["out"] = nc.dram_tensor("out", (n_nodes, features), _mybir.dt.float32, kind="ExternalOutput").ap()
    program(nc, args, n_nodes, inputs["src"].shape[0])
    r = _run(nc, [arrays], core_ids=[0])
    return r.results[0]["out"]
```

```python
import concourse.bass as bass
from concourse import mybir
from contextlib import ExitStack

F32 = mybir.dt.float32
BF16 = mybir.dt.bfloat16
FP16 = mybir.dt.float16
I32 = mybir.dt.int32
ALU = mybir.AluOpType
ACT = mybir.ActivationFunctionType
AX = mybir.AxisListType

P = 125
R = P + 1
K = 8
Q = 4
D = 128
HID = 64
RELS = 8
LOW_BITS = 9
BINS = 1 << LOW_BITS
EPS = 1e-5
SLOPE = 0.2
FAR = 1 << 20
COLS = 8
SRC, DST, REL, WEIGHT, LOGIT = range(5)


class Chain:

    def __init__(self, engine, sem, turn=0, steps=0, before=0, held=None):
        self.engine, self.sem, self.base, self.steps, self.n = engine, sem, turn * steps + before, steps, 0
        self.held = held

    def done(self, instruction):
        instruction.then_inc(self.sem, 1)
        self.n += 1
        self.engine.wait_ge(self.sem, self.base + self.n)

    def hold(self):
        self.engine.sem_inc(self.held, 1)

    def close(self):
        assert self.n == self.steps, (self.n, self.steps)


class Queue:

    def __init__(self, sem):
        self.sem, self.before, self.added = sem, 0, 0


class Kernel:

    def __init__(self, nc, ctx, args, n_nodes, n_edges):
        self.nc, self.ctx = nc, ctx
        self.N, self.E = n_nodes, n_edges
        self.sorting = ExitStack()
        self.in_use, self.free, self.queues = [], {"dma": [], "steps": []}, {}
        self.tiles = n_edges // P
        self.turns = self.tiles // K
        assert n_edges % (P * K) == 0 and n_nodes % (P * K) == 0
        self.groups = n_nodes // (P * K)
        self.arg = args

    def sb(self, name, shape, dt=F32):
        return self.ctx.enter_context(self.nc.sbuf_tensor(name, shape, dt))

    def sort_sb(self, name, shape, dt=F32):
        return self.sorting.enter_context(self.nc.sbuf_tensor(name, shape, dt))

    def semaphore(self, name):
        if any(x in name for x in ("loaded", "stored", "moved")):
            kind = "dma"
        else:
            kind = "steps"
        free = self.free[kind]
        s = free.pop(0) if free else self.nc.alloc_semaphore(name)
        self.in_use.append((kind, s))
        return s

    def queue(self, name, added):
        if name not in self.queues:
            self.queues[name] = Queue(self.nc.alloc_semaphore(name))
        q = self.queues[name]
        q.before, q.added = q.before + q.added, added
        return q

    def recycle(self):
        with self.nc.Block() as block:
            @block.gpsimd
            def _(pool):
                for _, s in self.in_use:
                    pool.sem_clear(s)
        for kind, s in self.in_use:
            self.free[kind].append(s)
        self.in_use = []

    def dram(self, name, shape, dt=F32):
        return self.nc.dram_tensor(name, shape, dt, kind="Internal").ap()


def row(ap):
    return ap.rearrange("(a n) -> a n", a=1)


def column(ap):
    return ap.rearrange("(n a) -> n a", a=1)


def over(ap, partitions):
    return row(ap).to_broadcast([partitions, ap.shape[0]])


def prepare(k):
    nc = k.nc
    k.ident = k.sb("ident", [D, D])
    k.ones_row = k.sb("ones_row", [1, 512])
    k.ones3 = k.sb("ones3", [3, R], BF16)
    k.eps1 = k.sb("eps1", [D, 1])
    k.eps2 = k.sb("eps2", [D, 1])
    k.W0cat = k.sb("W0cat", [D, 2 * D])
    k.bias0 = k.sb("bias0", [3, 2, 2 * D], BF16)
    k.betaB = k.sb("betaB", [R, D])
    k.sig2B = k.sb("sig2B", [R, D])
    k.sig1B = k.sb("sig1B", [P, K * HID])
    k.W2cat = k.sb("W2cat", [D, 2 * D])
    k.W2edge = k.sb("W2edge", [D, 2 * D])
    k.bias2 = k.sb("bias2", [3, 2, 2 * D], BF16)
    k.bias2e = k.sb("bias2e", [3, 2, 2 * D], BF16)
    k.WeB = k.sb("WeB", [P, D])
    k.usB = k.sb("usB", [R, D])
    k.udB = k.sb("udB", [R, D])
    k.logit0 = k.sb("logit0", [R, 1])
    k.W1aT = k.sb("W1aT", [D, D])
    k.W1bT = k.sb("W1bT", [D, D])
    k.relC = k.sb("relC", [RELS, D])
    k.w1 = k.sb("w1", [D, HID])
    k.w2 = k.sb("w2", [HID, D])
    k.b1r = k.sb("b1r", [1, Q * HID])
    k.b2r = k.sb("b2r", [1, Q * D])
    with ExitStack() as own:
        def sb(name, shape, dt=F32):
            return own.enter_context(nc.sbuf_tensor(name, shape, dt))

        def sem(name):
            return k.semaphore((name))

        W0 = sb("W0", [D, D])
        W1 = sb("W1", [D, 2 * D + HID])
        Wn = sb("Wn", [D, D])
        WnT = sb("WnT", [D, D])
        W1cT = sb("W1cT", [HID, D])
        emb = sb("emb", [RELS, HID])
        embT = sb("embT", [HID, RELS])
        gammaB = sb("gammaB", [D, D])
        b0 = sb("b0", [1, D])
        bn = sb("bn", [1, D])
        bncol = sb("bncol", [D, 1])
        b1e = sb("b1e", [1, D])
        wsd = sb("wsd", [D, 3])
        wsB = sb("wsB", [D, 3, R])
        bedge = sb("bedge", [R, 1])
        b2B = sb("b2B", [R, D])
        b1B = sb("b1B", [P, HID])
        W0T = sb("W0T", [D, D])
        mean = sb("mean", [D, 2])
        biasrow = sb("biasrow", [1, 3, 2, 2 * D])
        rest = sb("rest", [1, 2 * D])
        parts = sb("parts", [1, 3, 3, 2, 2 * D], BF16)
        b12 = sb("b12", [1, HID + D])
        ps = own.enter_context(nc.psum_tensor("ps", [D, 8, 512], F32))

        loaded = sem("weights_loaded")
        moved = sem("bias_rows_moved")
        ident_set = sem("ident_set")
        steps = sem("prepare_steps")
        cols_spread = sem("cols_spread")
        transposed = sem("weights_transposed")
        copied = sem("weights_copied")
        multiplied = sem("weights_multiplied")
        sigmoids = sem("sigmoids")
        LOADS = 20

        with nc.Block() as block:
            @block.sync
            def _(sp):
                n = 0
                for to, of in [
                    (W0[:, :], k.arg["L0_gnn_W"]), (W1[:, :], k.arg["L1_gnn_W"]), (Wn[:, :], k.arg["L2_gnn_W_node"]),
                    (emb[:, :], k.arg["L1_gnn_rel_emb"]), (gammaB[:, :], over(k.arg["L0_gnn_gamma"], D)),
                    (k.betaB[:, :], over(k.arg["L0_gnn_beta"], R)), (b0[:, :], row(k.arg["L0_gnn_b"])),
                    (bn[:, :], row(k.arg["L2_gnn_b_node"])), (bncol[:, :], column(k.arg["L2_gnn_b_node"])),
                    (b1e[:, :], row(k.arg["L1_gnn_b"])),
                    (k.WeB[:, :], over(k.arg["L2_gnn_W_edge"].rearrange("n a -> (n a)")[0:D], P)),
                    (wsd[:, 0:1], k.arg["L2_gnn_W_edge"][D:2 * D, :]), (wsd[:, 1:2], k.arg["L2_gnn_W_edge"][2 * D:3 * D, :]),
                    (bedge[:, :], over(k.arg["L2_gnn_b_edge"], R)), (b2B[:, :], over(k.arg["L3_gnn_b2"], R)),
                    (b1B[:, :], over(k.arg["L3_gnn_b1"], P)), (k.w1[:, :], k.arg["L3_gnn_w1"]), (k.w2[:, :], k.arg["L3_gnn_w2"]),
                    (b12[:, 0:HID], row(k.arg["L3_gnn_b1"])), (b12[:, HID:], row(k.arg["L3_gnn_b2"])),
                ]:
                    sp.dma_start(to, of).then_inc(loaded, 16)
                    n += 1
                assert n == LOADS
                sp.wait_ge(copied, 4)
                for m, to in enumerate((k.bias0, k.bias2, k.bias2e)):
                    sp.dma_start(to[:, :, :], parts[:, m, :, :, :]).then_inc(moved, 16)
                sp.wait_ge(moved, 48)

            @block.gpsimd
            def _(pool):
                nc.gpsimd.memset(k.ident[:, :], 0.0).then_inc(ident_set, 1)
                pool.wait_ge(ident_set, 1)
                nc.gpsimd.affine_select(out=k.ident[:, :], in_=k.ident[:, :], compare_op=ALU.not_equal, fill=1.0,
                                        base=0, pattern=[[-1, D]], channel_multiplier=1).then_inc(ident_set, 1)

            @block.scalar
            def _(act):
                act.wait_ge(loaded, 16 * LOADS)
                nc.scalar.activation(k.sig2B[:, :], b2B[:, :], ACT.Sigmoid)
                for j in range(K):
                    nc.scalar.activation(k.sig1B[:, j * HID:(j + 1) * HID], b1B[:, :], ACT.Sigmoid).then_inc(sigmoids, 1)

            @block.tensor
            def _(pe):
                pe.wait_ge(loaded, 16 * LOADS)
                pe.wait_ge(ident_set, 2)
                nc.tensor.transpose(ps[:, 0, 0:D], W0[:, :], k.ident[:, :])
                nc.tensor.transpose(ps[:, 1, 0:D], W1[:, 0:D], k.ident[:, :])
                nc.tensor.transpose(ps[:, 2, 0:D], W1[:, D:2 * D], k.ident[:, :])
                nc.tensor.transpose(ps[0:HID, 3, 0:D], W1[:, 2 * D:], k.ident[:, :])
                nc.tensor.transpose(ps[0:HID, 4, 0:RELS], emb[:, :], k.ident[0:RELS, 0:RELS])
                nc.tensor.transpose(ps[:, 5, 0:D], Wn[:, :], k.ident[:, :]).then_inc(transposed, 1)
                pe.wait_ge(copied, 1)
                nc.tensor.matmul(ps[0:RELS, 0, 0:D], embT[:, :], W1cT[:, :], start=True, stop=False)
                nc.tensor.matmul(ps[0:RELS, 0, 0:D], k.ones_row[:, 0:RELS], b1e[:, :], start=False, stop=True)
                pe.wait_ge(cols_spread, 1)
                nc.tensor.matmul(ps[0:R, 1, 0:D], wsB[:, 0, :], WnT[:, :], start=True, stop=True)
                nc.tensor.matmul(ps[0:R, 2, 0:D], wsB[:, 1, :], WnT[:, :], start=True, stop=True)
                nc.tensor.matmul(ps[0:R, 3, 0:1], wsB[:, 2, :], bncol[:, :], start=True, stop=True).then_inc(multiplied, 1)

            @block.vector
            def _(dve):
                v = nc.vector
                c = Chain(dve, steps)
                dve.wait_ge(loaded, 16 * LOADS)
                v.memset(k.ones_row[:, :], 1.0)
                v.memset(k.ones3[:, :], 1.0)
                v.memset(k.eps1[:, :], EPS)
                v.memset(k.eps2[:, :], EPS * EPS)
                c.done(v.tensor_tensor(wsd[:, 2:3], wsd[:, 0:1], wsd[:, 1:2], ALU.add))
                v.tensor_scalar(wsB[:, :, :], wsd[:, :].unsqueeze(2).to_broadcast([D, 3, R]), 1.0, None,
                                ALU.mult).then_inc(cols_spread, 1)
                dve.wait_ge(transposed, 1)
                v.tensor_copy(k.W1aT[:, :], ps[:, 1, 0:D])
                v.tensor_copy(k.W1bT[:, :], ps[:, 2, 0:D])
                v.tensor_copy(W1cT[:, :], ps[0:HID, 3, 0:D])
                v.tensor_copy(embT[:, :], ps[0:HID, 4, 0:RELS])
                v.tensor_copy(WnT[:, :], ps[:, 5, 0:D])
                c.done(v.tensor_copy(W0T[:, :], ps[:, 0, 0:D]))
                v.tensor_reduce(mean[:, 0:1], W0T[:, :], AX.X, ALU.add)
                c.done(v.tensor_reduce(mean[0:1, 1:2], b0[:, :], AX.X, ALU.add))
                c.done(v.tensor_scalar(mean[:, 0:1], mean[:, 0:1], 1.0 / D, None, ALU.mult))
                c.done(v.tensor_scalar(mean[0:1, 1:2], mean[0:1, 1:2], 1.0 / D, None, ALU.mult))
                v.tensor_scalar(k.W0cat[:, 0:D], W0T[:, :], mean[:, 0:1], None, ALU.subtract).then_inc(copied, 1)
                dve.wait_ge(copied, 1)
                v.tensor_tensor(k.W0cat[:, D:], k.W0cat[:, 0:D], gammaB[:, :], ALU.mult)
                c.done(v.tensor_scalar(biasrow[:, 0, 0, 0:D], b0[:, :], mean[0:1, 1:2], None, ALU.subtract))
                v.tensor_tensor(biasrow[:, 0, 0, D:], biasrow[:, 0, 0, 0:D], gammaB[0:1, :], ALU.mult)
                v.tensor_scalar(biasrow[:, 1, 0, 0:D], bn[:, :], 1 - SLOPE, None, ALU.mult)
                v.tensor_scalar(biasrow[:, 1, 0, D:], bn[:, :], SLOPE, None, ALU.mult)
                v.tensor_scalar(biasrow[:, 2, 0, 0:D], bn[:, :], 2 * (1 - SLOPE), None, ALU.mult)
                v.tensor_scalar(biasrow[:, 2, 0, D:], bn[:, :], 2 * SLOPE, None, ALU.mult)
                v.tensor_scalar(k.W2cat[:, 0:D], Wn[:, :], 1 - SLOPE, None, ALU.mult)
                v.tensor_scalar(k.W2edge[:, 0:D], Wn[:, :], 1 - SLOPE, None, ALU.mult)
                c.done(v.tensor_scalar(k.W2edge[:, D:], Wn[:, :], SLOPE, None, ALU.mult))
                dve.wait_ge(ident_set, 2)
                c.done(v.tensor_tensor(k.W2cat[:, D:], k.W2edge[:, D:], k.ident[:, :], ALU.add))
                for m in range(3):
                    b = biasrow[:, m, 0, :]
                    c.done(v.tensor_copy(rest[:, :], b))
                    for part in range(3):
                        c.done(v.tensor_copy(parts[:, m, part, 0, :], rest[:, :]))
                        c.done(v.tensor_tensor(rest[:, :], rest[:, :], parts[:, m, part, 0, :], ALU.subtract))
                        c.done(v.tensor_copy(parts[:, m, part, 1, :], parts[:, m, part, 0, :]))
                    dve.sem_inc(copied, 1)
                for j in range(Q):
                    v.tensor_copy(k.b1r[:, j * HID:(j + 1) * HID], b12[:, 0:HID])
                    v.tensor_copy(k.b2r[:, j * D:(j + 1) * D], b12[:, HID:])
                dve.wait_ge(multiplied, 1)
                v.tensor_copy(k.relC[:, :], ps[0:RELS, 0, 0:D])
                v.tensor_copy(k.usB[:, :], ps[0:R, 1, 0:D])
                v.tensor_copy(k.udB[:, :], ps[0:R, 2, 0:D])
                v.tensor_tensor(k.logit0[:, :], ps[0:R, 3, 0:1], bedge[:, :], ALU.add)


def edge_table(k):
    nc = k.nc
    k.edges = k.sort_sb("edges", [P, k.tiles, COLS])
    k.digits = k.sort_sb("digits", [P, 2, k.tiles])
    k.bins = k.sort_sb("bins", [P, BINS], FP16)
    k.below = k.sort_sb("below", [P, 3, P], BF16)
    k.base = k.sort_sb("base", [1, 4, BINS])
    with ExitStack() as own:
        def sb(name, shape, dt=F32):
            return own.enter_context(nc.sbuf_tensor(name, shape, dt))

        def sem(name):
            return k.semaphore((name))

        raw = sb("raw", [P, 3, k.tiles], I32)
        split = sb("split", [P, 2, 2, k.tiles], I32)
        dig = sb("dig", [P, 4, k.tiles])
        weight = sb("weight", [P, k.tiles])
        attr = sb("attr", [P, k.tiles, D])
        prod = sb("prod", [P, K, D])
        dot = sb("dot", [P, K])
        onehot = sb("onehot", [P, 8, BINS], BF16)
        ones_col = sb("ones_col", [P, 1], BF16)
        ones_bins = sb("ones_bins", [1, BINS])
        seen = sb("seen", [1, 4, BINS])
        guard = sb("guard", [1, COLS])
        count = own.enter_context(nc.psum_tensor("count", [1, 4, 512], F32))
        loaded = sem("edges_loaded")
        CHUNKS = 5
        turns = [k.turns * n // CHUNKS for n in range(CHUNKS + 1)]
        attr_loaded = [sem(f"attr_loaded{n}") for n in range(CHUNKS)]
        consts_set = sem("sort_consts_set")
        steps = sem("table_steps")
        loop_steps = sem("table_loop_steps")
        onehots = sem("onehots_ready")
        counted = sem("onehots_counted")
        guards = sem("guards_stored")
        attr_rows = k.arg["edge_attr_128"].rearrange("(p t) d -> p t d", p=P)

        with nc.Block() as block:
            @block.sync
            def _(sp):
                for n, a in enumerate((k.arg["src"], k.arg["dst"], k.arg["edge_type_8"])):
                    sp.dma_start(raw[:, n, :], a.rearrange("(p t) -> p t", p=P)).then_inc(loaded, 16)
                sp.dma_start(weight[:, :], k.arg["edge_weight"].rearrange("(p t) -> p t", p=P)).then_inc(loaded, 16)
                for n in range(CHUNKS):
                    t = slice(turns[n] * K, turns[n + 1] * K)
                    halves(sp, attr[:, t, :], attr_rows[:, t, :], attr_loaded[n])
                sp.wait_ge(consts_set, 5)
                for table in (k.by_src, k.by_dst):
                    sp.dma_start(table[0:1, :], guard[:, :]).then_inc(guards, 16)
                sp.wait_ge(guards, 32)

            @block.gpsimd
            def _(pool):
                g = nc.gpsimd
                g.iota(k.bins[:, :], [[1, BINS]], base=0, channel_multiplier=0,
                       allow_small_or_imprecise_dtypes=True).then_inc(consts_set, 1)
                g.memset(k.below[:, :, :], 1.0).then_inc(consts_set, 1)
                pool.wait_ge(consts_set, 2)
                g.affine_select(out=k.below[:, 0, :], in_=k.below[:, 0, :], compare_op=ALU.is_gt, fill=0.0,
                                base=0, pattern=[[1, P]], channel_multiplier=-1).then_inc(consts_set, 1)
                g.affine_select(out=k.below[:, 1, :], in_=k.below[:, 1, :], compare_op=ALU.is_ge, fill=0.0,
                                base=0, pattern=[[-1, P]], channel_multiplier=1).then_inc(consts_set, 1)
                g.memset(guard[:, :], -1.0).then_inc(consts_set, 1)

            @block.tensor
            def _(pe):
                pe.wait_ge(steps, 1)
                pe.sem_inc(counted, 1)
                with pe.Fori(0, k.tiles // 2) as i:
                    for t in range(2):
                        for m in range(4):
                            pe.wait_ge(onehots, i * 8 + t * 4 + m + 1)
                            nc.tensor.matmul(count[:, m, :], ones_col[:, :], onehot[:, t * 4 + m, :], start=False,
                                             stop=True, skip_group_check=True).then_inc(counted, 1)

            @block.vector
            def _(dve):
                v = nc.vector
                c = Chain(dve, steps)
                v.memset(ones_col[:, :], 1.0)
                v.memset(ones_bins[:, :], 1.0)
                c.done(v.memset(count[:, :, :], 0.0))
                dve.wait_ge(loaded, 64)
                v.memset(k.edges[:, :, :], 0.0)
                for n in range(2):
                    v.tensor_scalar(split[:, n, 0, :], raw[:, n, :], BINS - 1, None, ALU.bitwise_and)
                    c.done(v.tensor_scalar(split[:, n, 1, :], raw[:, n, :], LOW_BITS, None,
                                           ALU.logical_shift_right))
                v.tensor_copy(dig[:, :, :], split[:, :, :, :].rearrange("p a b t -> p (a b) t"))
                c.done(v.tensor_copy(k.edges[:, :, 0:3], raw[:, :, :].rearrange("p n t -> p t n")))
                c.done(v.tensor_copy(k.edges[:, :, WEIGHT], weight[:, :]))
                dve.wait_ge(consts_set, 4)

                def turn(i):
                    c1 = Chain(dve, loop_steps, i, 3)
                    c1.done(v.tensor_tensor(prod[:, :, :], attr[:, bass.ds(i * K, K), :],
                                            k.WeB[0:P, :].unsqueeze(1).to_broadcast([P, K, D]), ALU.mult))
                    c1.done(v.tensor_reduce(dot[:, :], prod[:, :, :], AX.X, ALU.add))
                    c1.done(v.tensor_copy(k.edges[:, bass.ds(i * K, K), LOGIT], dot[:, :]))
                    c1.close()
                    for t in range(K):
                        for m in range(4):
                            dve.wait_ge(counted, i * K * 4 + ((t - 2) * 4 + m + 2 if t >= 2 else 1))
                            v.tensor_scalar(onehot[:, (t % 2) * 4 + m, :], k.bins[:, :],
                                            dig[:, m, bass.ds(i * K + t, 1)], None,
                                            ALU.is_equal).then_inc(onehots, 1)

                for n in range(CHUNKS):
                    dve.wait_ge(attr_loaded[n], 32)
                    with dve.Fori(turns[n], turns[n + 1]) as i:
                        turn(i)
                dve.wait_ge(counted, k.tiles * 4 + 1)
                c.done(v.tensor_copy(seen[:, :, :], count[:, :, :]))
                for m in range(4):
                    c.done(v.tensor_tensor_scan(k.base[:, m, :], ones_bins[:, :], seen[:, m, :], 0.0,
                                                ALU.mult, ALU.add))
                c.done(v.tensor_tensor(k.base[:, :, :], k.base[:, :, :], seen[:, :, :], ALU.subtract))
                c.done(v.tensor_scalar(k.base[:, :, :], k.base[:, :, :], 1.0, None, ALU.add))
                for m in range(2):
                    c.done(v.tensor_copy(k.digits[:, m, :], dig[:, 2 * m, :]))


class Norms:

    def __init__(self, flow, rows, tiles):
        self.flow, self.k, self.rows = flow, flow.k, rows
        self.stats, self.mv = flow.each("stats", [rows, tiles, 6]), flow.each("mv", [rows, tiles, 2])
        self.std, self.rs, self.nm = (flow.each(n, [rows, tiles]) for n in ("std", "rs", "nm"))

    def moments(self, c, b, s):
        v, n = self.k.nc.vector, s.shape[1]
        for j in range(n):
            ins = v.bn_stats(self.stats[b][:, j, :], s[:, j, :])
        c.done(ins)
        c.hold()
        for j in range(n):
            ins = v.bn_aggr(self.mv[b][:, j, :], self.stats[b][:, j, :])
        return ins

    def root(self, act, which=""):
        def step(i, b):
            self.flow.wait(act, "mv" + which, i, b)
            self.k.nc.scalar.activation(self.std[b][:, :], self.mv[b][:, :, 1], ACT.Sqrt,
                                        bias=self.k.eps1[0:self.rows, :]).then_inc(self.flow.on["std" + which], 1)
        return step

    def shift(self, dve, which=""):
        def step(i, b):
            v = self.k.nc.vector
            c = self.flow.chain(dve, "v_shift" + which, i, b, 1)
            self.flow.wait(dve, "std" + which, i, b)
            c.done(v.reciprocal(self.rs[b][:, :], self.std[b][:, :]))
            v.scalar_tensor_tensor(self.nm[b][:, :], self.mv[b][:, :, 0], -1.0, self.rs[b][:, :], ALU.mult,
                                   ALU.mult).then_inc(self.flow.on["nm" + which], 1)
        return step


def normalise(k, out, s, rs, nm):
    for j in range(out.shape[1]):
        ins = k.nc.scalar.activation(out[:, j, :], s[:, j, :], ACT.Identity, bias=nm[:, j:j + 1],
                                     scale=rs[:, j:j + 1])
    return ins


def transpose_tiles(k, out, x):
    rows = x.shape[0]
    for j in range(x.shape[1]):
        ins = k.nc.tensor.transpose(out[:, j, 0:rows], x[:, j, :], k.ident[0:rows, 0:rows])
    return ins


def project_pair(k, out, xT, weights, bias3):
    rows = out.shape[0]
    k.nc.tensor.matmul(out[:, :, :], k.ones3[:, 0:rows], bias3[:, :, :], start=True, stop=False, skip_group_check=True)
    for j in range(2):
        ins = k.nc.tensor.matmul(out[:, j, :], xT[:, j, :], weights[:, :], start=False, stop=True,
                                 skip_group_check=True)
    return ins


def halves(sp, to, of, sem):
    rows = to.shape[0]
    sp.dma_start(to[0:112], of[0:112]).then_inc(sem, 16)
    sp.dma_start(to[112:rows], of[112:rows]).then_inc(sem, 16)


def pairs(quad):
    return quad[:, :, :].rearrange("p (a b) d -> p a b d", a=2)


class Flow:

    def __init__(self, k, name, turns, slots, stages):
        assert stages % slots == 0 and turns > 2
        self.k, self.name, self.turns, self.slots, self.stages = k, name, turns, slots, stages
        self.items = turns * slots
        self.own = ExitStack()
        self.on = {}
        self.links, self.held = {}, {}

    def sb(self, what, shape, dt=F32):
        return self.own.enter_context(self.k.nc.sbuf_tensor(f"{self.name}_{what}", shape, dt))

    def each(self, what, shape, dt=F32, copies=None):
        n = copies or self.slots
        some = [self.sb(f"{what}{b}", shape, dt) for b in range(n)]
        return [some[b % n] for b in range(self.slots)]

    def ps(self, what, shape, copies=1):
        some = [self.own.enter_context(self.k.nc.psum_tensor(f"{self.name}_{what}{n}", shape, F32))
                for n in range(copies)]
        return [some[b % copies] for b in range(self.slots)]

    def sem(self, what):
        return self.k.semaphore(f"{self.name}_{what}")

    def sems(self, *names):
        for n in names:
            self.on[n] = self.sem(n)

    def norms(self, rows, tiles):
        return Norms(self, rows, tiles)

    def item(self, i, b):
        return i * self.slots + b

    def wait(self, engine, event, i, b, back=0, per=1, part=1):
        if isinstance(event, str):
            event = self.on[event]
        value = (self.item(i, b) - back) * per + part
        if isinstance(value, int):
            value = min(value, self.items * per)
        if not isinstance(value, int) or value > 0:
            engine.wait_ge(event, value)

    def arrived(self, engine, sem, i, amount=16, before=0):
        value = (i + (1 - before)) * amount
        if isinstance(sem, Queue):
            sem, value = sem.sem, value + sem.before
        if not isinstance(value, int) or value > 0:
            engine.wait_ge(sem, value)

    def chain(self, engine, what, i, b, steps):
        if what not in self.links:
            self.links[what] = self.sem(what)
        return Chain(engine, self.links[what], self.item(i, b), steps, held=self.holder(engine))

    def holder(self, engine):
        if engine not in self.held:
            self.held[engine] = self.sem(f"held{len(self.held)}")
        return self.held[engine]

    def hold(self, engine):
        engine.sem_inc(self.holder(engine), 1)

    def run(self, engine, steps, parts=1, begin=None, before=None, beside=None):
        lag = self.stages // self.slots

        def turn(i, part=0, first=False, last=False):
            ahead = before(part) if before and not last else {}
            after = beside(part) if beside and not last else {}
            for tau in range(self.stages):
                slot, stage = divmod(tau, lag)
                if stage in ahead:
                    ahead[stage](i, slot)
                for b in reversed(range(self.slots)):
                    stage, back = tau - lag * b, 0
                    if stage < 0:
                        stage, back = stage + self.stages, 1
                    if stage in steps and not (back and first) and not (not back and last):
                        steps[stage](i - back, b)
                slot, stage = divmod(tau, lag)
                if stage in after:
                    after[stage](i, slot)

        for part in range(parts):
            start, end = part * self.turns // parts, (part + 1) * self.turns // parts
            if begin:
                begin(part)
            if part == 0:
                turn(0, first=True)
                turn(1)
                start = 2
            with engine.Fori(start, end) as i:
                turn(i, part)
        turn(self.turns, last=True)


class Radix:

    def __init__(self, k, fl, own):
        self.k, self.fl = k, fl
        nc = k.nc

        def sb(what, shape, dt=F32):
            return own.enter_context(nc.sbuf_tensor(f"radix_{what}", shape, dt))

        assert fl.turns % 4 == 0 and fl.slots % 2 == 0 and k.tiles * 4 == fl.items * Q
        self.part_turns = fl.turns // 4
        self.onehot = sb("onehot", [P, 2 * Q, BINS], BF16)
        self.apart = sb("apart", [P, Q, BINS], BF16)
        self.one = sb("one", [P, 1])
        self.picked = sb("picked", [P, 2, BINS])
        self.place = fl.each("place", [P, Q])
        self.place_i = fl.each("place_i", [P, Q], I32)
        self.payload = fl.each("payload", [P, Q, COLS])
        self.rows = sb("rows", [P, k.tiles, COLS])
        self.high = sb("high", [P, 2, k.tiles], I32)
        self.highf = sb("highf", [P, k.tiles])
        self.rank = own.enter_context(nc.psum_tensor("radix_rank", [P, 2, 512], F32))
        self.scattered = [k.queue(f"scattered_0_{b}", fl.turns * Q * 16) for b in range(fl.slots)]
        self.rows_loaded, self.digit_steps = fl.sem("rows_loaded"), fl.sem("digit_steps")
        fl.sems("onehots", "ranked", "read", "based", "placed", "digits", "apart")
        self.tables = (k.by_src1, k.by_src, k.by_dst1, k.by_dst)

    def tile(self, part, i, b):
        return (i - part * self.part_turns) * (self.fl.slots * Q) + b * Q

    def load_rows(self, sp, part):
        if part % 2:
            for b in range(self.fl.slots):
                self.fl.arrived(sp, self.scattered[b], part * self.part_turns - 1, Q * 16)
            sp.dma_start(self.rows[:, :, :], self.tables[part - 1][1:self.k.E + 1, :].rearrange("(t p) w -> p t w", p=P)
                         ).then_inc(self.rows_loaded, 16)

    def first_rows(self, pe, part):
        if part:
            pe.wait_ge(self.fl.on["read"], part * self.k.tiles)
        pe.wait_ge(self.fl.on["based"], part + 1)
        for bank in range(2):
            self.k.nc.tensor.matmul(self.rank[:, bank, :], self.k.ones_row[:, 0:P], self.k.base[:, part, :],
                                    start=True, stop=True, skip_group_check=True)

    def count(self, pe, h):
        def add(bank, mask, slot):
            return self.k.nc.tensor.matmul(self.rank[:, bank, :], self.k.below[:, mask, :], self.onehot[:, slot, :],
                                           start=False, stop=True, skip_group_check=True)

        def step(i, b):
            fl = self.fl
            for t in (2 * h, 2 * h + 1):
                at = (b % 2) * Q + t
                fl.wait(pe, "read", i, b, per=Q, part=t - 1)
                add(t % 2, 1, (at - 2) % (2 * Q))
                add(t % 2, 2, (at - 1) % (2 * Q))
                fl.wait(pe, "onehots", i, b, per=Q, part=t + 1)
                add(t % 2, 0, at).then_inc(fl.on["ranked"], 1)
        return step

    def digits(self, dve, part):
        v, k, fl = self.k.nc.vector, self.k, self.fl
        if part:
            dve.wait_ge(fl.on["ranked"], part * k.tiles)
        else:
            v.memset(self.one[:, :], 1.0).then_inc(fl.on["digits"], 1)
        v.memset(self.onehot[:, 2 * Q - 2:, :], 0.0).then_inc(fl.on["based"], 1)
        if part % 2:
            c = Chain(dve, self.digit_steps, part // 2, 3)
            dve.wait_ge(self.rows_loaded, 16 * (part // 2 + 1))
            c.done(v.tensor_copy(self.high[:, 0, :], self.rows[:, :, SRC if part == 1 else DST]))
            c.done(v.tensor_scalar(self.high[:, 1, :], self.high[:, 0, :], LOW_BITS, None, ALU.logical_shift_right))
            c.done(v.tensor_copy(self.highf[:, :], self.high[:, 1, :]))
            c.close()
        if part:
            dve.sem_inc(fl.on["digits"], 1)

    def mark(self, act, part):
        a, fl = self.k.nc.scalar, self.fl
        digits = self.highf[:, :] if part % 2 else self.k.digits[:, part // 2, :]

        def step(i, b):
            fl.wait(act, "onehots", i, b, per=Q, part=0)
            for t in range(Q):
                ins = a.activation(self.apart[:, t, :], self.k.bins[:, :], ACT.Square, scale=-1.0,
                                   bias=digits[:, bass.ds(self.tile(part, i, b) + t, 1)])
            ins.then_inc(fl.on["apart"], 1)
            fl.wait(act, "apart", i, b)
            fl.wait(act, "ranked", i, b, back=1, per=Q, part=2)
            at = (b % 2) * Q
            a.activation(self.onehot[:, at:at + Q, :], self.apart[:, :, :], ACT.Relu, scale=-1.0,
                         bias=self.one[:, :]).then_inc(fl.on["onehots"], Q)
        return step

    def pick(self, dve, part, h):
        v, fl = self.k.nc.vector, self.fl
        rows = self.rows if part % 2 else self.k.edges

        def step(i, b):
            c = fl.chain(dve, f"v_pick{h}", i, b, 2 + h)
            for t in (2 * h, 2 * h + 1):
                fl.wait(dve, "ranked", i, b, per=Q, part=t + 1)
                c.done(v.tensor_tensor_reduce(out=self.picked[:, t % 2, :], in0=self.rank[:, t % 2, :],
                                              in1=self.onehot[:, (b % 2) * Q + t, :], scale=1.0, scalar=0.0,
                                              op0=ALU.mult, op1=ALU.add, accum_out=self.place[b][:, t:t + 1]))
                dve.sem_inc(fl.on["read"], 1)
            if h:
                fl.arrived(dve, self.scattered[b], i, Q * 16, before=1)
                v.tensor_copy(self.payload[b][:, :, :], rows[:, bass.ds(self.tile(part, i, b), Q), :])
                c.done(v.tensor_copy(self.place_i[b][:, :], self.place[b][:, :]))
                dve.sem_inc(fl.on["placed"], 1)
            c.close()
        return step

    def scatter(self, pool, part):
        def step(i, b):
            self.fl.wait(pool, "placed", i, b)
            self.fl.hold(pool)
            for t in range(Q):
                self.k.nc.gpsimd.indirect_dma_start(
                    self.tables[part], bass.IndirectOffsetOnAxis(ap=self.place_i[b][:, t:t + 1], axis=0),
                    self.payload[b][:, t, :], None).then_inc(self.scattered[b].sem, 16)
        return step

    def landed(self, pool):
        for b in range(self.fl.slots):
            self.fl.arrived(pool, self.scattered[b], self.fl.turns - 1, Q * 16)


def dense(k):
    nc = k.nc
    fl = Flow(k, "dense", k.groups // 5, 10, 30)
    x, s, x1 = (fl.each(n, [P, Q, D]) for n in ("x", "s", "x1"))
    s3 = s4 = s
    x4 = x
    x23 = fl.each("x23", [P, Q, 2 * D])
    x2, x3 = [t[:, :, 0:D] for t in x23], [t[:, :, D:] for t in x23]
    xT, x2T = fl.each("xT", [D, Q, D], copies=2), fl.each("x2T", [D, Q, D], copies=2)
    junk = fl.each("junk", [P, D], copies=2)
    ss, std0, rs0, std2, rs2, nm2 = (fl.each(n, [P, Q]) for n in ("ss", "std0", "rs0", "std2", "rs2", "nm2"))
    norm = fl.norms(P, Q)
    T, T2, O, O2 = fl.ps("T", [D, Q, D]), fl.ps("T2", [D, Q, D]), fl.ps("O", [P, 2, 2, 2 * D]), fl.ps("O2", [P, 2, 2, 2 * D])
    x_loaded, x1_stored, x23_stored, out_stored = ([fl.sem(f"{n}{b}") for b in range(fl.slots)] for n in (
        "x_loaded", "x1_stored", "x23_stored", "out_stored"))
    h1_stored = fl.sem("h1_stored")
    fl.sems("t", "c", "o", "square", "std0", "o_read", "summed", "mv", "std", "nm", "x1", "x2", "t2", "c2", "o2", "relu", "summed3",
            "mv3", "std3", "nm3", "x3", "s4", "mv4", "std4", "nm4", "x4")

    radix = Radix(k, fl, fl.own)

    def rows(table, i, b):
        group = table[bass.ds((i * 5 + b // 2) * (P * K), P * K), :].rearrange("(p j) d -> p j d", p=P)
        return group[:, (b % 2) * Q:(b % 2) * Q + Q, :]

    with nc.Block() as block:
        @block.gpsimd
        def _(pool):
            def norm2(i, b):
                fl.wait(pool, "nm", i, b)
                fl.arrived(pool, x23_stored[b], i, 32, before=1)
                fl.hold(pool)
                for j in range(Q):
                    ins = nc.gpsimd.tensor_scalar(x2[b][:, j, :], s[b][:, j, :], rs2[b][:, j:j + 1], nm2[b][:, j:j + 1],
                                                  ALU.mult, ALU.add)
                ins.then_inc(fl.on["x2"], 1)

            def norm3(i, b):
                fl.wait(pool, "nm3", i, b)
                fl.hold(pool)
                for j in range(Q):
                    ins = nc.gpsimd.tensor_scalar(x3[b][:, j, :], s3[b][:, j, :], norm.rs[b][:, j:j + 1],
                                                  norm.nm[b][:, j:j + 1], ALU.mult, ALU.add)
                ins.then_inc(fl.on["x3"], 1)
                fl.wait(pool, "x3", i, b)
                nc.gpsimd.tensor_tensor(s4[b][:, :, :], x3[b], k.sig2B[0:P, :].unsqueeze(1).to_broadcast([P, Q, D]),
                                        ALU.add).then_inc(fl.on["s4"], 1)

            fl.run(pool, {10: norm2, 18: norm3}, 4, beside=lambda part: {2: radix.scatter(pool, part)})
            radix.landed(pool)

        @block.sync
        def _(sp):
            def load(i, b):
                fl.arrived(sp, out_stored[b], i, 32, before=1)
                fl.hold(sp)
                halves(sp, x[b], rows(k.arg["x"], i, b), x_loaded[b])

            def store_h1(i, b):
                if b % 2 == 0:
                    sp.dma_start(k.h1[bass.ds((i * 5 + b // 2) * (P * K), P * K), :].rearrange("(p j) d -> p (j d)", p=P),
                                 k.sig1B[:, :]).then_inc(h1_stored, 16)

            def store_x1(i, b):
                fl.wait(sp, "x1", i, b)
                fl.hold(sp)
                halves(sp, rows(k.x1, i, b), x1[b], x1_stored[b])

            def store_x23(i, b):
                fl.wait(sp, "x3", i, b)
                fl.hold(sp)
                halves(sp, rows(k.x23, i, b), x23[b], x23_stored[b])

            def store_out(i, b):
                fl.wait(sp, "x4", i, b)
                fl.hold(sp)
                halves(sp, rows(k.arg["out"], i, b), x4[b], out_stored[b])

            fl.run(sp, {0: load, 1: store_h1, 11: store_x1, 19: store_x23, 26: store_out}, 4,
                   begin=lambda part: radix.load_rows(sp, part))
            for b in range(fl.slots):
                for stored in (x1_stored, x23_stored, out_stored):
                    sp.wait_ge(stored[b], 32 * fl.turns)
            sp.wait_ge(h1_stored, 16 * k.groups)

        @block.tensor
        def _(pe):
            def transpose(i, b):
                fl.arrived(pe, x_loaded[b], i, 32)
                fl.wait(pe, "c", i, b, back=1)
                transpose_tiles(k, T[b], x[b]).then_inc(fl.on["t"], 1)

            def layer0(i, b):
                fl.wait(pe, "c", i, b)
                fl.wait(pe, "o_read", i, b, back=1)
                for h in range(2):
                    ins = project_pair(k, O[b][:, h, :, :], xT[b][:, 2 * h:2 * h + 2, 0:P], k.W0cat, k.bias0)
                ins.then_inc(fl.on["o"], 1)

            def transpose2(i, b):
                fl.wait(pe, "x2", i, b)
                fl.wait(pe, "c2", i, b, back=1)
                transpose_tiles(k, T2[b], x2[b]).then_inc(fl.on["t2"], 1)

            def layer2(i, b):
                fl.wait(pe, "c2", i, b)
                fl.wait(pe, "summed3", i, b, back=1)
                for h in range(2):
                    ins = project_pair(k, O2[b][:, h, :, :], x2T[b][:, 2 * h:2 * h + 2, 0:P], k.W2cat, k.bias2)
                ins.then_inc(fl.on["o2"], 1)

            fl.run(pe, {3: transpose, 5: layer0, 11: transpose2, 13: layer2}, 4,
                   begin=lambda part: radix.first_rows(pe, part),
                   beside=lambda part: {0: radix.count(pe, 0), 1: radix.count(pe, 1)})

        @block.scalar
        def _(act):
            a = nc.scalar

            def copy(i, b):
                fl.wait(act, "t", i, b)
                fl.wait(act, "o", i, b, back=2)
                a.activation(xT[b][:, :, 0:P], T[b][:, :, 0:P], ACT.Copy).then_inc(fl.on["c"], 1)

            def variance0(i, b):
                fl.wait(act, "o", i, b)
                fl.wait(act, "summed", i, b, back=fl.slots)
                for j in range(Q):
                    a.activation(junk[b][:, :], O[b][:, j // 2, j % 2, 0:D], ACT.Square,
                                 accum_out=ss[b][:, j:j + 1]).then_inc(fl.on["square"], 1)
                    fl.wait(act, "square", i, b, per=Q, part=j + 1)
                a.activation(std0[b][:, :], ss[b][:, :], ACT.Sqrt, bias=k.eps1[0:P, :],
                             scale=1.0 / D).then_inc(fl.on["std0"], 1)

            def root1(i, b):
                fl.wait(act, "mv", i, b)
                a.activation(norm.std[b][:, :], norm.mv[b][:, :, 1], ACT.Sqrt, bias=k.eps1[0:P, :])
                a.activation(std2[b][:, :], norm.mv[b][:, :, 1], ACT.Sqrt, bias=k.eps2[0:P, :],
                             scale=1.0 + EPS).then_inc(fl.on["std"], 1)

            def norm1(i, b):
                fl.wait(act, "nm", i, b)
                fl.arrived(act, x1_stored[b], i, 32, before=1)
                normalise(k, x1[b], s[b], norm.rs[b], norm.nm[b]).then_inc(fl.on["x1"], 1)

            def copy2(i, b):
                fl.wait(act, "t2", i, b)
                fl.wait(act, "o2", i, b, back=2)
                a.activation(x2T[b][:, :, 0:P], T2[b][:, :, 0:P], ACT.Copy).then_inc(fl.on["c2"], 1)

            def relu(i, b):
                fl.wait(act, "o2", i, b)
                a.activation(pairs(s4[b]), O2[b][:, :, :, 0:D], ACT.Relu).then_inc(fl.on["relu"], 1)

            def norm4(i, b):
                fl.wait(act, "nm4", i, b)
                fl.arrived(act, out_stored[b], i, 32, before=1)
                normalise(k, x4[b], s4[b], norm.rs[b], norm.nm[b]).then_inc(fl.on["x4"], 1)

            fl.run(act, {4: copy, 6: variance0, 8: root1, 10: norm1, 12: copy2, 14: relu, 16: norm.root(act, "3"),
                         21: norm.root(act, "4"), 24: norm4}, 4,
                   begin=lambda part: act.wait_ge(fl.on["digits"], part + 1),
                   before=lambda part: {0: radix.mark(act, part)})

        @block.vector
        def _(dve):
            v = nc.vector

            def sum1(i, b):
                c = fl.chain(dve, "v_sum1", i, b, 4)
                fl.wait(dve, "std0", i, b)
                fl.wait(dve, "x2", i, b, back=fl.slots)
                c.done(v.reciprocal(rs0[b][:, :], std0[b][:, :]))
                for j in range(Q):
                    ins = v.scalar_tensor_tensor(s[b][:, j, :], O[b][:, j // 2, j % 2, D:], rs0[b][:, j:j + 1],
                                                 k.betaB[0:P, :], ALU.mult, ALU.add)
                c.done(ins)
                dve.sem_inc(fl.on["o_read"], 1)
                c.done(v.scalar_tensor_tensor(s[b][:, :, :], s[b][:, :, :], 0.0, x[b][:, :, :], ALU.max, ALU.add))
                dve.sem_inc(fl.on["summed"], 1)
                norm.moments(c, b, s[b]).then_inc(fl.on["mv"], 1)
                c.close()

            def shift1(i, b):
                c = fl.chain(dve, "v_shift1", i, b, 1)
                fl.wait(dve, "std", i, b)
                v.reciprocal(norm.rs[b][:, :], norm.std[b][:, :])
                c.done(v.reciprocal(rs2[b][:, :], std2[b][:, :]))
                for nm, rs in ((norm.nm, norm.rs), (nm2, rs2)):
                    ins = v.scalar_tensor_tensor(nm[b][:, :], norm.mv[b][:, :, 0], -1.0, rs[b][:, :], ALU.mult, ALU.mult)
                ins.then_inc(fl.on["nm"], 1)

            def sum3(i, b):
                c = fl.chain(dve, "v_sum3", i, b, 2)
                fl.wait(dve, "relu", i, b)
                c.done(v.tensor_tensor(pairs(s3[b]), O2[b][:, :, :, D:], pairs(s4[b]), ALU.add))
                dve.sem_inc(fl.on["summed3"], 1)
                norm.moments(c, b, s3[b]).then_inc(fl.on["mv3"], 1)
                c.close()

            def sum4(i, b):
                c = fl.chain(dve, "v_sum4", i, b, 1)
                fl.wait(dve, "s4", i, b)
                norm.moments(c, b, s4[b]).then_inc(fl.on["mv4"], 1)
                c.close()

            fl.run(dve, {7: sum1, 9: shift1, 15: sum3, 17: norm.shift(dve, "3"), 20: sum4, 23: norm.shift(dve, "4")}, 4,
                   begin=lambda part: radix.digits(dve, part),
                   before=lambda part: {1: radix.pick(dve, part, 0),
                                         2: radix.pick(dve, part, 1)})
    fl.own.close()


class Order:

    def __init__(self, k, name, table, key):
        nc = k.nc
        self.k, self.key = k, key
        own = self.own = ExitStack()

        def sb(what, shape, dt=F32):
            return own.enter_context(nc.sbuf_tensor(f"{name}_{what}", shape, dt))

        def sem(what):
            return k.semaphore((f"{name}_{what}"))

        self.cols = sb("cols", [R, k.tiles, COLS])
        self.keys = sb("keys_in", [R, k.tiles])
        self.ids = sb("ids", [R, 6, k.tiles], I32)
        self.lead = sb("lead", [R, 2, k.tiles], I32)
        self.keys_out = k.dram(f"{name}_keys", (1, k.tiles * R))
        with ExitStack() as tmp:
            raw = tmp.enter_context(nc.sbuf_tensor(f"{name}_raw", [R, k.tiles, COLS], F32))
            before = tmp.enter_context(nc.sbuf_tensor(f"{name}_before", [R, k.tiles, 1], F32))
            same = tmp.enter_context(nc.sbuf_tensor(f"{name}_same", [R, k.tiles], F32))
            loaded, keys_stored, steps = (sem(x) for x in ("loaded", "keys_stored", "steps"))
            with nc.Block() as block:
                @block.sync
                def _(sp):
                    slow = dict(allow_slow_non_contiguous=True)
                    sp.dma_start(raw[1:R, :, :], table[1:k.E + 1, :].rearrange("(t p) w -> p t w", p=P)).then_inc(loaded, 16)
                    sp.dma_start(raw[0:1, 0:k.tiles - 1, :],
                                 table[1 + P:k.E + 1, :].rearrange("(t p) w -> p t w", p=P)[0:1]).then_inc(loaded, 16)
                    sp.dma_start(before[1:R, :, :], table[0:k.E, key:key + 1].rearrange("(t p) w -> p t w", p=P),
                                 **slow).then_inc(loaded, 16)
                    sp.wait_ge(loaded, 48)
                    out = self.keys_out.rearrange("a (t r) -> r t a", r=R)
                    sp.dma_start(out[1:R], raw[1:R, :, key:key + 1], **slow).then_inc(keys_stored, 16)
                    sp.dma_start(out[0:1], raw[1:2, :, key:key + 1], **slow).then_inc(keys_stored, 16)
                    sp.wait_ge(keys_stored, 32)

                @block.vector
                def _(dve):
                    v = nc.vector
                    c = Chain(dve, steps)
                    v.memset(raw[0:1, k.tiles - 1:, :], 0.0)
                    c.done(v.memset(before[0:1, :, :], 0.0))
                    dve.wait_ge(loaded, 48)
                    c.done(v.tensor_copy(self.cols[:, :, :], raw[:, ::-1, :]))
                    c.done(v.tensor_copy(self.keys[:, :], self.cols[:, :, key]))
                    v.memset(self.keys[0:1, 0:1], -1.0)
                    ends = self.cols[:, :, 0:2].rearrange("p t w -> p w t")
                    v.tensor_copy(self.ids[:, 0:2, :], ends)
                    v.tensor_scalar(self.ids[:, 2:4, :], ends, 2.0, None, ALU.mult)
                    v.tensor_scalar(self.ids[:, 4:6, :], ends, 2.0, 1.0, ALU.mult, ALU.add)
                    c.done(v.tensor_tensor(same[:, :], self.cols[:, :, key], before[:, ::-1, 0], ALU.is_equal))
                    c.done(v.memset(same[0:1, :], 1.0))
                    c.done(v.scalar_tensor_tensor(same[:, :], same[:, :], float(FAR), self.cols[:, :, key],
                                                  ALU.mult, ALU.add))
                    v.tensor_copy(self.lead[:, 0, :], same[:, :])
                    v.tensor_scalar(self.lead[:, 1, :], same[:, :], 2.0, 1.0, ALU.mult, ALU.add)


class Edges(Flow):

    def __init__(self, k, name, order, stages):
        slots = 10
        assert k.tiles % (2 * slots) == 0
        super().__init__(k, name, k.tiles // (2 * slots), slots, stages)
        self.order = order
        self.gather_list, self.scatter_list = (), ()

    def tile(self, i, b):
        return (i * self.slots + b) * 2

    def gathers(self, ids, freed, *of):
        self.gather_list, self.gather_ids, self.freed = of, ids, freed
        self.ix = self.each("ix", [R, len(of), 2], I32)
        self.gathered = [self.k.queue(f"gathered_{b}", self.turns * 32 * len(of)) for b in range(self.slots)]

    def scatters(self, *of):
        self.scatter_list = of
        self.lx = [self.each(f"lx{n}_", [R, 2], I32) for n in range(len(of))]
        self.scattered = [[self.k.queue(f"scattered_{n}_{b}", self.turns * 32) for b in range(self.slots)]
                          for n in range(len(of))]

    def gathered_all(self, engine, i, b):
        self.arrived(engine, self.gathered[b], i, 32 * len(self.gather_list))

    def scattered_before(self, engine, n, i, b):
        self.arrived(engine, self.scattered[n][b], i, 32, before=1)

    def gather(self, pool, i, b):
        g = self.k.nc.gpsimd
        for event in self.freed:
            self.wait(pool, event, i, b, back=self.slots)
            self.hold(pool)
        c = self.chain(pool, "rows_chosen", i, b, 1)
        c.done(g.tensor_copy(self.ix[b][:, :, :], self.order.ids[:, self.gather_ids, bass.ds(self.tile(i, b), 2)]))
        c.hold()
        for n, (table, to, width) in enumerate(self.gather_list):
            for j in range(2):
                g.indirect_dma_start(to[b][:, j, 0:width], None, table,
                                     bass.IndirectOffsetOnAxis(ap=self.ix[b][:, n, j:j + 1], axis=0)
                                     ).then_inc(self.gathered[b].sem, 16)

    def scatter(self, pool, n, i, b):
        g = self.k.nc.gpsimd
        table, of, width, ready, lead = self.scatter_list[n]
        self.scattered_before(pool, n, i, b)
        self.hold(pool)
        c = self.chain(pool, f"leads_chosen{n}", i, b, 1)
        c.done(g.tensor_copy(self.lx[n][b][:, :], self.order.lead[:, lead, bass.ds(self.tile(i, b), 2)]))
        c.hold()
        self.wait(pool, ready, i, b)
        self.hold(pool)
        for j in range(2):
            g.indirect_dma_start(table, bass.IndirectOffsetOnAxis(ap=self.lx[n][b][:, j:j + 1], axis=0),
                                 of[b][:, j, 0:width], None, bounds_check=table.shape[0] - 1,
                                 oob_is_err=False).then_inc(self.scattered[n][b].sem, 16)

    def landed(self, pool):
        for b in range(self.slots):
            if self.gather_list:
                self.arrived(pool, self.gathered[b], self.turns - 1, 32 * len(self.gather_list))
            for n in range(len(self.scatter_list)):
                self.arrived(pool, self.scattered[n][b], self.turns - 1, 32)

    def segments(self, width):
        self.sel = self.each("sel", [R, 2, R], copies=2)
        self.keysB = self.each("keysB", [R, 2 * R])
        self.keys_loaded = [self.sem(f"keys_loaded{b}") for b in range(self.slots)]
        self.spare_row = self.sb("spare_row", [1, width])
        self.sems("masks", "total", "carried")

    def load_keys(self, sp, i, b):
        self.wait(sp, "masks", i, b, back=self.slots)
        self.hold(sp)
        keys = self.order.keys_out[:, bass.ds((self.k.tiles - 2) * R - self.tile(i, b) * R, 2 * R)]
        for rows in (slice(0, 112), slice(112, R)):
            sp.dma_start(self.keysB[b][rows, :],
                         keys.to_broadcast([rows.stop - rows.start, 2 * R])).then_inc(self.keys_loaded[b], 16)

    def masks(self, dve, i, b):
        self.arrived(dve, self.keys_loaded[b], i, 32)
        self.wait(dve, "total", i, b, back=2, per=2, part=2)
        for j in range(2):
            n = self.tile(i, b) + j
            ins = self.k.nc.vector.tensor_scalar(self.sel[b][:, j, :],
                                                 self.keysB[b][:, (1 - j) * R:(2 - j) * R],
                                                 self.order.keys[:, bass.ds(n, 1)], None, ALU.is_equal)
        ins.then_inc(self.on["masks"], 1)

    def totals(self, pe, i, b, out, rows):
        self.wait(pe, "masks", i, b)
        for j in range(2):
            self.wait(pe, "carried", i, b, per=2, part=j)
            self.k.nc.tensor.matmul(out(j), self.sel[b][:, j, :], rows(j), start=True,
                                    stop=True).then_inc(self.on["total"], 1)

    def carry(self, act, i, b, buffers, tot, filled):
        width = self.spare_row.shape[1]
        for j in range(2):
            self.wait(act, "total", i, b, per=2, part=j + 1)
            if j == 0:
                to = buffers[b][0:1, 1, 0:width]
            else:
                next_i, next_b = (i + 1, 0) if b == self.slots - 1 else (i, b + 1)
                if isinstance(next_i, int) and next_i == self.turns:
                    to = self.spare_row[:, :]
                else:
                    filled(next_i, next_b)
                    to = buffers[next_b][0:1, 0, 0:width]
            self.k.nc.scalar.activation(to, tot[b][0:1, j, 0:width], ACT.Copy).then_inc(self.on["carried"], 1)

    def carried(self, engine, i, b):
        self.wait(engine, "carried", i, b, per=2, part=2)


def layer0(k, order):
    nc = k.nc
    fl = Edges(k, "l0", order, 30)
    W = D + 1
    XS, XD, mean, s, x1 = (fl.each(n, [R, 2, w]) for n, w in (("xs", D + 4), ("xd", D), ("mean", D), ("s", D), ("x1", D)))
    aT = fl.each("aT", [D, 2, R], copies=2)
    junk = fl.each("junk", [R, D])
    ss, deg, std0, rs0 = (fl.each(n, [R, 2]) for n in ("ss", "deg", "std0", "rs0"))
    norm = fl.norms(R, 2)
    T, O, tot = fl.ps("T", [D, 4, D], 2), fl.ps("O", [R, 2, 2 * D], 2), fl.ps("tot", [R, 2, 2 * D], 2)
    fl.segments(W)
    fl.sems("mean", "totals_used", "t", "c", "o", "square", "std0", "summed", "mv", "std", "nm", "x1")
    fl.gathers(slice(0, 2), ("summed",), (k.arg["x"], XS, D), (k.arg["x"], XD, D))
    fl.scatters((k.x1, x1, D, "x1", 0))

    with nc.Block() as block:
        @block.gpsimd
        def _(pool):
            fl.run(pool, {0: lambda i, b: fl.gather(pool, i, b), 20: lambda i, b: fl.scatter(pool, 0, i, b)})
            fl.landed(pool)

        @block.sync
        def _(sp):
            fl.run(sp, {2: lambda i, b: fl.load_keys(sp, i, b)})

        @block.tensor
        def _(pe):
            def totals(i, b):
                fl.gathered_all(pe, i, b)
                fl.wait(pe, "totals_used", i, b, back=2)
                fl.totals(pe, i, b, lambda j: tot[b][:, j, 0:W], lambda j: XS[b][:, j, 0:W])

            def transpose(i, b):
                fl.wait(pe, "mean", i, b)
                fl.wait(pe, "c", i, b, back=2)
                transpose_tiles(k, T[b], mean[b]).then_inc(fl.on["t"], 1)

            def project(i, b):
                fl.wait(pe, "c", i, b)
                fl.wait(pe, "summed", i, b, back=2)
                project_pair(k, O[b], aT[b], k.W0cat, k.bias0).then_inc(fl.on["o"], 1)

            fl.run(pe, {10: totals, 12: transpose, 14: project})

        @block.scalar
        def _(act):
            a = nc.scalar

            def carry(i, b):
                fl.carry(act, i, b, XS, tot, lambda ni, nb: fl.gathered_all(act, ni, nb))

            def copy(i, b):
                fl.wait(act, "t", i, b)
                fl.wait(act, "o", i, b, back=2)
                a.activation(aT[b][:, :, :], T[b][:, 0:2, 0:R], ACT.Copy).then_inc(fl.on["c"], 1)

            def variance0(i, b):
                fl.wait(act, "o", i, b)
                fl.wait(act, "summed", i, b, back=fl.slots)
                for j in range(2):
                    a.activation(junk[b][:, :], O[b][:, j, 0:D], ACT.Square,
                                 accum_out=ss[b][:, j:j + 1]).then_inc(fl.on["square"], 1)
                    fl.wait(act, "square", i, b, per=2, part=j + 1)
                a.activation(std0[b][:, :], ss[b][:, :], ACT.Sqrt, bias=k.eps1[0:R, :],
                             scale=1.0 / D).then_inc(fl.on["std0"], 1)

            def norm1(i, b):
                fl.wait(act, "nm", i, b)
                fl.scattered_before(act, 0, i, b)
                normalise(k, x1[b][:, :, :], s[b], norm.rs[b], norm.nm[b]).then_inc(fl.on["x1"], 1)

            fl.run(act, {10: carry, 13: copy, 15: variance0, 17: norm.root(act), 19: norm1})

        @block.vector
        def _(dve):
            v = nc.vector
            for x in XS:
                v.memset(x[:, :, D:D + 1], 1.0)

            def masks(i, b):
                fl.masks(dve, i, b)

            def mean_of(i, b):
                c = fl.chain(dve, "v_mean", i, b, 3)
                fl.carried(dve, i, b)
                c.done(v.tensor_scalar(deg[b][:, :], tot[b][:, :, D], 1.0, 1.0, ALU.add, ALU.max))
                fl.gathered_all(dve, i, b)
                c.done(v.tensor_tensor(mean[b][:, :, :], tot[b][:, :, 0:D], XD[b][:, :, :], ALU.add))
                dve.sem_inc(fl.on["totals_used"], 1)
                c.done(v.reciprocal(deg[b][:, :], deg[b][:, :]))
                v.tensor_tensor(mean[b][:, :, :], mean[b][:, :, :], deg[b][:, :].unsqueeze(2).to_broadcast([R, 2, D]),
                                ALU.mult).then_inc(fl.on["mean"], 1)

            def sum1(i, b):
                c = fl.chain(dve, "v_sum", i, b, 4)
                fl.wait(dve, "std0", i, b)
                c.done(v.reciprocal(rs0[b][:, :], std0[b][:, :]))
                for j in range(2):
                    ins = v.scalar_tensor_tensor(s[b][:, j, :], O[b][:, j, D:], rs0[b][:, j:j + 1], k.betaB[:, :],
                                                 ALU.mult, ALU.add)
                c.done(ins)
                c.done(v.scalar_tensor_tensor(s[b][:, :, :], s[b][:, :, :], 0.0, XD[b][:, :, :], ALU.max, ALU.add))
                dve.sem_inc(fl.on["summed"], 1)
                norm.moments(c, b, s[b]).then_inc(fl.on["mv"], 1)
                c.close()

            fl.run(dve, {9: masks, 11: mean_of, 16: sum1, 18: norm.shift(dve)})
    fl.own.close()


def layer1(k, order):
    nc = k.nc
    fl = Edges(k, "l1", order, 40)
    XS, XD = fl.each("xs", [R, 2, D]), fl.each("xd", [R, 2, D])
    s = s3 = XS
    x23 = fl.each("x23", [R, 2, 2 * D])
    x2, x3 = [t[:, :, 0:D] for t in x23], [t[:, :, D:] for t in x23]
    xT, x2T = fl.each("xT", [D, 4, R], copies=2), fl.each("x2T", [D, 2, R], copies=2)
    rels, relsT = fl.each("rels", [R, 2, RELS]), fl.each("relsT", [RELS, 2, R], copies=2)
    iota8 = fl.sb("iota8", [R, RELS])
    wide = fl.sb("wide", [R, 2, RELS * D])
    bent = fl.sb("bent", [R, 2, RELS * D])
    norm = fl.norms(R, 2)
    T, TR = fl.ps("T", [D, 4, D]), fl.ps("TR", [RELS, 4, D])
    Y, O2 = fl.ps("Y", [R, 4, D]), fl.ps("O2", [R, 2, 2 * D])
    tot = fl.ps("tot", [R, 2, 2, 512])[0]
    fl.segments(RELS * D)
    fl.sems("iota", "rels", "t", "c", "y", "wide", "bent", "reduced", "summed", "mv", "std", "nm", "x2", "t2", "c2", "o2", "relu",
            "summed3", "mv3", "std3", "nm3", "x3")
    fl.gathers(slice(0, 2), ("x3",), (k.x1, XS, D), (k.x1, XD, D))
    fl.scatters((k.x23, x23, 2 * D, "x3", 0))

    with nc.Block() as block:
        @block.gpsimd
        def _(pool):
            nc.gpsimd.iota(iota8[:, :], [[1, RELS]], base=0, channel_multiplier=0,
                           allow_small_or_imprecise_dtypes=True).then_inc(fl.on["iota"], 1)
            fl.run(pool, {0: lambda i, b: fl.gather(pool, i, b), 34: lambda i, b: fl.scatter(pool, 0, i, b)})
            fl.landed(pool)

        @block.sync
        def _(sp):
            fl.run(sp, {2: lambda i, b: fl.load_keys(sp, i, b)})

        @block.tensor
        def _(pe):
            t = nc.tensor

            def transpose(i, b):
                fl.gathered_all(pe, i, b)
                fl.wait(pe, "rels", i, b)
                fl.wait(pe, "c", i, b, back=1)
                fl.wait(pe, "c2", i, b, back=5)
                transpose_tiles(k, T[b], XS[b])
                transpose_tiles(k, T[b][:, 2:4, :], XD[b])
                transpose_tiles(k, TR[b], rels[b]).then_inc(fl.on["t"], 1)

            def message(i, b):
                fl.wait(pe, "c", i, b)
                fl.wait(pe, "wide", i, b, back=1, per=2, part=2)
                for j in range(2):
                    t.matmul(Y[b][:, j, :], xT[b][:, j, :], k.W1aT[:, :], start=True, stop=False)
                    t.matmul(Y[b][:, j, :], xT[b][:, 2 + j, :], k.W1bT[:, :], start=False, stop=False)
                    ins = t.matmul(Y[b][:, j, :], relsT[b][:, j, :], k.relC[:, :], start=False, stop=True)
                ins.then_inc(fl.on["y"], 1)

            def total(j):
                def step(i, b):
                    fl.wait(pe, "masks", i, b)
                    fl.wait(pe, "wide", i, b, per=2, part=j + 1)
                    fl.wait(pe, "carried", i, b, per=2, part=j)
                    fl.wait(pe, "bent", i, b, back=1, per=2, part=j + 1)
                    for h in range(2):
                        ins = t.matmul(tot[:, j, h, :], fl.sel[b][:, j, :], wide[:, j, 512 * h:512 * h + 512],
                                       start=True, stop=True)
                    ins.then_inc(fl.on["total"], 1)
                return step

            def transpose2(i, b):
                fl.wait(pe, "x2", i, b)
                fl.wait(pe, "c2", i, b, back=1)
                fl.wait(pe, "c", i, b, back=-4)
                transpose_tiles(k, T[b], x2[b]).then_inc(fl.on["t2"], 1)

            def project2(i, b):
                fl.wait(pe, "c2", i, b)
                fl.wait(pe, "summed3", i, b, back=1)
                project_pair(k, O2[b], x2T[b], k.W2cat, k.bias2).then_inc(fl.on["o2"], 1)

            fl.run(pe, {5: transpose, 7: message, 10: total(0), 13: total(1), 23: transpose2, 25: project2})

        @block.scalar
        def _(act):
            a = nc.scalar

            def carry_in(i, b):
                fl.wait(act, "wide", i, b, per=2, part=1)
                fl.wait(act, "total", i, b, per=2, part=0)
                if not (isinstance(i, int) and fl.item(i, b) == 0):
                    a.activation(wide[0:1, 0, :].rearrange("p (h d) -> p h d", h=2), tot[0:1, 1, :, :],
                                 ACT.Copy).then_inc(fl.on["carried"], 1)

            def carry_over(i, b):
                fl.wait(act, "wide", i, b, per=2, part=2)
                fl.wait(act, "total", i, b, per=2, part=1)
                a.activation(wide[0:1, 1, :].rearrange("p (h d) -> p h d", h=2), tot[0:1, 0, :, :],
                             ACT.Copy).then_inc(fl.on["carried"], 1)

            def bend(j):
                def step(i, b):
                    fl.wait(act, "total", i, b, per=2, part=j + 1)
                    fl.wait(act, "reduced", i, b, back=1, per=2, part=j + 1)
                    if j == 0:
                        carry_over(i, b)
                    a.activation(bent[:, j, :].rearrange("p (h d) -> p h d", h=2), tot[:, j, :, :],
                                 ACT.Tanh).then_inc(fl.on["bent"], 1)
                return step

            def norm2(i, b):
                fl.wait(act, "nm", i, b)
                fl.scattered_before(act, 0, i, b)
                normalise(k, x2[b], s[b], norm.rs[b], norm.nm[b]).then_inc(fl.on["x2"], 1)

            def copy2(i, b):
                fl.wait(act, "t2", i, b)
                fl.wait(act, "o2", i, b, back=2)
                a.activation(x2T[b][:, :, :], T[b][:, 0:2, 0:R], ACT.Copy).then_inc(fl.on["c2"], 1)

            def relu(i, b):
                fl.wait(act, "o2", i, b)
                a.activation(s3[b][:, :, :], O2[b][:, :, 0:D], ACT.Relu).then_inc(fl.on["relu"], 1)

            def norm3(i, b):
                fl.wait(act, "nm3", i, b)
                normalise(k, x3[b], s3[b], norm.rs[b], norm.nm[b]).then_inc(fl.on["x3"], 1)

            fl.run(act, {9: carry_in, 12: bend(0), 14: bend(1), 19: norm.root(act), 21: norm2, 24: copy2, 26: relu,
                         31: norm.root(act, "3"), 33: norm3})

        @block.vector
        def _(dve):
            v = nc.vector
            dve.wait_ge(fl.on["iota"], 1)

            def copy(i, b):
                fl.wait(dve, "t", i, b)
                fl.wait(dve, "y", i, b, back=2)
                v.tensor_copy(xT[b][:, :, :], T[b][:, :, 0:R])
                v.tensor_copy(relsT[b][:, :, :], TR[b][:, 0:2, 0:R]).then_inc(fl.on["c"], 1)

            def relations(i, b):
                fl.wait(dve, "wide", i, b, back=fl.slots, per=2, part=2)
                v.tensor_tensor(rels[b][:, :, :],
                                order.cols[:, bass.ds(fl.tile(i, b), 2), REL:REL + 1].to_broadcast([R, 2, RELS]),
                                iota8[:, :].unsqueeze(1).to_broadcast([R, 2, RELS]),
                                ALU.is_equal).then_inc(fl.on["rels"], 1)

            def widen(j):
                def step(i, b):
                    if j == 0:
                        fl.masks(dve, i, b)
                    fl.wait(dve, "y", i, b)
                    fl.wait(dve, "rels", i, b)
                    fl.wait(dve, "total", i, b, back=1, per=2, part=j + 1)
                    v.tensor_tensor(wide[:, j, :].rearrange("p (r d) -> p r d", r=RELS),
                                    Y[b][:, j, :].unsqueeze(1).to_broadcast([R, RELS, D]),
                                    rels[b][:, j, :].unsqueeze(2).to_broadcast([R, RELS, D]),
                                    ALU.mult).then_inc(fl.on["wide"], 1)
                return step

            def reduce(j):
                def step(i, b):
                    fl.wait(dve, "bent", i, b, per=2, part=j + 1)
                    fl.wait(dve, "x2", i, b, back=fl.slots)
                    v.tensor_reduce(s[b][:, j, :], bent[:, j, :].rearrange("p (r d) -> p d r", r=RELS),
                                    AX.X, ALU.add).then_inc(fl.on["reduced"], 1)
                return step

            def sum2(i, b):
                c = fl.chain(dve, "v_sum2", i, b, 2)
                fl.wait(dve, "reduced", i, b, per=2, part=2)
                c.done(v.tensor_tensor(s[b][:, :, :], s[b][:, :, :], XD[b][:, :, :], ALU.add))
                dve.sem_inc(fl.on["summed"], 1)
                norm.moments(c, b, s[b]).then_inc(fl.on["mv"], 1)
                c.close()

            def sum3(i, b):
                c = fl.chain(dve, "v_sum3", i, b, 2)
                fl.wait(dve, "relu", i, b)
                c.done(v.tensor_tensor(s3[b][:, :, :], O2[b][:, :, D:], s3[b][:, :, :], ALU.add))
                dve.sem_inc(fl.on["summed3"], 1)
                norm.moments(c, b, s3[b]).then_inc(fl.on["mv3"], 1)
                c.close()

            fl.run(dve, {4: relations, 6: copy, 8: widen(0), 10: widen(1), 13: reduce(0), 15: reduce(1), 16: sum2,
                         20: norm.shift(dve), 27: sum3, 32: norm.shift(dve, "3")})
    fl.own.close()


def logits(k, order, rows_s, rows_d, scores):
    nc = k.nc
    fl = Edges(k, "l2a", order, 10)
    XS, XD = fl.each("xs", [R, 2, D]), fl.each("xd", [R, 2, D])
    prod = fl.each("prod", [R, 2, D])
    part, e = fl.each("part", [R, 2, 2]), fl.each("e", [R, 2, 2])
    rows_stored = [fl.sem(f"stored{b}") for b in range(fl.slots)]
    fl.sems("dotted")
    fl.gathers(slice(2, 4), ("dotted",), (k.x23h, XS, D), (k.x23h, XD, D))

    with nc.Block() as block:
        @block.gpsimd
        def _(pool):
            def gather(i, b):
                fl.arrived(pool, rows_stored[b], i, 64, before=1)
                fl.hold(pool)
                fl.gather(pool, i, b)

            fl.run(pool, {0: gather})
            fl.landed(pool)

        @block.sync
        def _(sp):
            def store(i, b):
                fl.gathered_all(sp, i, b)
                fl.hold(sp)
                for to, of in ((rows_s, XS), (rows_d, XD)):
                    halves(sp, to[bass.ds(fl.item(i, b), 1), :, :].rearrange("a p n -> (a p) n"),
                           of[b][:, :, :].rearrange("p q d -> p (q d)"), rows_stored[b])

            fl.run(sp, {5: store})
            for b in range(fl.slots):
                sp.wait_ge(rows_stored[b], fl.turns * 64)

        @block.vector
        def _(dve):
            v = nc.vector

            def dots(i, b):
                c = fl.chain(dve, "v_dots", i, b, 4)
                fl.gathered_all(dve, i, b)
                for n, (x, u) in enumerate(((XS, k.usB), (XD, k.udB))):
                    for j in range(2):
                        ins = v.tensor_tensor_reduce(out=prod[b][:, j, :], in0=x[b][:, j, :], in1=u[:, :],
                                                     scale=1.0, scalar=0.0, op0=ALU.mult, op1=ALU.add,
                                                     accum_out=part[b][:, n, j:j + 1])
                    c.done(ins)
                dve.sem_inc(fl.on["dotted"], 1)
                c.done(v.tensor_tensor(e[b][:, 0, :], part[b][:, 0, :], part[b][:, 1, :], ALU.add))
                c.done(v.scalar_tensor_tensor(e[b][:, 1, :], e[b][:, 0, :], k.logit0[:, :],
                                              order.cols[:, bass.ds(fl.tile(i, b), 2), LOGIT], ALU.add, ALU.add))
                v.scalar_tensor_tensor(scores[:, bass.ds(fl.tile(i, b), 2)], e[b][:, 1, :], SLOPE,
                                       e[b][:, 1, :], ALU.mult, ALU.max)
                c.close()

            fl.run(dve, {5: dots})
    fl.own.close()


def segment_softmax(k, table, key, scores, probs):
    nc = k.nc
    L = k.tiles
    LOW = -1e30
    s_d, p_d = k.dram("scores_edges", (1, k.E)), k.dram("probs_edges", (1, k.E))
    ends_d, carry_d = k.dram("row_ends", (P, 6)), k.dram("row_carries", (2, P))
    with ExitStack() as own:
        def sb(what, shape, dt=F32):
            return own.enter_context(nc.sbuf_tensor(f"smax_{what}", shape, dt))

        def sem(what):
            return k.semaphore((f"smax_{what}"))

        turned = sb("turned", [R, L, 1])
        keys3 = sb("keys3", [P, 3, L])
        e = sb("e", [P, L])
        pen = sb("pen", [P, 2, L])
        run = sb("run", [P, 2, L])
        own_end = sb("own_end", [P, 2, L])
        ends = sb("ends", [P, 6])
        rows = sb("rows", [1, 6, P])
        scan_in = sb("scan_in", [1, 2, 2, P])
        carries = sb("carries", [1, 2, P])
        carry = sb("carry", [P, 2])
        guard = sb("guard", [P, 1])
        both = sb("both", [P, 3, L])
        p = sb("p", [P, L])
        loaded, dma, steps, exped = sem("loaded"), sem("moved"), sem("steps"), sem("exped")
        asked = sem("asked")
        flat = s_d.rearrange("a (p l) -> (a p) l", p=P)

        with nc.Block() as block:
            @block.sync
            def _(sp):
                n = [0]

                def move(to, of, when):
                    sp.wait_ge(asked, when)
                    sp.dma_start(to, of, allow_slow_non_contiguous=True).then_inc(dma, 16)
                    n[0] += 16
                    sp.wait_ge(dma, n[0])

                for at in range(2):
                    sp.dma_start(keys3[:, at, :].unsqueeze(2),
                                 table[at:at + k.E, key:key + 1].rearrange("(p l) w -> p l w", p=P),
                                 allow_slow_non_contiguous=True).then_inc(loaded, 16)
                move(s_d.rearrange("a (t p) -> p t a", p=P), turned[1:R, :, :], 1)
                move(e[:, :], flat, 1)
                move(ends_d, ends[:, :], 2)
                move(rows[:, :, :], ends_d.rearrange("p (a c) -> a c p", a=1), 2)
                move(carry_d.rearrange("(a c) p -> a c p", a=1), carries[:, :, :], 3)
                move(carry[:, :], carry_d.rearrange("c p -> p c"), 3)
                sp.wait_ge(exped, 1)
                move(p_d.rearrange("a (p l) -> (a p) l", p=P), p[:, :], 3)
                move(turned[1:R, :, :], p_d.rearrange("a (t p) -> p t a", p=P), 3)

            @block.scalar
            def _(act):
                act.wait_ge(asked, 4)
                nc.scalar.activation(p[:, :], both[:, 2, :], ACT.Exp).then_inc(exped, 1)

            @block.vector
            def _(dve):
                v = nc.vector
                c = Chain(dve, steps)
                c.done(v.tensor_copy(turned[:, :, 0], scores[:, ::-1]))
                dve.sem_inc(asked, 1)
                dve.wait_ge(loaded, 32)
                v.memset(keys3[:, 2, L - 1:], -2.0)
                c.done(v.tensor_copy(keys3[:, 2, 0:L - 1], keys3[:, 1, 1:L]))
                for w, at in ((0, 0), (1, 2)):
                    c.done(v.tensor_tensor(pen[:, w, :], keys3[:, at, :], keys3[:, 1, :], ALU.is_equal))
                    edge = keys3[:, 1, 0:1] if w == 0 else keys3[:, 1, L - 1:L]
                    c.done(v.tensor_scalar(own_end[:, w, :], keys3[:, 1, :], edge, None, ALU.is_equal))
                c.done(v.tensor_copy(ends[:, 4:5], pen[:, 0, 0:1]))
                c.done(v.tensor_copy(ends[:, 2:3], own_end[:, 0, L - 1:L]))
                for x in (pen, own_end):
                    c.done(v.tensor_scalar(x[:, :, :], x[:, :, :], -1.0, -LOW, ALU.add, ALU.mult))
                dve.wait_ge(dma, 32)
                v.tensor_tensor_scan(run[:, 0, :], pen[:, 0, :], e[:, :], LOW, ALU.add, ALU.max)
                c.done(v.tensor_tensor_scan(run[:, 1, ::-1], pen[:, 1, ::-1], e[:, ::-1], LOW, ALU.add, ALU.max))
                v.tensor_copy(ends[:, 0:1], run[:, 0, L - 1:L])
                v.tensor_copy(ends[:, 1:2], run[:, 1, 0:1])
                v.memset(ends[:, 3:4], 0.0)
                c.done(v.memset(ends[:, 5:6], 0.0))
                dve.sem_inc(asked, 1)
                dve.wait_ge(dma, 64)
                c.done(v.memset(scan_in[:, :, :, :], LOW))
                c.done(v.tensor_scalar(rows[:, 2, :], rows[:, 2, :], -1.0, -LOW, ALU.add, ALU.mult))
                c.done(v.tensor_scalar(rows[:, 4, :], rows[:, 4, :], -1.0, -LOW, ALU.add, ALU.mult))
                for m, x in enumerate((rows[:, 2, :], rows[:, 0, :])):
                    c.done(v.tensor_tensor(scan_in[:, 0, m, 1:], x[:, 0:P - 1], rows[:, 4, 1:], ALU.add))
                for m, x in enumerate((rows[:, 2, :], rows[:, 1, :])):
                    c.done(v.tensor_tensor(scan_in[:, 1, m, 0:P - 1], x[:, 1:], rows[:, 4, 1:], ALU.add))
                v.tensor_tensor_scan(carries[:, 0, :], scan_in[:, 0, 0, :], scan_in[:, 0, 1, :], LOW, ALU.add, ALU.max)
                c.done(v.tensor_tensor_scan(carries[:, 1, ::-1], scan_in[:, 1, 0, ::-1], scan_in[:, 1, 1, ::-1], LOW,
                                            ALU.add, ALU.max))
                dve.sem_inc(asked, 1)
                dve.wait_ge(dma, 96)
                c.done(v.scalar_tensor_tensor(both[:, 0, :], own_end[:, 0, :], carry[:, 0:1], run[:, 0, :],
                                              ALU.add, ALU.max))
                c.done(v.scalar_tensor_tensor(both[:, 1, :], own_end[:, 1, :], carry[:, 1:2], run[:, 1, :],
                                              ALU.add, ALU.max))
                c.done(v.tensor_tensor(both[:, 0, :], both[:, 0, :], both[:, 1, :], ALU.max))
                c.done(v.tensor_tensor(both[:, 2, :], e[:, :], both[:, 0, :], ALU.subtract))
                dve.sem_inc(asked, 1)
                dve.wait_ge(dma, 128)
                v.tensor_copy(probs[:, :], turned[:, ::-1, 0])


def layer2(k, order, rows_s, rows_d, probs):
    nc = k.nc
    fl = Edges(k, "l2b", order, 30)
    W = D + 1
    XS, XD, z, x3, x4 = (fl.each(n, [R, 2, D]) for n in ("xs", "xd", "z", "x3", "x4"))
    s = s4 = z
    V = fl.each("v", [R, 2, D + 4])
    zT = fl.each("zT", [D, 2, R], copies=2)
    den = fl.each("den", [R, 2])
    norm = fl.norms(R, 2)
    T, O, tot = fl.ps("T", [D, 4, D], 2), fl.ps("O", [R, 2, 2 * D], 2), fl.ps("tot", [R, 2, 2 * D], 2)
    rows_loaded = [fl.sem(f"loaded{b}") for b in range(fl.slots)]
    fl.segments(W)
    fl.sems("weighted", "totals_used", "z", "t", "c", "o", "relu", "taken", "summed", "mv", "std", "nm", "x3", "mv4", "std4", "nm4", "x4")
    fl.scatters((k.x23h, x3, D, "x3", 1), (k.arg["out"], x4, D, "x4", 0))

    with nc.Block() as block:
        @block.gpsimd
        def _(pool):
            fl.run(pool, {21: lambda i, b: fl.scatter(pool, 0, i, b), 25: lambda i, b: fl.scatter(pool, 1, i, b)})
            fl.landed(pool)

        @block.sync
        def _(sp):
            def load(i, b):
                fl.wait(sp, "summed", i, b, back=fl.slots)
                fl.hold(sp)
                for to, of in ((XS, rows_s), (XD, rows_d)):
                    halves(sp, to[b][:, :, :].rearrange("p q d -> p (q d)"),
                           of[bass.ds(fl.item(i, b), 1), :, :].rearrange("a p n -> (a p) n"), rows_loaded[b])

            fl.run(sp, {0: load, 2: lambda i, b: fl.load_keys(sp, i, b)})

        @block.tensor
        def _(pe):
            def totals(i, b):
                fl.wait(pe, "weighted", i, b)
                fl.wait(pe, "totals_used", i, b, back=2)
                fl.totals(pe, i, b, lambda j: tot[b][:, j, 0:W], lambda j: V[b][:, j, 0:W])

            def transpose(i, b):
                fl.wait(pe, "z", i, b)
                fl.wait(pe, "c", i, b, back=2)
                transpose_tiles(k, T[b], z[b]).then_inc(fl.on["t"], 1)

            def project(i, b):
                fl.wait(pe, "c", i, b)
                fl.wait(pe, "taken", i, b, back=2)
                project_pair(k, O[b], zT[b], k.W2edge, k.bias2e).then_inc(fl.on["o"], 1)

            fl.run(pe, {11: totals, 13: transpose, 15: project})

        @block.scalar
        def _(act):
            a = nc.scalar

            def weigh(i, b):
                fl.arrived(act, rows_loaded[b], i, 64)
                fl.wait(act, "total", i, b, back=fl.slots, per=2, part=2)
                for j in range(2):
                    prob = probs[:, bass.ds(fl.tile(i, b) + j, 1)]
                    a.activation(V[b][:, j, 0:D], XD[b][:, j, :], ACT.Copy, scale=prob)
                a.activation(V[b][:, :, D], probs[:, bass.ds(fl.tile(i, b), 2)], ACT.Copy).then_inc(fl.on["weighted"], 1)

            def carry(i, b):
                fl.carry(act, i, b, V, tot, lambda ni, nb: fl.wait(act, "weighted", ni, nb))

            def copy(i, b):
                fl.wait(act, "t", i, b)
                fl.wait(act, "o", i, b, back=2)
                a.activation(zT[b][:, :, :], T[b][:, 0:2, 0:R], ACT.Copy).then_inc(fl.on["c"], 1)

            def relu(i, b):
                fl.wait(act, "o", i, b)
                fl.wait(act, "x3", i, b, back=fl.slots)
                a.activation(s[b][:, :, :], O[b][:, :, 0:D], ACT.Relu).then_inc(fl.on["relu"], 1)

            def norm3(i, b):
                fl.wait(act, "nm", i, b)
                fl.scattered_before(act, 0, i, b)
                normalise(k, x3[b], s[b], norm.rs[b], norm.nm[b]).then_inc(fl.on["x3"], 1)

            def norm4(i, b):
                fl.wait(act, "nm4", i, b)
                fl.scattered_before(act, 1, i, b)
                normalise(k, x4[b], s4[b], norm.rs[b], norm.nm[b]).then_inc(fl.on["x4"], 1)

            fl.run(act, {2: weigh, 11: carry, 14: copy, 16: relu, 18: norm.root(act), 20: norm3, 22: norm.root(act, "4"),
                         24: norm4})

        @block.vector
        def _(dve):
            v = nc.vector

            def attend(i, b):
                c = fl.chain(dve, "v_attend", i, b, 3)
                fl.carried(dve, i, b)
                c.done(v.tensor_scalar(den[b][:, :], tot[b][:, :, D], 1e-30, None, ALU.max))
                c.done(v.reciprocal(den[b][:, :], den[b][:, :]))
                c.done(v.tensor_tensor(z[b][:, :, :], tot[b][:, :, 0:D], den[b][:, :].unsqueeze(2).to_broadcast([R, 2, D]),
                                       ALU.mult))
                dve.sem_inc(fl.on["totals_used"], 1)
                v.tensor_tensor(z[b][:, :, :], z[b][:, :, :], XS[b][:, :, :], ALU.add).then_inc(fl.on["z"], 1)

            def sum3(i, b):
                c = fl.chain(dve, "v_sum3", i, b, 3)
                fl.wait(dve, "relu", i, b)
                c.done(v.tensor_tensor(s[b][:, :, :], O[b][:, :, D:], s[b][:, :, :], ALU.add))
                dve.sem_inc(fl.on["taken"], 1)
                c.done(v.tensor_tensor(s[b][:, :, :], s[b][:, :, :], XS[b][:, :, :], ALU.add))
                dve.sem_inc(fl.on["summed"], 1)
                norm.moments(c, b, s[b]).then_inc(fl.on["mv"], 1)
                c.close()

            def sum4(i, b):
                c = fl.chain(dve, "v_sum4", i, b, 2)
                fl.wait(dve, "x3", i, b)
                c.done(v.tensor_tensor(s4[b][:, :, :], x3[b][:, :, :], k.sig2B[:, :].unsqueeze(1).to_broadcast([R, 2, D]),
                                       ALU.add))
                norm.moments(c, b, s4[b]).then_inc(fl.on["mv4"], 1)
                c.close()

            fl.run(dve, {10: lambda i, b: fl.masks(dve, i, b), 12: attend, 17: sum3, 19: norm.shift(dve),
                         21: sum4, 23: norm.shift(dve, "4")})
    fl.own.close()


def layer3(k, order, last):
    nc = k.nc
    fl = Edges(k, f"l3{'b' if last else 'a'}", order, 30)
    W, to_width = (HID, D) if last else (D, HID)
    XS, V, A = (fl.each(n, [R, 2, W]) for n in ("xs", "v", "a"))
    XD, s, x4 = (fl.each(n, [R, 2, D]) for n in ("xd", "s", "x4"))
    y = fl.each("y", [R, 2, to_width])
    AT = fl.each("aT", [W, 2, R], copies=2)
    norm = fl.norms(R, 2)
    T, O, tot = fl.ps("T", [W, 4, D], 2), fl.ps("O", [R, 4, D], 2), fl.ps("tot", [R, 4, D], 2)
    weights, bias = (k.w2, k.b2r) if last else (k.w1, k.b1r)
    fl.segments(W)
    fl.sems("weighted", "a", "totals_used", "t", "c", "o", "y", "summed", "mv", "std", "nm", "x4")
    if last:
        fl.gathers(slice(0, 6, 5), ("weighted", "summed"), (k.h1, XS, HID), (k.x23h, XD, D))
        fl.scatters((k.arg["out"], x4, D, "x4", 0))
    else:
        fl.gathers(slice(4, 5), ("weighted",), (k.x23h, XS, D))
        fl.scatters((k.h1, y, HID, "y", 0))

    with nc.Block() as block:
        @block.gpsimd
        def _(pool):
            fl.run(pool, {0: lambda i, b: fl.gather(pool, i, b),
                          21 if last else 17: lambda i, b: fl.scatter(pool, 0, i, b)})
            fl.landed(pool)

        @block.sync
        def _(sp):
            fl.run(sp, {2: lambda i, b: fl.load_keys(sp, i, b)})

        @block.tensor
        def _(pe):
            t = nc.tensor

            def totals(i, b):
                fl.wait(pe, "weighted", i, b)
                fl.wait(pe, "totals_used", i, b, back=2)
                fl.totals(pe, i, b, lambda j: tot[b][:, j, 0:W], lambda j: V[b][:, j, :])

            def transpose(i, b):
                fl.wait(pe, "a", i, b)
                fl.wait(pe, "c", i, b, back=2)
                fl.hold(pe)
                transpose_tiles(k, T[b], A[b]).then_inc(fl.on["t"], 1)

            def project(i, b):
                fl.wait(pe, "c", i, b)
                fl.wait(pe, "y", i, b, back=2)
                t.matmul(O[b][:, 0:2, 0:to_width], k.ones_row[:, 0:R],
                         bias[:, 0:2 * to_width].rearrange("a (q d) -> a q d", q=2), start=True, stop=False,
                         skip_group_check=True)
                for j in range(2):
                    ins = t.matmul(O[b][:, j, 0:to_width], AT[b][:, j, :], weights[:, :], start=False, stop=True,
                                   skip_group_check=True)
                ins.then_inc(fl.on["o"], 1)

            fl.run(pe, {11: totals, 13: transpose, 15: project})

        @block.scalar
        def _(act):
            a = nc.scalar

            def weigh(i, b):
                fl.gathered_all(act, i, b)
                fl.wait(act, "total", i, b, back=fl.slots, per=2, part=2)
                for j in range(2):
                    ins = a.activation(V[b][:, j, :], XS[b][:, j, :], ACT.Copy,
                                       scale=order.cols[:, bass.ds(fl.tile(i, b) + j, 1), WEIGHT])
                ins.then_inc(fl.on["weighted"], 1)

            def carry(i, b):
                fl.carry(act, i, b, V, tot, lambda ni, nb: fl.wait(act, "weighted", ni, nb))

            def copy(i, b):
                fl.wait(act, "t", i, b)
                fl.wait(act, "o", i, b, back=2)
                a.activation(AT[b][:, :, :], T[b][:, 0:2, 0:R], ACT.Copy).then_inc(fl.on["c"], 1)

            def bend(i, b):
                fl.wait(act, "o", i, b)
                if last:
                    fl.wait(act, "summed", i, b, back=fl.slots)
                else:
                    fl.scattered_before(act, 0, i, b)
                a.activation(y[b][:, :, :], O[b][:, 0:2, 0:to_width], ACT.Sigmoid).then_inc(fl.on["y"], 1)

            def norm4(i, b):
                fl.wait(act, "nm", i, b)
                fl.scattered_before(act, 0, i, b)
                normalise(k, x4[b], s[b], norm.rs[b], norm.nm[b]).then_inc(fl.on["x4"], 1)

            steps = {4: weigh, 11: carry, 14: copy, 16: bend}
            if last:
                steps[18], steps[20] = norm.root(act), norm4
            fl.run(act, steps)

        @block.vector
        def _(dve):
            v = nc.vector

            def take(i, b):
                fl.carried(dve, i, b)
                fl.wait(dve, "t", i, b, back=fl.slots)
                v.tensor_copy(A[b][:, :, :], tot[b][:, 0:2, 0:W]).then_inc(fl.on["a"], 1)
                fl.wait(dve, "a", i, b)
                dve.sem_inc(fl.on["totals_used"], 1)

            def sum4(i, b):
                c = fl.chain(dve, "v_sum4", i, b, 2)
                fl.wait(dve, "y", i, b)
                fl.gathered_all(dve, i, b)
                fl.wait(dve, "x4", i, b, back=fl.slots)
                c.done(v.tensor_tensor(s[b][:, :, :], XD[b][:, :, :], y[b][:, :, :], ALU.add))
                dve.sem_inc(fl.on["summed"], 1)
                norm.moments(c, b, s[b]).then_inc(fl.on["mv"], 1)
                c.close()

            steps = {10: lambda i, b: fl.masks(dve, i, b), 12: take}
            if last:
                steps[17], steps[19] = sum4, norm.shift(dve)
            fl.run(dve, steps)
    fl.own.close()


def program(nc, args, n_nodes, n_edges, upto=99, probe=None):
    with ExitStack() as ctx:
        k = Kernel(nc, ctx, args, n_nodes, n_edges)
        k.by_src1 = k.dram("by_src_low", (k.E + 1, COLS))
        k.by_dst1 = k.dram("by_dst_low", (k.E + 1, COLS))
        k.by_src = k.dram("by_src", (k.E + 1, COLS)) if probe is None else probe["by_src"]
        k.by_dst = k.dram("by_dst", (k.E + 1, COLS)) if probe is None else probe["by_dst"]
        prepare(k)
        k.recycle()
        edge_table(k)
        k.recycle()
        k.x1, k.x23 = k.dram("x1_nodes", (k.N, D)), k.dram("x2_x3_nodes", (k.N, 2 * D))
        k.h1 = k.dram("h1_nodes", (k.N, HID))
        if probe:
            k.x1, k.x23, k.h1 = probe["x1"], probe["x23"], probe["h1"]
        k.x23h = k.x23.rearrange("n (h d) -> (n h) d", h=2)
        dense(k)
        k.recycle()
        k.sorting.close()

        k.scores = k.sb("scores", [R, k.tiles])
        k.probs = k.sb("probs", [R, k.tiles])
        dst = Order(k, "dst", k.by_dst, DST)
        k.recycle()
        layer0(k, dst)
        k.recycle()
        layer1(k, dst)
        k.recycle()
        rows_s = k.dram("x2_of_src", (k.tiles // 2, R, 2 * D))
        rows_d = k.dram("x2_of_dst", (k.tiles // 2, R, 2 * D))
        src = Order(k, "src", k.by_src, SRC)
        k.recycle()
        logits(k, src, rows_s, rows_d, k.scores)
        k.recycle()
        segment_softmax(k, k.by_src, SRC, k.scores, k.probs)
        k.recycle()
        layer2(k, src, rows_s, rows_d, k.probs)
        k.recycle()
        src.own.close()
        layer3(k, dst, False)
        k.recycle()
        layer3(k, dst, True)
        dst.own.close()


_INS = ["x", "src", "dst", "edge_attr_128", "edge_type_8", "edge_weight",
        "L0_gnn_W", "L0_gnn_b", "L0_gnn_gamma", "L0_gnn_beta",
        "L1_gnn_rel_emb", "L1_gnn_W", "L1_gnn_b",
        "L2_gnn_W_node", "L2_gnn_b_node", "L2_gnn_W_edge", "L2_gnn_b_edge",
        "L3_gnn_w1", "L3_gnn_b1", "L3_gnn_w2", "L3_gnn_b2"]


def kernel(**inputs):
    import numpy as _np
    import concourse.bacc as _bacc
    from concourse import mybir as _mybir
    from concourse.bass_utils import run_bass_kernel_spmd as _run

    nc = _bacc.Bacc("TRN2", target_bir_lowering=False, num_devices=1)
    arrays, args = {}, {}
    for name in _INS:
        a = _np.ascontiguousarray(inputs[name])
        arrays[f"in_{name}"] = a
        args[name] = nc.dram_tensor(f"in_{name}", a.shape, _mybir.dt.from_np(a.dtype), kind="ExternalInput").ap()
    n_nodes, features = inputs["x"].shape
    args["out"] = nc.dram_tensor("out", (n_nodes, features), _mybir.dt.float32, kind="ExternalOutput").ap()
    program(nc, args, n_nodes, inputs["src"].shape[0])
    r = _run(nc, [arrays], core_ids=[0])
    return r.results[0]["out"]
```
